# Optimizing a Trainium2 kernel written in Bass

```python
import numpy as np
import jax
import jax.numpy as jnp

def _softmax(x, axis=-1):
    return jax.nn.softmax(x, axis=axis)

def _gelu(x):
    return jax.nn.gelu(x, approximate=True)

def _silu(x):
    return jax.nn.silu(x)

def _sigmoid(x):
    return jax.nn.sigmoid(x)

def _layernorm(x, axis=-1, eps=1e-05):
    m = jnp.mean(x, axis=axis, keepdims=True)
    v = jnp.var(x, axis=axis, keepdims=True)
    return (x - m) / jnp.sqrt(v + eps)

def _scatter_add(tgt, idx, src, axis=0):
    return tgt.at[idx].add(src)

def _segment_sum(src, seg, n):
    return jax.ops.segment_sum(src, seg, n)
kernel_name = 'mk_xattn_ffn_d1_seqx_r4_e53879'

def setup_inputs(seed: int=0):
    np.random.seed(seed)
    _w = jnp.asarray

    def _rec_inputs():
        import jax
        import jax.numpy as jnp
        _rk = jax.random.key(seed)
        x = -0.0003929 + 0.9999 * jax.random.normal(jax.random.fold_in(_rk, 1), (4, 512, 256), jnp.float32)
        _lenS = 512 - jax.random.randint(jax.random.fold_in(_rk, 7), (4,), 0, max(1, 512 // 4) + 1, jnp.int32)
        _lenS2 = 1601 - jax.random.randint(jax.random.fold_in(_rk, 8), (4,), 0, max(1, 1601 // 4) + 1, jnp.int32)
        _ctx_1024P = jax.random.normal(jax.random.fold_in(_rk, 11), (4, 16, 256), jnp.float32)
        _ctx_1024c = jax.random.dirichlet(jax.random.fold_in(_rk, 511), 0.3 * jnp.ones((16,), jnp.float32), (4, 1601))
        _ctx_1024t = jnp.einsum('bsk,bkd->bsd', _ctx_1024c, _ctx_1024P)
        _ctx_1024t = _ctx_1024t * jax.lax.rsqrt(jnp.mean(jnp.square(_ctx_1024t)) + 1e-12) * 0.953939
        ctx_1024 = 2.81802e-05 + 1.00001 * (_ctx_1024t + 0.3 * jax.random.normal(jax.random.fold_in(_rk, 611), (4, 1601, 256), jnp.float32))
        _validS = jnp.arange(512)[None, :] < _lenS[:, None]
        _validS2 = jnp.arange(1601)[None, :] < _lenS2[:, None]
        _causal = jnp.tril(jnp.ones((512, 512), dtype=bool))
        mask_S2_ik0 = jnp.where(_validS2[0], 0, 1).astype(jnp.int32)
        return (x, ctx_1024, mask_S2_ik0)
    x, ctx_1024, mask_S2_ik0 = _rec_inputs()

    def _L0_xattn_setup():
        import jax, jax.numpy as jnp
        import numpy as np
        DIM = 256
        NUM_HEADS = 8
        SCALE = (DIM // NUM_HEADS) ** (-0.5)
        key = jax.random.key(seed)
        k1, k2, k3, k4, k5, k6 = jax.random.split(key, 6)
        B, N, M, C = (8, 512, 512, DIM)
        x = jax.random.normal(k1, (B, N, C), dtype=jnp.float32)
        support = jax.random.normal(k2, (B, M, C), dtype=jnp.float32)
        attn_mask = jax.random.randint(k3, (M,), 0, 2, dtype=jnp.int32)
        qkv_w = jax.random.normal(k4, (3 * C, C), dtype=jnp.float32) * C ** (-0.5)
        proj_w = jax.random.normal(k5, (C, C), dtype=jnp.float32) * C ** (-0.5)
        proj_b = jax.random.normal(k6, (C,), dtype=jnp.float32) * 0.01
        return {'x': x, 'support': support, 'attn_mask': attn_mask, 'qkv_w': qkv_w, 'proj_w': proj_w, 'proj_b': proj_b}
    _L0_xattn_all = _L0_xattn_setup()
    _L0_xattn_in = {k: v for k, v in _L0_xattn_all.items() if k in ('qkv_w', 'proj_w', 'proj_b')}
    del _L0_xattn_all

    def _L0_ffn_setup():
        import jax, jax.numpy as jnp
        import numpy as np
        D = 256
        H = 16
        DK = D // H
        E = 8
        DFF = 4 * D
        TOPK = 2
        EPS = 1e-05

        def _layernorm(x, g, b):
            m = jnp.mean(x, axis=-1, keepdims=True)
            v = jnp.mean(jnp.square(x - m), axis=-1, keepdims=True)
            return (x - m) * jax.lax.rsqrt(v + EPS) * g + b
        key = jax.random.key(seed)
        ks = jax.random.split(key, 16)
        s_in = 1.0 / np.sqrt(D)
        s_ff = 1.0 / np.sqrt(DFF)
        return {'x': jax.random.normal(ks[0], (2, 512, D), dtype=jnp.float32), 'ln1_g': jnp.ones((D,), jnp.float32), 'ln1_b': jnp.zeros((D,), jnp.float32), 'w_qkv': jax.random.normal(ks[1], (D, 3 * D), jnp.float32) * s_in, 'b_qkv': jnp.zeros((3 * D,), jnp.float32), 'w_o': jax.random.normal(ks[2], (D, D), jnp.float32) * s_in, 'b_o': jnp.zeros((D,), jnp.float32), 'ln2_g': jnp.ones((D,), jnp.float32), 'ln2_b': jnp.zeros((D,), jnp.float32), 'gate_w': jax.random.normal(ks[3], (D, E), jnp.float32) * s_in, 'gate_b': jnp.zeros((E,), jnp.float32), 'W1': jax.random.normal(ks[4], (E, D, DFF), jnp.float32) * s_in, 'b1': jnp.zeros((E, DFF), jnp.float32), 'W2': jax.random.normal(ks[5], (E, DFF, D), jnp.float32) * s_ff, 'b2': jnp.zeros((E, D), jnp.float32)}
    _L0_ffn_all = _L0_ffn_setup()
    _L0_ffn_in = {k: v for k, v in _L0_ffn_all.items() if k in ('ln1_g', 'ln1_b', 'w_qkv', 'b_qkv', 'w_o', 'b_o', 'ln2_g', 'ln2_b', 'gate_w', 'gate_b', 'W1', 'b1', 'W2', 'b2')}
    del _L0_ffn_all
    return {'x': x, 'ctx_1024': ctx_1024, 'mask_S2_ik0': mask_S2_ik0, 'L0_xattn_qkv_w': _L0_xattn_in['qkv_w'], 'L0_xattn_proj_w': _L0_xattn_in['proj_w'], 'L0_xattn_proj_b': _L0_xattn_in['proj_b'], 'L0_ffn_ln1_g': _L0_ffn_in['ln1_g'], 'L0_ffn_ln1_b': _L0_ffn_in['ln1_b'], 'L0_ffn_w_qkv': _L0_ffn_in['w_qkv'], 'L0_ffn_b_qkv': _L0_ffn_in['b_qkv'], 'L0_ffn_w_o': _L0_ffn_in['w_o'], 'L0_ffn_b_o': _L0_ffn_in['b_o'], 'L0_ffn_ln2_g': _L0_ffn_in['ln2_g'], 'L0_ffn_ln2_b': _L0_ffn_in['ln2_b'], 'L0_ffn_gate_w': _L0_ffn_in['gate_w'], 'L0_ffn_gate_b': _L0_ffn_in['gate_b'], 'L0_ffn_W1': _L0_ffn_in['W1'], 'L0_ffn_b1': _L0_ffn_in['b1'], 'L0_ffn_W2': _L0_ffn_in['W2'], 'L0_ffn_b2': _L0_ffn_in['b2']}

def reference(x, ctx_1024, mask_S2_ik0, L0_xattn_qkv_w, L0_xattn_proj_w, L0_xattn_proj_b, L0_ffn_ln1_g, L0_ffn_ln1_b, L0_ffn_w_qkv, L0_ffn_b_qkv, L0_ffn_w_o, L0_ffn_b_o, L0_ffn_ln2_g, L0_ffn_ln2_b, L0_ffn_gate_w, L0_ffn_gate_b, L0_ffn_W1, L0_ffn_b1, L0_ffn_W2, L0_ffn_b2):
    import jax
    import jax.numpy as jnp

    def _L0_xattn_ref(x, support, attn_mask, qkv_w, proj_w, proj_b):
        import jax, jax.numpy as jnp
        import numpy as np
        DIM = 256
        NUM_HEADS = 8
        SCALE = (DIM // NUM_HEADS) ** (-0.5)
        B, N, C = x.shape
        wq, wk, wv = (qkv_w[:C], qkv_w[C:2 * C], qkv_w[2 * C:])
        q = jnp.einsum('bnc,dc->bnd', x, wq)
        k = jnp.einsum('bmc,dc->bmd', support, wk)
        v = jnp.einsum('bmc,dc->bmd', support, wv)
        attn = jnp.einsum('bnd,bmd->bnm', q, k) * SCALE
        attn = jax.nn.softmax(attn, axis=-1)
        attn = jnp.where(attn_mask[None, None, :] == 0, 0.0, attn)
        out = jnp.einsum('bnm,bmd->bnd', attn, v)
        out = jnp.swapaxes(out, 1, 2).reshape(B, N, C)
        out = jnp.einsum('bnc,dc->bnd', out, proj_w) + proj_b
        return out

    def _L0_ffn_ref(x, ln1_g, ln1_b, w_qkv, b_qkv, w_o, b_o, ln2_g, ln2_b, gate_w, gate_b, W1, b1, W2, b2):
        import jax, jax.numpy as jnp
        import numpy as np
        D = 256
        H = 16
        DK = D // H
        E = 8
        DFF = 4 * D
        TOPK = 2
        EPS = 1e-05

        def _layernorm(x, g, b):
            m = jnp.mean(x, axis=-1, keepdims=True)
            v = jnp.mean(jnp.square(x - m), axis=-1, keepdims=True)
            return (x - m) * jax.lax.rsqrt(v + EPS) * g + b
        B, S, _ = x.shape
        h = _layernorm(x, ln1_g, ln1_b)
        qkv = h @ w_qkv + b_qkv
        q, k, v = jnp.split(qkv, 3, axis=-1)
        q = q.reshape(B, S, H, DK)
        k = k.reshape(B, S, H, DK)
        v = v.reshape(B, S, H, DK)
        scores = jnp.einsum('bqhd,bkhd->bhqk', q, k) / np.sqrt(DK)
        attn = jax.nn.softmax(scores, axis=-1)
        o = jnp.einsum('bhqk,bkhd->bqhd', attn, v).reshape(B, S, D)
        x = x + o @ w_o + b_o
        h = _layernorm(x, ln2_g, ln2_b).reshape(B * S, D)
        logits = h @ gate_w + gate_b
        topv, topi = jax.lax.top_k(logits, TOPK)
        gw = jax.nn.softmax(topv, axis=-1)
        ew = jnp.sum(jax.nn.one_hot(topi, E, dtype=h.dtype) * gw[..., None], axis=1)
        hid = jax.nn.relu(jnp.einsum('td,edf->etf', h, W1) + b1[:, None, :])
        out_e = jnp.einsum('etf,efd->etd', hid, W2) + b2[:, None, :]
        moe = jnp.einsum('etd,te->td', out_e, ew)
        return x + moe.reshape(B, S, D)
    x = x + _L0_xattn_ref(_layernorm(x, axis=-1), ctx_1024, mask_S2_ik0, L0_xattn_qkv_w, L0_xattn_proj_w, L0_xattn_proj_b)
    x = x + _L0_ffn_ref(_layernorm(x, axis=-1), L0_ffn_ln1_g, L0_ffn_ln1_b, L0_ffn_w_qkv, L0_ffn_b_qkv, L0_ffn_w_o, L0_ffn_b_o, L0_ffn_ln2_g, L0_ffn_ln2_b, L0_ffn_gate_w, L0_ffn_gate_b, L0_ffn_W1, L0_ffn_b1, L0_ffn_W2, L0_ffn_b2)
    return x

_drawn_inputs = setup_inputs


def setup_inputs(seed=0):
    import zlib

    import numpy as np

    out = dict(_drawn_inputs(seed))
    spreads = {'L0_ffn_ln1_g': (1.0, 0.2),
     'L0_ffn_ln1_b': (0.0, 0.1),
     'L0_ffn_b_qkv': (0.0, 0.1),
     'L0_ffn_b_o': (0.0, 0.1),
     'L0_ffn_ln2_g': (1.0, 0.2),
     'L0_ffn_ln2_b': (0.0, 0.1),
     'L0_ffn_gate_b': (0.0, 0.1),
     'L0_ffn_b1': (0.0, 0.317),
     'L0_ffn_b2': (0.0, 0.1)}
    factors = {'L0_xattn_proj_b': 2.938}
    for name, (base, spread) in spreads.items():
        noise = np.random.default_rng([zlib.crc32(name.encode()), seed]).standard_normal(out[name].shape)
        drawn = base * np.exp(spread * noise) if base else spread * noise
        out[name] = jnp.asarray(drawn.astype(out[name].dtype))
    for name, factor in factors.items():
        out[name] = (out[name] * factor).astype(out[name].dtype)
    return out
```

```python
from contextlib import ExitStack

import numpy as np

import concourse.bass as bass
from concourse import mybir

P = 128
F32 = mybir.dt.float32
F32R = mybir.dt.float32r
I32 = mybir.dt.int32
U32 = mybir.dt.uint32
ALU = mybir.AluOpType
ACT = mybir.ActivationFunctionType
AX = mybir.AxisListType.X

PASSES = ((1, 0), (0, 1), (0, 0))


def xattn_moe_kernel(nc, x, ctx_in, mask, qkv_w, proj_w, proj_b, ln1_g, ln1_b, w_qkv, b_qkv, w_o, b_o,
                     ln2_g, ln2_b, gate_w, gate_b, W1, b1, W2, b2, out):
    B, S, D = x.shape
    M = ctx_in.shape[1]
    E, _, DFF = W1.shape
    DC = D // P
    NT = S // P
    MT = -(-M // P)
    ML = M - (MT - 1) * P
    MG = -(-M // 512)
    H = 16
    DK = D // H
    HG = H // 4
    FT = DFF // P
    NB = B * NT
    XSCALE = float(D // 8) ** -0.5
    SSCALE = float(DK) ** -0.5
    EPS = 1e-5

    def mrows(t):
        return P if t < MT - 1 else ML

    def mcols(g):
        return min(512, M - 512 * g)

    def bcast_rows(v, n):
        return v.rearrange("(a n) -> a n", a=1).to_broadcast([P, n])

    with ExitStack() as keep:
        def sb(name, shape, dt=F32, stack=keep):
            return stack.enter_context(nc.sbuf_tensor(name, shape, dt))

        PS = keep.enter_context(nc.psum_tensor("banks", [P, 8, 512], F32))

        def bank(i):
            return PS[:, i, :]

        ident = sb("ident", [P, P])
        halves = sb("minus_half", [P, NT])
        M_s = sb("wq_wk", [P, 2, DC, D], F32R)
        WvT_s = sb("wv_t", [P, 2, DC, D], F32R)
        PT_s = sb("proj_t", [P, 2, DC, D], F32R)
        Wqkv_s = sb("w_qkv_s", [P, 2, DC, 3 * D], F32R)
        Wo_s = sb("w_o_s", [P, 2, DC, D], F32R)
        Wg_s = sb("gate_s", [P, 2, DC, E], F32R)
        b2_sb = sb("b2_sb", [E, D])
        pb_row = sb("proj_b_row", [P, D])
        bo_row = sb("b_o_row", [P, D])
        bv_row = sb("b_v_row", [P, D])
        gb_row = sb("gate_b_row", [P, E])
        iota_e = sb("iota_e", [P, E])
        cols = sb("cols", [P, 4, DC])
        bqk_col = sb("bqk_col", [P, 2 * DC])
        mask01 = sb("mask01", [P, MT])
        b1_col = sb("b1_col", [P, E * FT])
        acc = sb("acc", [P, NB, D])
        ew = sb("expert_weight", [P, NB, E])
        hT_s = sb("h_t", [P, 2, DC, B * S], F32R)

        def clear(sems):
            for s in sems:
                nc.sync.sem_clear(s)
            nc.all_engine_barrier()

        def semaphores(stack, names):
            made = {n: stack.enter_context(nc.semaphore(n)) for n in names.split()}
            return made, list(made.values())

        def chain(eng, sem):
            count = [0]

            def step(ins):
                count[0] += 1
                ins.then_inc(sem, 1)
                eng.wait_ge(sem, count[0])
            return step

        def product(pe, out_ap, lhsT, rhs, k_chunks, first=True, last=True):
            n = 0
            for k in range(k_chunks):
                for a, b in PASSES:
                    ins = pe.matmul(out_ap, lhsT(a, k), rhs(b, k), start=first and n == 0,
                                    stop=last and n == 3 * k_chunks - 1)
                    n += 1
            return ins

        with ExitStack() as st:
            wq_raw = sb("wq_raw", [P, 3 * DC, D], stack=st)
            pj_raw = sb("pj_raw", [P, DC, D], stack=st)
            wqkv_raw = sb("wqkv_raw", [P, DC, 3 * D], stack=st)
            wo_raw = sb("wo_raw", [P, DC, D], stack=st)
            wg_raw = sb("wg_raw", [P, DC, E], stack=st)
            mask_i = sb("mask_i", [P, MT], I32, stack=st)
            mask_f = sb("mask_f", [P, MT], stack=st)
            b1_rows = sb("b1_rows", [E * FT, P], stack=st)
            s, every = semaphores(st, "w_loaded ident_zero ident_ready w_psum w_hi w_lo raw_hi v_loaded own")
            with nc.Block() as block:
                @block.sync
                def _(sp):
                    loads = [
                        (wq_raw[:, :, :], qkv_w.rearrange("(c p) d -> p c d", p=P)),
                        (pj_raw[:, :, :], proj_w.rearrange("(c p) d -> p c d", p=P)),
                        (b1_rows[:, :], b1.rearrange("e (f p) -> (e f) p", p=P)),
                        (wqkv_raw[:, :, :], w_qkv.rearrange("(c p) n -> p c n", p=P)),
                        (wo_raw[:, :, :], w_o.rearrange("(c p) n -> p c n", p=P)),
                        (wg_raw[:, :, :], gate_w.rearrange("(c p) e -> p c e", p=P)),
                    ]
                    for dst, src in loads:
                        sp.dma_start(dst, src).then_inc(s["w_loaded"], 16)
                    sp.wait_ge(s["w_loaded"], 16 * len(loads))

                @block.scalar
                def _(act):
                    vectors = [
                        (b2_sb[:, :], b2),
                        (pb_row[:, :], bcast_rows(proj_b, D)),
                        (bo_row[:, :], bcast_rows(b_o, D)),
                        (bv_row[:, :], bcast_rows(b_qkv[2 * D:3 * D], D)),
                        (gb_row[:, :], bcast_rows(gate_b, E)),
                        (bqk_col[:, :], b_qkv[0:2 * D].rearrange("(c p) -> p c", p=P)),
                        (mask_i[:, 0:MT - 1], mask[0:(MT - 1) * P].rearrange("(t p) -> p t", p=P)),
                        (mask_i[0:ML, MT - 1:MT], mask[(MT - 1) * P:M].rearrange("(t p) -> p t", t=1)),
                    ] + [(cols[:, n, :], v.rearrange("(c p) -> p c", p=P))
                         for n, v in enumerate((ln1_g, ln1_b, ln2_g, ln2_b))]
                    for dst, src in vectors:
                        act.dma_start(dst, src, allow_slow_non_contiguous=True).then_inc(s["v_loaded"], 16)
                    for n, dst in enumerate([M_s] * DC + [WvT_s] * DC + [PT_s] * DC):
                        act.wait_ge(s["w_psum"], n + 1)
                        act.activation(dst[:, 0, n % DC, :], PS[:, n, 0:D], ACT.Copy).then_inc(s["w_hi"], 1)
                    act.wait_ge(s["w_psum"], 3 * DC + 1)
                    act.activation(b1_col[:, :], PS[:, 6, 0:E * FT], ACT.Copy)
                    act.wait_ge(s["v_loaded"], 16 * len(vectors))

                @block.gpsimd
                def _(pool):
                    pool.memset(ident[:, :], 0.0).then_inc(s["ident_zero"], 1)
                    pool.memset(halves[:, :], -0.5)
                    for e in range(E):
                        pool.memset(iota_e[:, e:e + 1], float(e))
                    pool.wait_ge(s["ident_zero"], 1)
                    pool.affine_select(out=ident[:, :], in_=ident[:, :], compare_op=ALU.not_equal, fill=1.0,
                                       base=0, pattern=[[-1, P]], channel_multiplier=1).then_inc(s["ident_ready"], 1)
                    pool.wait_ge(s["w_loaded"], 96)
                    for dst, src in ((Wqkv_s, wqkv_raw), (Wo_s, wo_raw), (Wg_s, wg_raw)):
                        pool.tensor_copy(dst[:, 0], src[:, :, :]).then_inc(s["raw_hi"], 1)

                @block.tensor
                def _(pe):
                    pe.wait_ge(s["ident_ready"], 1)
                    pe.wait_ge(s["w_loaded"], 96)
                    for c in range(DC):
                        for k in range(DC):
                            ins = pe.matmul(PS[:, c, 0:D], wq_raw[:, k, c * P:(c + 1) * P], wq_raw[:, DC + k, :],
                                            start=k == 0, stop=k == DC - 1)
                        ins.then_inc(s["w_psum"], 1)
                    for raw, base, b0 in ((wq_raw, 2 * DC, DC), (pj_raw, 0, 2 * DC)):
                        for c in range(DC):
                            for k in range(DC):
                                ins = pe.transpose(PS[:, b0 + c, k * P:(k + 1) * P],
                                                   raw[:, base + k, c * P:(c + 1) * P], ident[:, :])
                            ins.then_inc(s["w_psum"], 1)
                    pe.transpose(PS[:, 6, 0:E * FT], b1_rows[:, :], ident[0:E * FT, 0:E * FT]).then_inc(s["w_psum"], 1)

                @block.vector
                def _(dve):
                    own = chain(dve, s["own"])
                    for n, dst in enumerate([M_s] * DC + [WvT_s] * DC + [PT_s] * DC):
                        dve.wait_ge(s["w_hi"], n + 1)
                        dve.tensor_tensor(dst[:, 1, n % DC, :], PS[:, n, 0:D], dst[:, 0, n % DC, :].bitcast(F32),
                                          ALU.subtract)
                    for n, (dst, src) in enumerate(((Wqkv_s, wqkv_raw), (Wo_s, wo_raw), (Wg_s, wg_raw))):
                        dve.wait_ge(s["raw_hi"], n + 1)
                        dve.tensor_tensor(dst[:, 1], src[:, :, :], dst[:, 0].bitcast(F32), ALU.subtract)
                    dve.wait_ge(s["v_loaded"], 16 * 12)
                    for p, c0, c1 in ((P, 0, MT - 1), (ML, MT - 1, MT)):
                        own(dve.tensor_copy(mask_f[0:p, c0:c1], mask_i[0:p, c0:c1]))
                        dve.tensor_scalar(mask01[0:p, c0:c1], mask_f[0:p, c0:c1], 0.0, None, ALU.not_equal)
            clear(every)

        with ExitStack() as bs:
            x1 = sb("x1", [P, NT, D], stack=bs)
            st_a = sb("st_a", [P, NT, 6], stack=bs)
            mv = sb("mean_var", [P, NT, 2], stack=bs)
            veps = sb("var_eps", [P, NT], stack=bs)
            rstd = sb("rstd", [P, NT], stack=bs)

            def layer_norm(dve, own, src, dst, stats_ready, rstd_ready, n):
                for t in range(NT):
                    own(dve.bn_stats(st_a[:, t, :], src[:, t, :]))
                for t in range(NT):
                    own(dve.bn_aggr(mv[:, t, :], st_a[:, t, :]))
                dve.tensor_scalar(veps[:, :], mv[:, :, 1], EPS, None, ALU.add).then_inc(stats_ready, 1)
                dve.wait_ge(rstd_ready, n)
                for t in range(NT):
                    ins = dve.tensor_scalar(dst[:, t, :], src[:, t, :], mv[:, t, 0:1], rstd[:, t:t + 1],
                                            ALU.subtract, ALU.mult)
                    own(ins)

            def inverse_root(pool, stats_ready, rstd_ready, n):
                pool.wait_ge(stats_ready, n)
                pool.tensor_tensor(rstd[:, :], veps[:, :], halves[:, :], ALU.pow).then_inc(rstd_ready, 1)

            with nc.Fori(0, B) as b:
                with ExitStack() as st:
                    xq = sb("x_tokens", [P, NT, D], stack=st)
                    xr = sb("x_residual", [P, NT, D], stack=st)
                    xn = sb("x_norm", [P, NT, D], stack=st)
                    xnT = sb("x_norm_t", [P, 2, DC, S], F32R, stack=st)
                    qT = sb("q_t", [P, 2, DC, S], F32R, stack=st)
                    cn = sb("ctx", [P, MT, D], stack=st)
                    cm = sb("ctx_masked", [P, 2, MT, D], F32R, stack=st)
                    cT = sb("ctx_t", [P, 2, DC, M + 1], F32R, stack=st)
                    pr = sb("probs", [P, M], stack=st)
                    pT = sb("probs_t", [P, 2, MT, P], F32R, stack=st)
                    mx = sb("row_max", [P, NT], stack=st)
                    nb = sb("neg_max", [P, NT], stack=st)
                    rs = sb("row_sum", [P, NT], stack=st)
                    ri = sb("row_inv", [P, NT], stack=st)
                    ac = sb("attn_ctx", [P, 2, NT, D], F32R, stack=st)
                    tT = xnT
                    s, every = semaphores(st, "xq_in ctx_in xr_in stats inv xn_ready own cT_ps cT_hi cT_lo cm_hi cm_lo "
                                              "xT_ps xT_hi xT_lo q_ps q_hi q_lo s_ps s_max p_ready pT_ps pT_hi pT_lo "
                                              "ac_ps ac_inv ac_hi ac_lo t_ps t_hi t_lo y_ps xr_ready pzero")
                    groups = [(g, c) for g in range(MG) for c in range(DC)]
                    xb = x[bass.ds(b, 1)].rearrange("a n d -> (a n) d")
                    cb = ctx_in[bass.ds(b, 1)].rearrange("a n d -> (a n) d")
                    with nc.Block() as block:
                        @block.sync
                        def _(sp):
                            sp.dma_start(xq[:, :, :], xb.rearrange("(t p) d -> p t d", p=P)).then_inc(s["xq_in"], 16)
                            sp.dma_start(cn[:, 0:MT - 1, :], cb[0:(MT - 1) * P, :].rearrange("(t p) d -> p t d", p=P))\
                                .then_inc(s["ctx_in"], 16)
                            sp.dma_start(cn[0:ML, MT - 1, :], cb[(MT - 1) * P:M, :]).then_inc(s["ctx_in"], 16)
                            sp.dma_start(xr[:, :, :].rearrange("p (c r) d -> p c r d", r=2),
                                         xb.rearrange("(c p r) d -> p c r d", p=P, r=2)).then_inc(s["xr_in"], 16)
                            sp.wait_ge(s["xr_in"], 16)

                        @block.gpsimd
                        def _(pool):
                            inverse_root(pool, s["stats"], s["inv"], 1)
                            pool.wait_ge(s["ctx_in"], 32)
                            for t in range(MT):
                                m = mrows(t)
                                pool.tensor_scalar(cm[0:m, 0, t, :], cn[0:m, t, :], mask01[0:m, t:t + 1], None,
                                                   ALU.mult).then_inc(s["cm_hi"], 1)
                            pool.wait_ge(s["xr_in"], 16)
                            for t in range(NT):
                                pool.tensor_tensor(xr[:, t, :], xr[:, t, :], pb_row[:, :], ALU.add).then_inc(s["xr_ready"], 1)

                        @block.tensor
                        def _(pe):
                            pe.wait_ge(s["ctx_in"], 32)
                            for n, (g, c) in enumerate(groups):
                                if n >= 4:
                                    pe.wait_ge(s["cT_lo"], n - 3)
                                for t in range(4 * g, min(4 * g + 4, MT)):
                                    m = mrows(t)
                                    o = (t - 4 * g) * P
                                    ins = pe.transpose(PS[:, n % 4, o:o + m], cn[0:m, t, c * P:(c + 1) * P],
                                                       ident[0:m, 0:m])
                                ins.then_inc(s["cT_ps"], 1)
                            pe.wait_ge(s["xn_ready"], 1)
                            for c in range(DC):
                                for t in range(NT):
                                    ins = pe.transpose(PS[:, 4 + c, t * P:(t + 1) * P], xn[:, t, c * P:(c + 1) * P],
                                                       ident[:, :])
                                ins.then_inc(s["xT_ps"], 1)
                            pe.wait_ge(s["xT_lo"], DC)
                            for c in range(DC):
                                product(pe, bank(6 + c), lambda a, k: M_s[:, a, k, c * P:(c + 1) * P],
                                        lambda a, k: xnT[:, a, k, :], DC).then_inc(s["q_ps"], 1)
                            pe.wait_ge(s["q_lo"], DC)
                            pe.wait_ge(s["cT_lo"], len(groups))

                            def scores(t):
                                if t:
                                    pe.wait_ge(s["p_ready"], t)
                                for g in range(MG):
                                    w = mcols(g) + mcols(g) % 2
                                    ins = product(pe, PS[:, g, 0:w], lambda a, k: qT[:, a, k, t * P:(t + 1) * P],
                                                  lambda a, k: cT[:, a, k, g * 512:g * 512 + w], DC)
                                ins.then_inc(s["s_ps"], 1)

                            def turn_probs(t):
                                pe.wait_ge(s["p_ready"], t + 1)
                                for g in range(MG):
                                    n = t * MG + g
                                    if n >= 2:
                                        pe.wait_ge(s["pT_lo"], n - 1)
                                    for i in range(4 * g, min(4 * g + 4, MT)):
                                        m = mrows(i)
                                        o = (i - 4 * g) * P
                                        ins = pe.transpose(PS[0:m, 4 + n % 2, o:o + P], pr[:, i * P:i * P + m],
                                                           ident[:, :])
                                    ins.then_inc(s["pT_ps"], 1)

                            def attend(t):
                                pe.wait_ge(s["pT_lo"], MG * (t + 1))
                                if t == 0:
                                    pe.wait_ge(s["cm_lo"], MT)
                                if t >= 2:
                                    pe.wait_ge(s["ac_lo"], t - 1)
                                n = 0
                                for i in range(MT):
                                    m = mrows(i)
                                    for a, c in PASSES:
                                        ins = pe.matmul(PS[:, 6 + t % 2, 0:D], pT[0:m, a, i, :], cm[0:m, c, i, :],
                                                        start=n == 0, stop=n == 3 * MT - 1)
                                        n += 1
                                ins.then_inc(s["ac_ps"], 1)

                            scores(0)
                            for t in range(NT):
                                turn_probs(t)
                                if t + 1 < NT:
                                    scores(t + 1)
                                attend(t)
                            for r in range(2):
                                pe.wait_ge(s["ac_lo"], 2 * r + 2)
                                for c in range(DC):
                                    ins = product(pe, PS[:, 4 + r, c * D:(c + 1) * D],
                                                  lambda a, k: ac[:, a, 2 * r + k, c * P:(c + 1) * P],
                                                  lambda a, k: PT_s[:, a, k, :], DC)
                                ins.then_inc(s["t_ps"], 1)
                            for r in range(2):
                                pe.wait_ge(s["t_lo"], r + 1)
                                for c in range(DC):
                                    product(pe, PS[:, 2 * r + c, 0:D],
                                            lambda a, k: WvT_s[:, a, k, c * P:(c + 1) * P],
                                            lambda a, k: tT[:, a, r, k * D:(k + 1) * D], DC).then_inc(s["y_ps"], 1)

                        @block.scalar
                        def _(act):
                            def round_off(src, dst, ready, n, done):
                                act.wait_ge(ready, n)
                                act.activation(dst, src, ACT.Copy).then_inc(done, 1)

                            for n, (g, c) in enumerate(groups):
                                w = mcols(g)
                                round_off(PS[:, n % 4, 0:w], cT[:, 0, c, g * 512:g * 512 + w], s["cT_ps"], n + 1, s["cT_hi"])
                            for c in range(DC):
                                round_off(bank(4 + c), xnT[:, 0, c, :], s["xT_ps"], c + 1, s["xT_hi"])
                            for c in range(DC):
                                round_off(bank(6 + c), qT[:, 0, c, :], s["q_ps"], c + 1, s["q_hi"])

                            def exp(t):
                                act.wait_ge(s["s_max"], t + 1)
                                if t:
                                    act.wait_ge(s["pT_ps"], MG * t)
                                act.activation(pr[:, :], PS[:, 0:MG, :].rearrange("p g n -> p (g n)")[:, 0:M],
                                               ACT.Exp, bias=nb[:, t:t + 1], scale=XSCALE,
                                               accum_out=rs[:, t:t + 1]).then_inc(s["p_ready"], 1)

                            exp(0)
                            for t in range(NT):
                                if t:
                                    act.wait_ge(s["ac_ps"], t)
                                for g in range(MG):
                                    n = t * MG + g
                                    k = min(4, MT - 4 * g)
                                    m = mrows(4 * g + k - 1)
                                    round_off(PS[0:m, 4 + n % 2, 0:k * P],
                                              pT[0:m, 0, 4 * g:4 * g + k, :].rearrange("p t n -> p (t n)"),
                                              s["pT_ps"], n + 1, s["pT_hi"])
                                if t + 1 < NT:
                                    exp(t + 1)
                                act.wait_ge(s["ac_ps"], t + 1)
                                act.wait_ge(s["ac_inv"], t + 1)
                                act.activation(ac[:, 0, t, :], PS[:, 6 + t % 2, 0:D], ACT.Copy,
                                               scale=ri[:, t:t + 1]).then_inc(s["ac_hi"], 1)
                            for r in range(2):
                                round_off(bank(4 + r), tT[:, 0, r, :], s["t_ps"], r + 1, s["t_hi"])

                        @block.vector
                        def _(dve):
                            own = chain(dve, s["own"])
                            dve.memset(cT[:, :, :, M:M + 1].bitcast(F32), 0.0).then_inc(s["pzero"], 1)
                            dve.wait_ge(s["xq_in"], 16)
                            layer_norm(dve, own, xq, xn, s["stats"], s["inv"], 1)
                            dve.engine_nop().then_inc(s["xn_ready"], 1)

                            def remainder(src, hi, lo, ready, n, done):
                                dve.wait_ge(ready, n)
                                dve.tensor_tensor(lo, src, hi.bitcast(F32), ALU.subtract).then_inc(done, 1)

                            for n, (g, c) in enumerate(groups):
                                w = mcols(g)
                                a = g * 512
                                remainder(PS[:, n % 4, 0:w], cT[:, 0, c, a:a + w], cT[:, 1, c, a:a + w], s["cT_hi"], n + 1,
                                          s["cT_lo"])
                            for c in range(DC):
                                remainder(bank(4 + c), xnT[:, 0, c, :], xnT[:, 1, c, :], s["xT_hi"], c + 1, s["xT_lo"])
                            for c in range(DC):
                                remainder(bank(6 + c), qT[:, 0, c, :], qT[:, 1, c, :], s["q_hi"], c + 1, s["q_lo"])

                            def row_max(t):
                                dve.wait_ge(s["s_ps"], t + 1)
                                own(dve.tensor_reduce(mx[:, t:t + 1],
                                                      PS[:, 0:MG, :].rearrange("p g n -> p (g n)")[:, 0:M], AX, ALU.max))
                                dve.tensor_scalar(nb[:, t:t + 1], mx[:, t:t + 1], -XSCALE, None, ALU.mult)\
                                    .then_inc(s["s_max"], 1)

                            row_max(0)
                            for t in range(MT):
                                m = mrows(t)
                                dve.wait_ge(s["cm_hi"], t + 1)
                                dve.scalar_tensor_tensor(out=cm[0:m, 1, t, :], in0=cn[0:m, t, :],
                                                         scalar=mask01[0:m, t:t + 1],
                                                         in1=cm[0:m, 0, t, :].bitcast(F32), op0=ALU.mult,
                                                         op1=ALU.subtract).then_inc(s["cm_lo"], 1)
                            for t in range(NT):
                                for g in range(MG):
                                    n = t * MG + g
                                    k = min(4, MT - 4 * g)
                                    m = mrows(4 * g + k - 1)
                                    remainder(PS[0:m, 4 + n % 2, 0:k * P],
                                              pT[0:m, 0, 4 * g:4 * g + k, :].rearrange("p t n -> p (t n)"),
                                              pT[0:m, 1, 4 * g:4 * g + k, :].rearrange("p t n -> p (t n)"),
                                              s["pT_hi"], n + 1, s["pT_lo"])
                                dve.wait_ge(s["p_ready"], t + 1)
                                dve.reciprocal(ri[:, t:t + 1], rs[:, t:t + 1]).then_inc(s["ac_inv"], 1)
                                if t + 1 < NT:
                                    row_max(t + 1)
                                dve.wait_ge(s["ac_hi"], t + 1)
                                dve.scalar_tensor_tensor(out=ac[:, 1, t, :], in0=PS[:, 6 + t % 2, 0:D],
                                                         scalar=ri[:, t:t + 1], in1=ac[:, 0, t, :].bitcast(F32),
                                                         op0=ALU.mult, op1=ALU.subtract).then_inc(s["ac_lo"], 1)
                            for r in range(2):
                                remainder(bank(4 + r), tT[:, 0, r, :],
                                          tT[:, 1, r, :], s["t_hi"], r + 1, s["t_lo"])
                            dve.wait_ge(s["xr_ready"], NT)
                            for r in range(2):
                                for c in range(DC):
                                    dve.wait_ge(s["y_ps"], 2 * r + c + 1)
                                    dve.tensor_tensor(x1[:, 2 * c + r, :], PS[:, 2 * r + c, 0:D], xr[:, 2 * c + r, :],
                                                      ALU.add)
                    clear(every)

                with ExitStack() as st:
                    h0 = sb("h0", [P, NT, D], stack=st)
                    hn = sb("h_norm", [P, NT, D], stack=st)
                    h32 = sb("h_t32", [P, DC, S], stack=st)
                    hT = sb("h_ts", [P, 2, DC, S], F32R, stack=st)
                    qk = sb("qk_t", [P, 2, 2 * DC, S], F32R, stack=st)
                    va = sb("v_ones", [P, NT, H, 32], stack=st)
                    Qs = sb("q_stack", [P, H // 2, S], F32R, stack=st)
                    Ks = sb("k_stack", [P, H // 2, S], F32R, stack=st)
                    mx = sb("s_max_rows", [P, NT, H], stack=st)
                    m2 = sb("neg_max_rows", [4, HG, 2, S], F32R, stack=st)
                    pe_ring = 3
                    pb = sb("s_probs", [P, pe_ring, 4, S], stack=st)
                    late = qk[:, :, :, :].bitcast(F32)
                    oT = late[:, 0]
                    rec = sb("s_inv", [P, NT, H], stack=st)
                    on = late[:, 1, 0:2, :].rearrange("p a (b d) -> p (a b) d", d=D)
                    x2 = late[:, 1, 2:4, :].rearrange("p a (b d) -> p (a b) d", d=D)
                    oS = hT
                    lg = sb("logits", [P, NT, E], stack=st)
                    top = sb("top", [P, NT, 8], stack=st)
                    ti = sb("top_index", [P, NT, 8], U32, stack=st)
                    tf = sb("top_index_f", [P, NT, 8], stack=st)
                    dd = sb("top_diff", [P, NT], stack=st)
                    e2 = sb("top_exp", [P, NT], stack=st)
                    sm = sb("top_sum", [P, NT], stack=st)
                    w1c = sb("top_w1", [P, NT], stack=st)
                    w2c = sb("top_w2", [P, NT], stack=st)
                    wa = sb("w_first", [P, NT, E], stack=st)
                    wb = sb("w_second", [P, NT, E], stack=st)
                    wT = sb("w_t", [E, S], stack=st)
                    s, every = semaphores(st, "stats inv hn_ready own hT_ps h32_ready hT_hi hT_lo qk_ps qk_hi qk_lo v_ps v_ready "
                                              "ones_ready stacked s_ps s_max m_ps m_hi m_lo m_rows st_ps p_ready pv_done o_ps "
                                              "oT_ready on_ps on_ready oS_ps oS_hi oS_lo x2_ps x2_ready h2_ready h2T_ps lg_ps "
                                              "d_ready e_ready w_ready wT_ps wT_ready bias_ps h0_ready h0b stored hT_kept")
                    LAG = 24
                    UNITS = H * NT

                    def s_unit(i):
                        return i // NT, i % NT

                    def t_unit(j):
                        return j // (4 * NT), (j // 4) % NT, j % 4

                    with nc.Block() as block:
                        @block.sync
                        def _(sp):
                            sp.wait_ge(s["ones_ready"], 1)
                            sp.wait_ge(s["qk_lo"], 2 * DC)
                            heads = P // DK
                            for hh in range(heads):
                                row = 64 * (hh % 2)
                                at = hh // 2
                                for base, dst, copies in ((0, Qs, (0, 1, 0)), (DC, Ks, (0, 0, 1))):
                                    for n, part in enumerate(copies):
                                        sp.dma_start(
                                            dst[row + n * DK:row + (n + 1) * DK, at:at + heads // 2 * (DC - 1) + 1:heads // 2, :]
                                            .bitcast(F32),
                                            qk[hh * DK:(hh + 1) * DK, part, base:base + DC, :].bitcast(F32)).then_inc(s["stacked"], 16)
                            for g in range(HG):
                                sp.wait_ge(s["m_lo"], g + 1)
                                for h in range(4):
                                    row = 64 * (h % 2) + 3 * DK
                                    sp.dma_start(Qs[row:row + 2, (4 * g + h) // 2, :].bitcast(F32),
                                                 m2[h:h + 1, g, :, :].bitcast(F32))\
                                        .then_inc(s["m_rows"], 16)
                            sp.wait_ge(s["hT_lo"], 2 * DC)
                            sp.dma_start(hT_s[:, :, :, bass.ds(b * S, S)].rearrange("p a c n -> p (a c) n").bitcast(F32),
                                         hT[:, :, :, :].rearrange("p a c n -> p (a c) n").bitcast(F32)).then_inc(s["hT_kept"], 16)
                            sp.wait_ge(s["hT_kept"], 16)

                        @block.gpsimd
                        def _(pool):
                            pool.memset(Ks[:, :, :].bitcast(F32), 1.0).then_inc(s["ones_ready"], 1)
                            inverse_root(pool, s["stats"], s["inv"], 1)
                            pool.memset(va[:, :, :, DK:32], 1.0)
                            inverse_root(pool, s["stats"], s["inv"], 2)
                            pool.wait_ge(s["h0_ready"], 1)
                            for t in range(NT):
                                pool.tensor_tensor(h0[:, t, :], h0[:, t, :], bo_row[:, :], ALU.add).then_inc(s["h0b"], 1)
                            inverse_root(pool, s["stats"], s["inv"], 3)

                        @block.tensor
                        def _(pe):
                            def turn(src, b0, done):
                                for c in range(DC):
                                    for t in range(NT):
                                        ins = pe.transpose(PS[:, b0 + c, t * P:(t + 1) * P],
                                                           src[:, t, c * P:(c + 1) * P], ident[:, :])
                                    ins.then_inc(done, 1)

                            pe.wait_ge(s["hn_ready"], 1)
                            turn(hn, 0, s["hT_ps"])
                            pe.wait_ge(s["hT_lo"], DC)
                            for n in range(2 * DC):
                                product(pe, bank(2 + n), lambda a, k: Wqkv_s[:, a, k, n * P:(n + 1) * P],
                                        lambda a, k: hT[:, a, k, :], DC).then_inc(s["qk_ps"], 1)
                            for t in range(NT):
                                product(pe, PS[:, (6, 7, 0, 1)[t], 0:D], lambda a, k: hT[:, a, k, t * P:(t + 1) * P],
                                        lambda a, k: Wqkv_s[:, a, k, 2 * D:3 * D], DC).then_inc(s["v_ps"], 1)
                            pe.wait_ge(s["stacked"], 16 * 6 * (P // DK))
                            pe.wait_ge(s["v_ready"], NT)

                            def pv(u):
                                g, kt = u // NT, u % NT
                                pe.wait_ge(s["p_ready"], 4 * u + 4)
                                if kt == 0 and g:
                                    pe.wait_ge(s["oT_ready"], g)
                                for h in range(4):
                                    ins = pe.matmul(PS[32 * h:32 * h + 32, 6, :], va[:, kt, 4 * g + h, :],
                                                    pb[:, u % pe_ring, h, :], start=kt == 0, stop=kt == NT - 1)
                                ins.then_inc(s["pv_done"], 1)

                            for i in range(UNITS + LAG + 8):
                                if i < UNITS:
                                    h, qt = s_unit(i)
                                    r = 64 * (h % 2)
                                    if i >= 3:
                                        pe.wait_ge(s["s_max"], i - 2)
                                    pe.matmul(bank(i % 3), Qs[r:r + 3 * DK, h // 2, qt * P:(qt + 1) * P],
                                              Ks[r:r + 3 * DK, h // 2, :], start=True, stop=True).then_inc(s["s_ps"], 1)
                                if i % 16 == 2 and 1 <= i // 16 <= HG:
                                    g = i // 16 - 1
                                    pe.wait_ge(s["s_max"], 16 * (g + 1))
                                    if g:
                                        pe.wait_ge(s["m_lo"], g)
                                    for qt in range(NT):
                                        ins = pe.transpose(PS[0:4, 7, qt * P:(qt + 1) * P], mx[:, qt, 4 * g:4 * g + 4],
                                                           ident[:, :])
                                    ins.then_inc(s["m_ps"], 1)
                                j = i - LAG
                                if 0 <= j < UNITS:
                                    g, kt, hh = t_unit(j)
                                    h = 4 * g + hh
                                    r = 64 * (h % 2)
                                    if j % 16 == 0:
                                        pe.wait_ge(s["m_rows"], 64 * (g + 1))
                                    if j >= 3:
                                        pe.wait_ge(s["p_ready"], j - 2)
                                    pe.matmul(bank(3 + j % 3), Ks[r:r + 3 * DK + 2, h // 2, kt * P:(kt + 1) * P],
                                              Qs[r:r + 3 * DK + 2, h // 2, :], start=True, stop=True).then_inc(s["st_ps"], 1)
                                if j >= 6 and (j - 6) % 4 == 0 and (j - 6) // 4 < UNITS // 4:
                                    pv((j - 6) // 4)
                            pe.wait_ge(s["oT_ready"], HG)
                            for t in range(NT):
                                for g in range(HG):
                                    ins = pe.transpose(PS[:, t, g * P:(g + 1) * P], oT[:, g, t * P:(t + 1) * P], ident[:, :])
                                ins.then_inc(s["on_ps"], 1)
                            pe.wait_ge(s["on_ready"], NT)
                            turn(on, 4, s["oS_ps"])
                            pe.wait_ge(s["oS_lo"], DC)
                            for t in range(NT):
                                product(pe, PS[:, t, 0:D], lambda a, k: oS[:, a, k, t * P:(t + 1) * P],
                                        lambda a, k: Wo_s[:, a, k, :], DC).then_inc(s["x2_ps"], 1)
                            pe.wait_ge(s["h2_ready"], 1)
                            turn(hn, 4, s["h2T_ps"])
                            pe.wait_ge(s["hT_lo"], 2 * DC)
                            for t in range(NT):
                                ins = product(pe, PS[:, 6, t * E:(t + 1) * E], lambda a, k: hT[:, a, k, t * P:(t + 1) * P],
                                              lambda a, k: Wg_s[:, a, k, :], DC)
                            ins.then_inc(s["lg_ps"], 1)
                            pe.wait_ge(s["w_ready"], 1)
                            for t in range(NT):
                                ins = pe.transpose(PS[0:E, 7, t * P:(t + 1) * P], wa[:, t, :], ident[:, :])
                            ins.then_inc(s["wT_ps"], 1)
                            pe.wait_ge(s["wT_ready"], 1)
                            for t in range(NT):
                                pe.matmul(PS[:, t, 0:D], wT[:, t * P:(t + 1) * P], b2_sb[:, :], start=True, stop=True)\
                                    .then_inc(s["bias_ps"], 1)

                        @block.scalar
                        def _(act):
                            def affine(b0, g, c, ready, n):
                                act.wait_ge(ready, n)
                                act.activation(h32[:, c, :], bank(b0 + c), ACT.Identity, bias=cols[:, g + 1, c:c + 1],
                                               scale=cols[:, g, c:c + 1]).then_inc(s["h32_ready"], 1)
                                act.wait_ge(s["h32_ready"], (g // 2) * DC + c + 1)
                                act.activation(hT[:, 0, c, :], h32[:, c, :], ACT.Copy).then_inc(s["hT_hi"], 1)

                            for c in range(DC):
                                affine(0, 0, c, s["hT_ps"], c + 1)
                            for n in range(2 * DC):
                                act.wait_ge(s["qk_ps"], n + 1)
                                act.activation(qk[:, 0, n, :], bank(2 + n), ACT.Identity, bias=bqk_col[:, n:n + 1])\
                                    .then_inc(s["qk_hi"], 1)

                            def keep_o(g):
                                act.wait_ge(s["pv_done"], NT * (g + 1))
                                act.activation(oT[:, g, :], bank(6), ACT.Copy).then_inc(s["oT_ready"], 1)

                            def round_max(g):
                                act.wait_ge(s["m_ps"], g + 1)
                                act.activation(m2[:, g, 0, :], PS[0:4, 7, :], ACT.Copy, scale=-1.0).then_inc(s["m_hi"], 1)

                            round_max(0)
                            for j in range(UNITS):
                                if j % 16 == 10 and j // 16 + 1 < HG:
                                    round_max(j // 16 + 1)
                                u = j // 4
                                if j % 4 == 0 and u >= pe_ring:
                                    act.wait_ge(s["pv_done"], u - pe_ring + 1)
                                act.wait_ge(s["st_ps"], j + 1)
                                act.activation(pb[:, u % pe_ring, j % 4, :], bank(3 + j % 3), ACT.Exp, scale=SSCALE)\
                                    .then_inc(s["p_ready"], 1)
                                if j % 16 == 4 and j > 16:
                                    keep_o(j // 16 - 1)
                            keep_o(HG - 1)
                            for c in range(DC):
                                act.wait_ge(s["oS_ps"], c + 1)
                                act.activation(oS[:, 0, c, :], bank(4 + c), ACT.Copy).then_inc(s["oS_hi"], 1)
                            for c in range(DC):
                                affine(4, 2, c, s["h2T_ps"], c + 1)
                            act.wait_ge(s["d_ready"], 1)
                            act.activation(e2[:, :], dd[:, :], ACT.Exp).then_inc(s["e_ready"], 1)
                            act.wait_ge(s["wT_ps"], 1)
                            act.activation(wT[:, :], PS[0:E, 7, :], ACT.Copy).then_inc(s["wT_ready"], 1)

                        @block.vector
                        def _(dve):
                            own = chain(dve, s["own"])
                            layer_norm(dve, own, x1, h0, s["stats"], s["inv"], 1)
                            layer_norm(dve, own, h0, hn, s["stats"], s["inv"], 2)
                            dve.engine_nop().then_inc(s["hn_ready"], 1)
                            dve.engine_nop().then_inc(s["h0_ready"], 1)

                            def h_lo(n, c):
                                dve.wait_ge(s["hT_hi"], n)
                                dve.tensor_tensor(hT[:, 1, c, :], h32[:, c, :], hT[:, 0, c, :].bitcast(F32), ALU.subtract)\
                                    .then_inc(s["hT_lo"], 1)

                            for c in range(DC):
                                h_lo(c + 1, c)
                            for n in range(2 * DC):
                                dve.wait_ge(s["qk_hi"], n + 1)
                                dve.scalar_tensor_tensor(out=qk[:, 1, n, :], in0=bank(2 + n), scalar=bqk_col[:, n:n + 1],
                                                         in1=qk[:, 0, n, :].bitcast(F32), op0=ALU.add,
                                                         op1=ALU.subtract).then_inc(s["qk_lo"], 1)
                            for t in range(NT):
                                dve.wait_ge(s["v_ps"], t + 1)
                                dve.tensor_tensor(va[:, t, :, 0:DK],
                                                  PS[:, (6, 7, 0, 1)[t], 0:D].rearrange("p (h d) -> p h d", h=H),
                                                  bv_row[:, :].rearrange("p (h d) -> p h d", h=H), ALU.add)\
                                    .then_inc(s["v_ready"], 1)

                            def max_lo(g):
                                dve.wait_ge(s["m_hi"], g + 1)
                                dve.scalar_tensor_tensor(out=m2[:, g, 1, :], in0=PS[0:4, 7, :], scalar=-1.0,
                                                         in1=m2[:, g, 0, :].bitcast(F32), op0=ALU.mult,
                                                         op1=ALU.subtract).then_inc(s["m_lo"], 1)

                            for i in range(UNITS):
                                h, qt = s_unit(i)
                                dve.wait_ge(s["s_ps"], i + 1)
                                dve.tensor_reduce(mx[:, qt, h:h + 1], bank(i % 3), AX, ALU.max).then_inc(s["s_max"], 1)
                                if i % 16 == 4 and i > 16:
                                    max_lo(i // 16 - 1)
                            max_lo(HG - 1)
                            for t in range(NT):
                                o = PS[:, t, :].rearrange("p (h d) -> p h d", d=32)
                                dve.wait_ge(s["on_ps"], t + 1)
                                own(dve.reciprocal(rec[:, t, :], o[:, :, DK]))
                                dve.tensor_tensor(on[:, t, :].rearrange("p (h d) -> p h d", h=H), o[:, :, 0:DK],
                                                  rec[:, t, :].unsqueeze(2).to_broadcast([P, H, DK]), ALU.mult)\
                                    .then_inc(s["on_ready"], 1)
                            for c in range(DC):
                                dve.wait_ge(s["oS_hi"], c + 1)
                                dve.tensor_tensor(oS[:, 1, c, :], bank(4 + c), oS[:, 0, c, :].bitcast(F32), ALU.subtract)\
                                    .then_inc(s["oS_lo"], 1)
                            dve.wait_ge(s["h0b"], NT)
                            for t in range(NT):
                                dve.wait_ge(s["x2_ps"], t + 1)
                                own(dve.tensor_tensor(x2[:, t, :], PS[:, t, 0:D], h0[:, t, :], ALU.add))
                            layer_norm(dve, own, x2, hn, s["stats"], s["inv"], 3)
                            dve.engine_nop().then_inc(s["h2_ready"], 1)
                            for t in range(NT):
                                own(dve.tensor_tensor(x2[:, t, :], x2[:, t, :], x1[:, t, :], ALU.add))
                            for c in range(DC):
                                h_lo(DC + c + 1, c)
                            dve.wait_ge(s["lg_ps"], 1)
                            for t in range(NT):
                                own(dve.tensor_tensor(lg[:, t, :], PS[:, 6, t * E:(t + 1) * E], gb_row[:, :], ALU.add))
                                own(dve.max(top[:, t, :], lg[:, t, :]))
                                own(dve.max_index(ti[:, t, :], top[:, t, :], lg[:, t, :]))
                            own(dve.tensor_copy(tf[:, :, :], ti[:, :, :]))
                            dve.tensor_tensor(dd[:, :], top[:, :, 1], top[:, :, 0], ALU.subtract).then_inc(s["d_ready"], 1)
                            dve.wait_ge(s["e_ready"], 1)
                            own(dve.tensor_scalar(sm[:, :], e2[:, :], 1.0, None, ALU.add))
                            own(dve.reciprocal(w1c[:, :], sm[:, :]))
                            own(dve.tensor_tensor(w2c[:, :], e2[:, :], w1c[:, :], ALU.mult))
                            for t in range(NT):
                                own(dve.tensor_scalar(wa[:, t, :], iota_e[:, :], tf[:, t, 0:1], w1c[:, t:t + 1],
                                                      ALU.is_equal, ALU.mult))
                                own(dve.tensor_scalar(wb[:, t, :], iota_e[:, :], tf[:, t, 1:2], w2c[:, t:t + 1],
                                                      ALU.is_equal, ALU.mult))
                            own(dve.tensor_tensor(wa[:, :, :], wa[:, :, :], wb[:, :, :], ALU.add))
                            dve.tensor_copy(ew[:, bass.ds(b * NT, NT), :], wa[:, :, :]).then_inc(s["w_ready"], 1)
                            for t in range(NT):
                                dve.wait_ge(s["bias_ps"], t + 1)
                                dve.tensor_tensor(acc[:, bass.ds(b * NT + t, 1), :].rearrange("p a d -> p (a d)"),
                                                  PS[:, t, 0:D], x2[:, t, :], ALU.add)
                    clear(every)

        with ExitStack() as st:
            w1r = sb("w1_raw", [P, DC, DFF], stack=st)
            w2r = sb("w2_raw", [P, FT, D], stack=st)
            w1s = sb("w1_s", [P, 2, 2, DC, DFF], F32R, stack=st)
            w2s = sb("w2_s", [P, 2, 2, FT, D], F32R, stack=st)
            RING = 3
            hid = sb("hid", [P, RING, 512], stack=st)
            hs = sb("hid_s", [P, RING, 2, 512], F32R, stack=st)
            ewc = sb("ew_now", [P, NB, 2], stack=st)
            b1c = sb("b1_now", [P, 2 * FT], stack=st)
            s, every = semaphores(st, "w_in w_split own cols_ready hid_ps hid_ready hid_hi hid_lo used y_ps y_read stored w_hi")
            TB = B * S // 512
            UNITS = 2 * TB * FT

            def load(sp, e):
                sp.dma_start(w1r[:, :, :], W1[e].rearrange("a (c p) f -> p (a c) f", p=P)).then_inc(s["w_in"], 16)
                sp.dma_start(w2r[:, :, :], W2[e].rearrange("a (c p) d -> p (a c) d", p=P)).then_inc(s["w_in"], 16)

            def split(pool, buf, n):
                pool.wait_ge(s["w_in"], 32 * n)
                pool.tensor_copy(w1s[:, buf, 0], w1r[:, :, :]).then_inc(s["w_hi"], 1)
                pool.tensor_copy(w2s[:, buf, 0], w2r[:, :, :]).then_inc(s["w_hi"], 1)
                pool.wait_ge(s["w_hi"], 2 * n)
                pool.tensor_tensor(w1s[:, buf, 1], w1r[:, :, :], w1s[:, buf, 0].bitcast(F32), ALU.subtract)\
                    .then_inc(s["w_split"], 1)
                pool.tensor_tensor(w2s[:, buf, 1], w2r[:, :, :], w2s[:, buf, 0].bitcast(F32), ALU.subtract)\
                    .then_inc(s["w_split"], 1)

            with nc.Block() as block:
                @block.sync
                def _(sp):
                    load(sp, slice(0, 1))

                @block.gpsimd
                def _(pool):
                    split(pool, 0, 1)
            clear(every)

            with nc.Fori(0, E // 2) as pair:
                with nc.Block() as block:
                    @block.sync
                    def _(sp):
                        load(sp, bass.ds(2 * pair + 1, 1))
                        sp.wait_ge(s["w_split"], 2)
                        load(sp, bass.ds((2 * pair + 2) % E, 1))
                        sp.wait_ge(s["w_in"], 64)

                    @block.gpsimd
                    def _(pool):
                        split(pool, 1, 1)
                        pool.wait_ge(s["y_read"], 4 * TB)
                        split(pool, 0, 2)

                    @block.tensor
                    def _(pe):
                        def hidden(u):
                            k, tb, f = u // (TB * FT), u // FT % TB, u % FT
                            if u == TB * FT:
                                pe.wait_ge(s["w_split"], 2)
                            if u >= 4:
                                pe.wait_ge(s["hid_ready"], u - 3)
                            product(pe, bank(u % 4), lambda a, c: w1s[:, k, a, c, f * P:(f + 1) * P],
                                    lambda a, c: hT_s[:, a, c, tb * 512:(tb + 1) * 512], DC).then_inc(s["hid_ps"], 1)

                        def outputs(u):
                            k, f = u // (TB * FT), u % FT
                            pe.wait_ge(s["hid_lo"], u + 1)
                            if f == 0 and u:
                                pe.wait_ge(s["y_read"], 4 * (u // FT))
                            for t in range(4):
                                for n, (a, c) in enumerate(PASSES):
                                    ins = pe.matmul(PS[:, 4 + t, 0:D], hs[:, u % RING, a, t * P:(t + 1) * P],
                                                    w2s[:, k, c, f, :], start=f == 0 and n == 0,
                                                    stop=f == FT - 1 and n == 2)
                                if f == FT - 1:
                                    ins.then_inc(s["y_ps"], 1)
                                elif t == 3:
                                    ins.then_inc(s["used"], 1)

                        for u in range(UNITS + 2):
                            if u < UNITS:
                                hidden(u)
                            if u >= 2:
                                outputs(u - 2)

                    def free(eng, u):
                        v = u - RING
                        if v % FT == FT - 1:
                            eng.wait_ge(s["y_ps"], 4 * (v // FT + 1))
                        else:
                            eng.wait_ge(s["used"], v // FT * (FT - 1) + v % FT + 1)

                    @block.scalar
                    def _(act):
                        act.wait_ge(s["cols_ready"], 1)
                        for u in range(UNITS):
                            k, f = u // (TB * FT), u % FT
                            act.wait_ge(s["hid_ps"], u + 1)
                            if u >= RING:
                                act.wait_ge(s["hid_lo"], u - RING + 1)
                            act.activation(hid[:, u % RING, :], bank(u % 4), ACT.Relu,
                                           bias=b1c[:, k * FT + f:k * FT + f + 1]).then_inc(s["hid_ready"], 1)
                            if u >= RING:
                                free(act, u)
                            act.wait_ge(s["hid_ready"], u + 1)
                            act.activation(hs[:, u % RING, 0, :], hid[:, u % RING, :], ACT.Copy).then_inc(s["hid_hi"], 1)

                    def add_block(dve, n):
                        k, tb = n // TB, n % TB
                        for t in range(4):
                            i = 4 * tb + t
                            dve.wait_ge(s["y_ps"], 4 * n + t + 1)
                            dve.scalar_tensor_tensor(out=acc[:, i, :], in0=PS[:, 4 + t, 0:D], scalar=ewc[:, i, k:k + 1],
                                                     in1=acc[:, i, :], op0=ALU.mult, op1=ALU.add).then_inc(s["y_read"], 1)

                    @block.vector
                    def _(dve):
                        own = chain(dve, s["own"])
                        own(dve.tensor_copy(ewc[:, :, :], ew[:, :, bass.ds(2 * pair, 2)]))
                        dve.tensor_copy(b1c[:, :], b1_col[:, bass.ds(2 * FT * pair, 2 * FT)]).then_inc(s["cols_ready"], 1)
                        for u in range(UNITS):
                            k, tb, f = u // (TB * FT), u // FT % TB, u % FT
                            dve.wait_ge(s["hid_hi"], u + 1)
                            dve.tensor_tensor(hs[:, u % RING, 1, :], hid[:, u % RING, :],
                                              hs[:, u % RING, 0, :].bitcast(F32), ALU.subtract).then_inc(s["hid_lo"], 1)
                            if f == 1 and u > FT:
                                add_block(dve, u // FT - 1)
                        add_block(dve, 2 * TB - 1)
                clear(every)

            with nc.Block() as block:
                @block.sync
                def _(sp):
                    sp.dma_start(out.rearrange("b (c p r) d -> p (b c) r d", p=P, r=2),
                                 acc[:, :, :].rearrange("p (c r) d -> p c r d", r=2)).then_inc(s["stored"], 16)
                    sp.wait_ge(s["stored"], 16)


_INS = ['x', 'ctx_1024', 'mask_S2_ik0', 'L0_xattn_qkv_w', 'L0_xattn_proj_w', 'L0_xattn_proj_b', 'L0_ffn_ln1_g',
        'L0_ffn_ln1_b', 'L0_ffn_w_qkv', 'L0_ffn_b_qkv', 'L0_ffn_w_o', 'L0_ffn_b_o', 'L0_ffn_ln2_g', 'L0_ffn_ln2_b',
        'L0_ffn_gate_w', 'L0_ffn_gate_b', 'L0_ffn_W1', 'L0_ffn_b1', 'L0_ffn_W2', 'L0_ffn_b2']


def kernel(**inputs):
    import numpy as _np
    import concourse.bacc as _bacc
    from concourse import mybir as _mybir
    from concourse.bass_utils import run_bass_kernel_spmd as _run

    nc = _bacc.Bacc("TRN2", target_bir_lowering=False, num_devices=1)
    arrays, args = {}, []
    for name in _INS:
        a = _np.ascontiguousarray(inputs[name])
        arrays[f"in_{name}_dram"] = a
        args.append(nc.dram_tensor(f"in_{name}_dram", a.shape, _mybir.dt.from_np(a.dtype), kind="ExternalInput").ap())
    args.append(nc.dram_tensor("out_0_dram", (4, 512, 256), _mybir.dt.float32, kind="ExternalOutput").ap())
    xattn_moe_kernel(nc, *args)
    r = _run(nc, [arrays], core_ids=[0])
    return r.results[0]["out_0_dram"]
```

```python
from contextlib import ExitStack

import numpy as np

import concourse.bass as bass
from concourse import mybir

P = 128
F32 = mybir.dt.float32
F32R = mybir.dt.float32r
I32 = mybir.dt.int32
U32 = mybir.dt.uint32
ALU = mybir.AluOpType
ACT = mybir.ActivationFunctionType
AX = mybir.AxisListType.X

PASSES = ((1, 0), (0, 1), (0, 0))


def xattn_moe_kernel(nc, x, ctx_in, mask, qkv_w, proj_w, proj_b, ln1_g, ln1_b, w_qkv, b_qkv, w_o, b_o,
                     ln2_g, ln2_b, gate_w, gate_b, W1, b1, W2, b2, out):
    B, S, D = x.shape
    M = ctx_in.shape[1]
    E, _, DFF = W1.shape
    DC = D // P
    NT = S // P
    MT = -(-M // P)
    ML = M - (MT - 1) * P
    MG = -(-M // 512)
    H = 16
    DK = D // H
    HG = H // 4
    FT = DFF // P
    NB = B * NT
    XSCALE = float(D // 8) ** -0.5
    SSCALE = float(DK) ** -0.5
    EPS = 1e-5

    def mrows(t):
        return P if t < MT - 1 else ML

    def mcols(g):
        return min(512, M - 512 * g)

    def bcast_rows(v, n):
        return v.rearrange("(a n) -> a n", a=1).to_broadcast([P, n])

    with ExitStack() as keep:
        def sb(name, shape, dt=F32, stack=keep):
            return stack.enter_context(nc.sbuf_tensor(name, shape, dt))

        PS = keep.enter_context(nc.psum_tensor("banks", [P, 8, 512], F32))

        def bank(i):
            return PS[:, i, :]

        ident = sb("ident", [P, P])
        halves = sb("minus_half", [P, NT])
        M_s = sb("wq_wk", [P, 2, DC, D], F32R)
        WvT_s = sb("wv_t", [P, 2, DC, D], F32R)
        PT_s = sb("proj_t", [P, 2, DC, D], F32R)
        Wqkv_s = sb("w_qkv_s", [P, 2, DC, 3 * D], F32R)
        Wo_s = sb("w_o_s", [P, 2, DC, D], F32R)
        Wg_s = sb("gate_s", [P, 2, DC, E], F32R)
        b2_sb = sb("b2_sb", [E, D])
        pb_row = sb("proj_b_row", [P, D])
        bo_row = sb("b_o_row", [P, D])
        bv_row = sb("b_v_row", [P, D])
        gb_row = sb("gate_b_row", [P, E])
        iota_e = sb("iota_e", [P, E])
        cols = sb("cols", [P, 4, DC])
        bqk_col = sb("bqk_col", [P, 2 * DC])
        mask01 = sb("mask01", [P, MT])
        pile = sb("pile", [P, 2, 2, 4, P], F32R)
        ones_at = sb("ones_at", [P, 1])
        b1_col = sb("b1_col", [P, E * FT])
        tri = sb("before", [P, P])
        ones = sb("ones", [P, P])
        pick = sb("pick", [P, 2, NB, E])
        gate = sb("gate", [P, 2, NB])
        h_rows = nc.dram_tensor("h_rows", (NB * P, D), F32).ap()
        base_rows = nc.dram_tensor("base_rows", (NB * P, D), F32).ap()
        BT = 2 * P
        BODY = 8
        NBLK = -(-(2 * NB * P // BT + E - 1) // BODY) * BODY
        sorted_in = nc.dram_tensor("sorted_in", ((NBLK + 1) * BT, D), F32).ap()
        sorted_out = nc.dram_tensor("sorted_out", (NBLK * BT, D), F32).ap()
        zeroed = keep.enter_context(nc.semaphore("zeroed"))
        ZR = (NBLK + 1) * BT // P
        ZC = ZR // 5

        def clear(sems):
            for s in sems:
                nc.sync.sem_clear(s)
            nc.all_engine_barrier()

        def semaphores(stack, names):
            made = {n: stack.enter_context(nc.semaphore(n)) for n in names.split()}
            return made, list(made.values())

        def chain(eng, sem):
            count = [0]

            def step(ins):
                count[0] += 1
                ins.then_inc(sem, 1)
                eng.wait_ge(sem, count[0])
            return step

        def product(pe, out_ap, lhsT, rhs, k_chunks, first=True, last=True):
            n = 0
            for k in range(k_chunks):
                for a, b in PASSES:
                    ins = pe.matmul(out_ap, lhsT(a, k), rhs(b, k), start=first and n == 0,
                                    stop=last and n == 3 * k_chunks - 1)
                    n += 1
            return ins

        with ExitStack() as st:
            wq_raw = sb("wq_raw", [P, 3 * DC, D], stack=st)
            pj_raw = sb("pj_raw", [P, DC, D], stack=st)
            wqkv_raw = sb("wqkv_raw", [P, DC, 3 * D], stack=st)
            wo_raw = sb("wo_raw", [P, DC, D], stack=st)
            wg_raw = sb("wg_raw", [P, DC, E], stack=st)
            mask_i = sb("mask_i", [P, MT], I32, stack=st)
            mask_f = sb("mask_f", [P, MT], stack=st)
            b1_rows = sb("b1_rows", [E * FT, P], stack=st)
            zeros = sb("zeros", [P, ZC, D], stack=st)
            two = sb("ones_at_terms", [P, 2], stack=st)
            s, every = semaphores(st, "w_loaded pile_zero ident_zero ident_ready w_psum w_hi w_lo raw_hi v_loaded own zero_ready tri_one")
            with nc.Block() as block:
                @block.sync
                def _(sp):
                    loads = [
                        (wq_raw[:, :, :], qkv_w.rearrange("(c p) d -> p c d", p=P)),
                        (pj_raw[:, :, :], proj_w.rearrange("(c p) d -> p c d", p=P)),
                        (b1_rows[:, :], b1.rearrange("e (f p) -> (e f) p", p=P)),
                        (wqkv_raw[:, :, :], w_qkv.rearrange("(c p) n -> p c n", p=P)),
                        (wo_raw[:, :, :], w_o.rearrange("(c p) n -> p c n", p=P)),
                        (wg_raw[:, :, :], gate_w.rearrange("(c p) e -> p c e", p=P)),
                    ]
                    for dst, src in loads:
                        sp.dma_start(dst, src).then_inc(s["w_loaded"], 16)
                    sp.wait_ge(s["zero_ready"], 1)
                    zv = sorted_in.rearrange("(p r) d -> p r d", p=P)
                    for z in range(0, ZR, ZC):
                        sp.dma_start(zv[:, z:z + ZC, :], zeros[:, :, :]).then_inc(zeroed, 16)
                    sp.wait_ge(zeroed, 16 * 5)
                    sp.wait_ge(s["w_loaded"], 16 * len(loads))

                @block.scalar
                def _(act):
                    vectors = [
                        (b2_sb[:, :], b2),
                        (pb_row[:, :], bcast_rows(proj_b, D)),
                        (bo_row[:, :], bcast_rows(b_o, D)),
                        (bv_row[:, :], bcast_rows(b_qkv[2 * D:3 * D], D)),
                        (gb_row[:, :], bcast_rows(gate_b, E)),
                        (bqk_col[:, :], b_qkv[0:2 * D].rearrange("(c p) -> p c", p=P)),
                        (mask_i[:, 0:MT - 1], mask[0:(MT - 1) * P].rearrange("(t p) -> p t", p=P)),
                        (mask_i[0:ML, MT - 1:MT], mask[(MT - 1) * P:M].rearrange("(t p) -> p t", t=1)),
                    ] + [(cols[:, n, :], v.rearrange("(c p) -> p c", p=P))
                         for n, v in enumerate((ln1_g, ln1_b, ln2_g, ln2_b))]
                    for dst, src in vectors:
                        act.dma_start(dst, src, allow_slow_non_contiguous=True).then_inc(s["v_loaded"], 16)
                    for n, dst in enumerate([M_s] * DC + [WvT_s] * DC + [PT_s] * DC):
                        act.wait_ge(s["w_psum"], n + 1)
                        act.activation(dst[:, 0, n % DC, :], PS[:, n, 0:D], ACT.Copy).then_inc(s["w_hi"], 1)
                    act.wait_ge(s["w_psum"], 3 * DC + 1)
                    act.activation(b1_col[:, :], PS[:, 6, 0:E * FT], ACT.Copy)
                    act.wait_ge(s["v_loaded"], 16 * len(vectors))

                @block.gpsimd
                def _(pool):
                    pool.memset(ident[:, :], 0.0).then_inc(s["ident_zero"], 1)
                    pool.memset(pile[:, :, :, :, :].bitcast(F32), 0.0).then_inc(s["pile_zero"], 1)
                    pool.memset(ones[:, :], 1.0).then_inc(s["tri_one"], 1)
                    pool.memset(halves[:, :], -0.5)
                    for e in range(E):
                        pool.memset(iota_e[:, e:e + 1], float(e))
                    pool.wait_ge(s["ident_zero"], 1)
                    pool.affine_select(out=ident[:, :], in_=ident[:, :], compare_op=ALU.not_equal, fill=1.0,
                                       base=0, pattern=[[-1, P]], channel_multiplier=1).then_inc(s["ident_ready"], 1)
                    pool.wait_ge(s["tri_one"], 1)
                    pool.affine_select(out=tri[:, :], in_=ones[:, :], compare_op=ALU.is_gt, fill=0.0,
                                       base=0, pattern=[[1, P]], channel_multiplier=-1)
                    pool.wait_ge(s["w_loaded"], 96)
                    for dst, src in ((Wqkv_s, wqkv_raw), (Wo_s, wo_raw), (Wg_s, wg_raw)):
                        pool.tensor_copy(dst[:, 0], src[:, :, :]).then_inc(s["raw_hi"], 1)

                @block.tensor
                def _(pe):
                    pe.wait_ge(s["ident_ready"], 1)
                    pe.wait_ge(s["w_loaded"], 96)
                    for c in range(DC):
                        for k in range(DC):
                            ins = pe.matmul(PS[:, c, 0:D], wq_raw[:, k, c * P:(c + 1) * P], wq_raw[:, DC + k, :],
                                            start=k == 0, stop=k == DC - 1)
                        ins.then_inc(s["w_psum"], 1)
                    for raw, base, b0 in ((wq_raw, 2 * DC, DC), (pj_raw, 0, 2 * DC)):
                        for c in range(DC):
                            for k in range(DC):
                                ins = pe.transpose(PS[:, b0 + c, k * P:(k + 1) * P],
                                                   raw[:, base + k, c * P:(c + 1) * P], ident[:, :])
                            ins.then_inc(s["w_psum"], 1)
                    pe.transpose(PS[:, 6, 0:E * FT], b1_rows[:, :], ident[0:E * FT, 0:E * FT]).then_inc(s["w_psum"], 1)

                @block.vector
                def _(dve):
                    own = chain(dve, s["own"])
                    dve.memset(zeros[:, :, :], 0.0).then_inc(s["zero_ready"], 1)
                    for n, dst in enumerate([M_s] * DC + [WvT_s] * DC + [PT_s] * DC):
                        dve.wait_ge(s["w_hi"], n + 1)
                        dve.tensor_tensor(dst[:, 1, n % DC, :], PS[:, n, 0:D], dst[:, 0, n % DC, :].bitcast(F32),
                                          ALU.subtract)
                    for n, (dst, src) in enumerate(((Wqkv_s, wqkv_raw), (Wo_s, wo_raw), (Wg_s, wg_raw))):
                        dve.wait_ge(s["raw_hi"], n + 1)
                        dve.tensor_tensor(dst[:, 1], src[:, :, :], dst[:, 0].bitcast(F32), ALU.subtract)
                    dve.wait_ge(s["ident_ready"], 1)
                    dve.wait_ge(s["pile_zero"], 1)
                    heads = ident[:, :].rearrange("p (a b i) -> p a b i", b=2, i=DK)
                    for q_or_k, copies in enumerate(((0, 1, 0), (0, 0, 1))):
                        for n, part in enumerate(copies):
                            dst = pile[:, q_or_k, part].rearrange("p a (b n i) -> p a b n i", b=2, i=DK)
                            dve.tensor_copy(dst[:, :, :, n, :], heads)
                    own(dve.tensor_reduce(two[:, :], ident[:, :].rearrange("p (b n) -> p b n", b=2)
                                          [:, :, 3 * DK:3 * DK + 2], AX, ALU.add))
                    dve.tensor_tensor(ones_at[:, :], two[:, 0:1], two[:, 1:2], ALU.add)
                    dve.wait_ge(s["v_loaded"], 16 * 12)
                    for p, c0, c1 in ((P, 0, MT - 1), (ML, MT - 1, MT)):
                        own(dve.tensor_copy(mask_f[0:p, c0:c1], mask_i[0:p, c0:c1]))
                        dve.tensor_scalar(mask01[0:p, c0:c1], mask_f[0:p, c0:c1], 0.0, None, ALU.not_equal)
            clear(every)

        with ExitStack() as bs:
            x1 = sb("x1", [P, NT, D], stack=bs)
            st_a = sb("st_a", [P, NT, 6], stack=bs)
            mv = sb("mean_var", [P, NT, 2], stack=bs)
            veps = sb("var_eps", [P, NT], stack=bs)
            rstd = sb("rstd", [P, NT], stack=bs)

            def layer_norm(dve, own, src, dst, stats_ready, rstd_ready, n):
                for t in range(NT):
                    own(dve.bn_stats(st_a[:, t, :], src[:, t, :]))
                for t in range(NT):
                    own(dve.bn_aggr(mv[:, t, :], st_a[:, t, :]))
                dve.tensor_scalar(veps[:, :], mv[:, :, 1], EPS, None, ALU.add).then_inc(stats_ready, 1)
                dve.wait_ge(rstd_ready, n)
                for t in range(NT):
                    ins = dve.tensor_scalar(dst[:, t, :], src[:, t, :], mv[:, t, 0:1], rstd[:, t:t + 1],
                                            ALU.subtract, ALU.mult)
                    own(ins)

            def inverse_root(pool, stats_ready, rstd_ready, n):
                pool.wait_ge(stats_ready, n)
                pool.tensor_tensor(rstd[:, :], veps[:, :], halves[:, :], ALU.pow).then_inc(rstd_ready, 1)

            with nc.Fori(0, B) as b:
                with ExitStack() as st:
                    xq = sb("x_tokens", [P, NT, D], stack=st)
                    xr = sb("x_residual", [P, NT, D], stack=st)
                    xn = sb("x_norm", [P, NT, D], stack=st)
                    xnT = sb("x_norm_t", [P, 2, DC, S], F32R, stack=st)
                    qT = sb("q_t", [P, 2, DC, S], F32R, stack=st)
                    cn = sb("ctx", [P, MT, D], stack=st)
                    cm = sb("ctx_masked", [P, 2, MT, D], F32R, stack=st)
                    cT = sb("ctx_t", [P, 2, DC, M + 1], F32R, stack=st)
                    pr = sb("probs", [P, M], stack=st)
                    pT = sb("probs_t", [P, 2, MT, P], F32R, stack=st)
                    mx = sb("row_max", [P, NT], stack=st)
                    nb = sb("neg_max", [P, NT], stack=st)
                    rs = sb("row_sum", [P, NT], stack=st)
                    ri = sb("row_inv", [P, NT], stack=st)
                    ac = sb("attn_ctx", [P, 2, NT, D], F32R, stack=st)
                    tT = xnT
                    s, every = semaphores(st, "xq_in ctx_in xr_in stats inv xn_ready own cT_ps cT_hi cT_lo cm_hi cm_lo "
                                              "xT_ps xT_hi xT_lo q_ps q_hi q_lo s_ps s_max p_ready pT_ps pT_hi pT_lo "
                                              "ac_ps ac_inv ac_hi ac_lo t_ps t_hi t_lo y_ps xr_ready pzero")
                    groups = [(g, c) for g in range(MG) for c in range(DC)]
                    xb = x[bass.ds(b, 1)].rearrange("a n d -> (a n) d")
                    cb = ctx_in[bass.ds(b, 1)].rearrange("a n d -> (a n) d")
                    with nc.Block() as block:
                        @block.sync
                        def _(sp):
                            sp.dma_start(xq[:, :, :], xb.rearrange("(t p) d -> p t d", p=P)).then_inc(s["xq_in"], 16)
                            sp.dma_start(cn[:, 0:MT - 1, :], cb[0:(MT - 1) * P, :].rearrange("(t p) d -> p t d", p=P))\
                                .then_inc(s["ctx_in"], 16)
                            sp.dma_start(cn[0:ML, MT - 1, :], cb[(MT - 1) * P:M, :]).then_inc(s["ctx_in"], 16)
                            sp.dma_start(xr[:, :, :].rearrange("p (c r) d -> p c r d", r=2),
                                         xb.rearrange("(c p r) d -> p c r d", p=P, r=2)).then_inc(s["xr_in"], 16)
                            sp.wait_ge(s["xr_in"], 16)

                        @block.gpsimd
                        def _(pool):
                            inverse_root(pool, s["stats"], s["inv"], 1)
                            pool.wait_ge(s["ctx_in"], 32)
                            for t in range(MT):
                                m = mrows(t)
                                pool.tensor_scalar(cm[0:m, 0, t, :], cn[0:m, t, :], mask01[0:m, t:t + 1], None,
                                                   ALU.mult).then_inc(s["cm_hi"], 1)
                            pool.wait_ge(s["xr_in"], 16)
                            for t in range(NT):
                                pool.tensor_tensor(xr[:, t, :], xr[:, t, :], pb_row[:, :], ALU.add).then_inc(s["xr_ready"], 1)

                        @block.tensor
                        def _(pe):
                            pe.wait_ge(s["ctx_in"], 32)
                            for n, (g, c) in enumerate(groups):
                                if n >= 4:
                                    pe.wait_ge(s["cT_lo"], n - 3)
                                for t in range(4 * g, min(4 * g + 4, MT)):
                                    m = mrows(t)
                                    o = (t - 4 * g) * P
                                    ins = pe.transpose(PS[:, n % 4, o:o + m], cn[0:m, t, c * P:(c + 1) * P],
                                                       ident[0:m, 0:m])
                                ins.then_inc(s["cT_ps"], 1)
                            pe.wait_ge(s["xn_ready"], 1)
                            for c in range(DC):
                                for t in range(NT):
                                    ins = pe.transpose(PS[:, 4 + c, t * P:(t + 1) * P], xn[:, t, c * P:(c + 1) * P],
                                                       ident[:, :])
                                ins.then_inc(s["xT_ps"], 1)
                            pe.wait_ge(s["xT_lo"], DC)
                            for c in range(DC):
                                product(pe, bank(6 + c), lambda a, k: M_s[:, a, k, c * P:(c + 1) * P],
                                        lambda a, k: xnT[:, a, k, :], DC).then_inc(s["q_ps"], 1)
                            pe.wait_ge(s["q_lo"], DC)
                            pe.wait_ge(s["cT_lo"], len(groups))

                            def scores(t):
                                if t:
                                    pe.wait_ge(s["p_ready"], t)
                                for g in range(MG):
                                    w = mcols(g) + mcols(g) % 2
                                    ins = product(pe, PS[:, g, 0:w], lambda a, k: qT[:, a, k, t * P:(t + 1) * P],
                                                  lambda a, k: cT[:, a, k, g * 512:g * 512 + w], DC)
                                ins.then_inc(s["s_ps"], 1)

                            def turn_probs(t):
                                pe.wait_ge(s["p_ready"], t + 1)
                                for g in range(MG):
                                    n = t * MG + g
                                    if n >= 2:
                                        pe.wait_ge(s["pT_lo"], n - 1)
                                    for i in range(4 * g, min(4 * g + 4, MT)):
                                        m = mrows(i)
                                        o = (i - 4 * g) * P
                                        ins = pe.transpose(PS[0:m, 4 + n % 2, o:o + P], pr[:, i * P:i * P + m],
                                                           ident[:, :])
                                    ins.then_inc(s["pT_ps"], 1)

                            def attend(t):
                                pe.wait_ge(s["pT_lo"], MG * (t + 1))
                                if t == 0:
                                    pe.wait_ge(s["cm_lo"], MT)
                                if t >= 2:
                                    pe.wait_ge(s["ac_lo"], t - 1)
                                n = 0
                                for i in range(MT):
                                    m = mrows(i)
                                    for a, c in PASSES:
                                        ins = pe.matmul(PS[:, 6 + t % 2, 0:D], pT[0:m, a, i, :], cm[0:m, c, i, :],
                                                        start=n == 0, stop=n == 3 * MT - 1)
                                        n += 1
                                ins.then_inc(s["ac_ps"], 1)

                            scores(0)
                            for t in range(NT):
                                turn_probs(t)
                                if t + 1 < NT:
                                    scores(t + 1)
                                attend(t)
                            for r in range(2):
                                pe.wait_ge(s["ac_lo"], 2 * r + 2)
                                for c in range(DC):
                                    ins = product(pe, PS[:, 4 + r, c * D:(c + 1) * D],
                                                  lambda a, k: ac[:, a, 2 * r + k, c * P:(c + 1) * P],
                                                  lambda a, k: PT_s[:, a, k, :], DC)
                                ins.then_inc(s["t_ps"], 1)
                            for r in range(2):
                                pe.wait_ge(s["t_lo"], r + 1)
                                for c in range(DC):
                                    product(pe, PS[:, 2 * r + c, 0:D],
                                            lambda a, k: WvT_s[:, a, k, c * P:(c + 1) * P],
                                            lambda a, k: tT[:, a, r, k * D:(k + 1) * D], DC).then_inc(s["y_ps"], 1)

                        @block.scalar
                        def _(act):
                            def round_off(src, dst, ready, n, done):
                                act.wait_ge(ready, n)
                                act.activation(dst, src, ACT.Copy).then_inc(done, 1)

                            for n, (g, c) in enumerate(groups):
                                w = mcols(g)
                                round_off(PS[:, n % 4, 0:w], cT[:, 0, c, g * 512:g * 512 + w], s["cT_ps"], n + 1, s["cT_hi"])
                            for c in range(DC):
                                round_off(bank(4 + c), xnT[:, 0, c, :], s["xT_ps"], c + 1, s["xT_hi"])
                            for c in range(DC):
                                round_off(bank(6 + c), qT[:, 0, c, :], s["q_ps"], c + 1, s["q_hi"])

                            def exp(t):
                                act.wait_ge(s["s_max"], t + 1)
                                if t:
                                    act.wait_ge(s["pT_ps"], MG * t)
                                act.activation(pr[:, :], PS[:, 0:MG, :].rearrange("p g n -> p (g n)")[:, 0:M],
                                               ACT.Exp, bias=nb[:, t:t + 1], scale=XSCALE,
                                               accum_out=rs[:, t:t + 1]).then_inc(s["p_ready"], 1)

                            exp(0)
                            for t in range(NT):
                                if t:
                                    act.wait_ge(s["ac_ps"], t)
                                for g in range(MG):
                                    n = t * MG + g
                                    k = min(4, MT - 4 * g)
                                    m = mrows(4 * g + k - 1)
                                    round_off(PS[0:m, 4 + n % 2, 0:k * P],
                                              pT[0:m, 0, 4 * g:4 * g + k, :].rearrange("p t n -> p (t n)"),
                                              s["pT_ps"], n + 1, s["pT_hi"])
                                if t + 1 < NT:
                                    exp(t + 1)
                                act.wait_ge(s["ac_ps"], t + 1)
                                act.wait_ge(s["ac_inv"], t + 1)
                                act.activation(ac[:, 0, t, :], PS[:, 6 + t % 2, 0:D], ACT.Copy,
                                               scale=ri[:, t:t + 1]).then_inc(s["ac_hi"], 1)
                            for r in range(2):
                                round_off(bank(4 + r), tT[:, 0, r, :], s["t_ps"], r + 1, s["t_hi"])

                        @block.vector
                        def _(dve):
                            own = chain(dve, s["own"])
                            dve.memset(cT[:, :, :, M:M + 1].bitcast(F32), 0.0).then_inc(s["pzero"], 1)
                            dve.wait_ge(s["xq_in"], 16)
                            layer_norm(dve, own, xq, xn, s["stats"], s["inv"], 1)
                            dve.engine_nop().then_inc(s["xn_ready"], 1)

                            def remainder(src, hi, lo, ready, n, done):
                                dve.wait_ge(ready, n)
                                dve.tensor_tensor(lo, src, hi.bitcast(F32), ALU.subtract).then_inc(done, 1)

                            for n, (g, c) in enumerate(groups):
                                w = mcols(g)
                                a = g * 512
                                remainder(PS[:, n % 4, 0:w], cT[:, 0, c, a:a + w], cT[:, 1, c, a:a + w], s["cT_hi"], n + 1,
                                          s["cT_lo"])
                            for c in range(DC):
                                remainder(bank(4 + c), xnT[:, 0, c, :], xnT[:, 1, c, :], s["xT_hi"], c + 1, s["xT_lo"])
                            for c in range(DC):
                                remainder(bank(6 + c), qT[:, 0, c, :], qT[:, 1, c, :], s["q_hi"], c + 1, s["q_lo"])

                            def row_max(t):
                                dve.wait_ge(s["s_ps"], t + 1)
                                own(dve.tensor_reduce(mx[:, t:t + 1],
                                                      PS[:, 0:MG, :].rearrange("p g n -> p (g n)")[:, 0:M], AX, ALU.max))
                                dve.tensor_scalar(nb[:, t:t + 1], mx[:, t:t + 1], -XSCALE, None, ALU.mult)\
                                    .then_inc(s["s_max"], 1)

                            row_max(0)
                            for t in range(MT):
                                m = mrows(t)
                                dve.wait_ge(s["cm_hi"], t + 1)
                                dve.scalar_tensor_tensor(out=cm[0:m, 1, t, :], in0=cn[0:m, t, :],
                                                         scalar=mask01[0:m, t:t + 1],
                                                         in1=cm[0:m, 0, t, :].bitcast(F32), op0=ALU.mult,
                                                         op1=ALU.subtract).then_inc(s["cm_lo"], 1)
                            for t in range(NT):
                                for g in range(MG):
                                    n = t * MG + g
                                    k = min(4, MT - 4 * g)
                                    m = mrows(4 * g + k - 1)
                                    remainder(PS[0:m, 4 + n % 2, 0:k * P],
                                              pT[0:m, 0, 4 * g:4 * g + k, :].rearrange("p t n -> p (t n)"),
                                              pT[0:m, 1, 4 * g:4 * g + k, :].rearrange("p t n -> p (t n)"),
                                              s["pT_hi"], n + 1, s["pT_lo"])
                                dve.wait_ge(s["p_ready"], t + 1)
                                dve.reciprocal(ri[:, t:t + 1], rs[:, t:t + 1]).then_inc(s["ac_inv"], 1)
                                if t + 1 < NT:
                                    row_max(t + 1)
                                dve.wait_ge(s["ac_hi"], t + 1)
                                dve.scalar_tensor_tensor(out=ac[:, 1, t, :], in0=PS[:, 6 + t % 2, 0:D],
                                                         scalar=ri[:, t:t + 1], in1=ac[:, 0, t, :].bitcast(F32),
                                                         op0=ALU.mult, op1=ALU.subtract).then_inc(s["ac_lo"], 1)
                            for r in range(2):
                                remainder(bank(4 + r), tT[:, 0, r, :],
                                          tT[:, 1, r, :], s["t_hi"], r + 1, s["t_lo"])
                            dve.wait_ge(s["xr_ready"], NT)
                            for r in range(2):
                                for c in range(DC):
                                    dve.wait_ge(s["y_ps"], 2 * r + c + 1)
                                    dve.tensor_tensor(x1[:, 2 * c + r, :], PS[:, 2 * r + c, 0:D], xr[:, 2 * c + r, :],
                                                      ALU.add)
                    clear(every)

                with ExitStack() as st:
                    h0 = sb("h0", [P, NT, D], stack=st)
                    hn = sb("h_norm", [P, NT, D], stack=st)
                    h32 = sb("h_t32", [P, DC, S], stack=st)
                    hT = sb("h_ts", [P, 2, DC, S], F32R, stack=st)
                    qk = sb("qk_t", [P, 2, 2 * DC, S], F32R, stack=st)
                    va = sb("v_ones", [P, NT, H, 32], stack=st)
                    Qs = sb("q_stack", [P, H // 2, S], F32R, stack=st)
                    Ks = sb("k_stack", [P, H // 2, S], F32R, stack=st)
                    mx = sb("s_max_rows", [P, NT, H], stack=st)
                    m2 = sb("neg_max_rows", [4, HG, 2, S], F32R, stack=st)
                    PG = 4
                    pe_ring = 6
                    pb = sb("s_probs", [P, pe_ring, 4, S], stack=st)
                    oT = sb("s_out_t", [P, HG, S], stack=st)
                    rec = sb("s_inv", [P, NT, H], stack=st)
                    on = sb("s_out", [P, NT, D], stack=st)
                    x2 = sb("x2", [P, NT, D], stack=st)
                    oS = hT
                    lg = sb("logits", [P, NT, E], stack=st)
                    top = sb("top", [P, NT, 8], stack=st)
                    ti = sb("top_index", [P, NT, 8], U32, stack=st)
                    tf = sb("top_index_f", [P, NT, 8], stack=st)
                    dd = sb("top_diff", [P, NT], stack=st)
                    e2 = sb("top_exp", [P, NT], stack=st)
                    sm = sb("top_sum", [P, NT], stack=st)
                    w1c = sb("top_w1", [P, NT], stack=st)
                    w2c = sb("top_w2", [P, NT], stack=st)
                    wa = sb("w_first", [P, NT, E], stack=st)
                    wb = sb("w_second", [P, NT, E], stack=st)
                    wT = sb("w_t", [E, S], stack=st)
                    s, every = semaphores(st, "stats inv hn_ready own hT_ps h32_ready hT_hi hT_lo qk_ps qk_hi qk_lo v_ps v_ready "
                                              "pile_ps q_piled k_piled s_ps s_max m_ps m_hi m_lo m_rows st_ps p_ready pv_done o_ps "
                                              "oT_ready on_ps on_ready oS_ps oS_hi oS_lo x2_ps x2_ready h2_ready h2T_ps lg_ps "
                                              "d_ready e_ready w_ready wT_ps wT_ready bias_ps h0_ready h0b stored base_ready")
                    LAG = 24
                    UNITS = H * NT

                    def s_unit(i):
                        return i // NT, i % NT

                    def t_unit(j):
                        return j // (4 * NT), (j // 4) % NT, j % 4

                    with nc.Block() as block:
                        @block.sync
                        def _(sp):
                            for g in range(HG):
                                sp.wait_ge(s["m_lo"], g + 1)
                                for h in range(4):
                                    row = 64 * (h % 2) + 3 * DK
                                    sp.dma_start(Qs[row:row + 2, (4 * g + h) // 2, :].bitcast(F32),
                                                 m2[h:h + 1, g, :, :].bitcast(F32))\
                                        .then_inc(s["m_rows"], 16)
                            sp.wait_ge(s["h2_ready"], 1)
                            sp.dma_start(h_rows[bass.ds(b * S, S), :].rearrange("(t p) d -> p t d", p=P), hn[:, :, :])\
                                .then_inc(s["stored"], 16)
                            sp.wait_ge(s["base_ready"], NT)
                            sp.dma_start(base_rows[bass.ds(b * S, S), :].rearrange("(t p) d -> p t d", p=P), x2[:, :, :])\
                                .then_inc(s["stored"], 16)
                            sp.wait_ge(s["stored"], 32)

                        @block.gpsimd
                        def _(pool):
                            inverse_root(pool, s["stats"], s["inv"], 1)
                            pool.memset(va[:, :, :, DK:32], 1.0)
                            inverse_root(pool, s["stats"], s["inv"], 2)
                            pool.wait_ge(s["h0_ready"], 1)
                            for t in range(NT):
                                pool.tensor_tensor(h0[:, t, :], h0[:, t, :], bo_row[:, :], ALU.add).then_inc(s["h0b"], 1)
                            inverse_root(pool, s["stats"], s["inv"], 3)

                        @block.tensor
                        def _(pe):
                            def turn(src, b0, done):
                                for c in range(DC):
                                    for t in range(NT):
                                        ins = pe.transpose(PS[:, b0 + c, t * P:(t + 1) * P],
                                                           src[:, t, c * P:(c + 1) * P], ident[:, :])
                                    ins.then_inc(done, 1)

                            pe.wait_ge(s["hn_ready"], 1)
                            turn(hn, 0, s["hT_ps"])
                            pe.wait_ge(s["hT_lo"], DC)
                            for n in range(2 * DC):
                                product(pe, bank(2 + n), lambda a, k: Wqkv_s[:, a, k, n * P:(n + 1) * P],
                                        lambda a, k: hT[:, a, k, :], DC).then_inc(s["qk_ps"], 1)
                            for t in range(NT):
                                product(pe, PS[:, (6, 7, 0, 1)[t], 0:D], lambda a, k: hT[:, a, k, t * P:(t + 1) * P],
                                        lambda a, k: Wqkv_s[:, a, k, 2 * D:3 * D], DC).then_inc(s["v_ps"], 1)
                            pe.wait_ge(s["qk_lo"], 2 * DC)
                            for n in range(H):
                                at, q_or_k = n // 2, n % 2
                                if n >= 4:
                                    pe.wait_ge(s[("q_piled", "k_piled")[q_or_k]], at - 1)
                                for part in range(2):
                                    ins = pe.matmul(bank(2 + n % 4), pile[:, q_or_k, part, at % 4, :],
                                                    qk[:, part, q_or_k * DC + at // 4, :], start=part == 0, stop=part == 1)
                                ins.then_inc(s["pile_ps"], 1)
                            pe.wait_ge(s["v_ready"], NT)
                            pe.wait_ge(s["q_piled"], H // 2)
                            pe.wait_ge(s["k_piled"], H // 2)

                            def pv(u):
                                g, kt = u // NT, u % NT
                                pe.wait_ge(s["p_ready"], 4 * u + 4)
                                if kt == 0 and g:
                                    pe.wait_ge(s["oT_ready"], g)
                                for h in range(4):
                                    ins = pe.matmul(PS[32 * h:32 * h + 32, 6, :], va[:, kt, 4 * g + h, :],
                                                    pb[:, u % pe_ring, h, :], start=kt == 0, stop=kt == NT - 1)
                                ins.then_inc(s["pv_done"], 1)

                            for i in range(UNITS + LAG + 8):
                                if i < UNITS:
                                    h, qt = s_unit(i)
                                    r = 64 * (h % 2)
                                    if i >= 3:
                                        pe.wait_ge(s["s_max"], i - 2)
                                    pe.matmul(bank(i % 3), Qs[r:r + 3 * DK, h // 2, qt * P:(qt + 1) * P],
                                              Ks[r:r + 3 * DK, h // 2, :], start=True, stop=True).then_inc(s["s_ps"], 1)
                                if i % 16 == 2 and 1 <= i // 16 <= HG:
                                    g = i // 16 - 1
                                    pe.wait_ge(s["s_max"], 16 * (g + 1))
                                    if g:
                                        pe.wait_ge(s["m_lo"], g)
                                    for qt in range(NT):
                                        ins = pe.transpose(PS[0:4, 7, qt * P:(qt + 1) * P], mx[:, qt, 4 * g:4 * g + 4],
                                                           ident[:, :])
                                    ins.then_inc(s["m_ps"], 1)
                                j = i - LAG
                                if 0 <= j < UNITS:
                                    g, kt, hh = t_unit(j)
                                    h = 4 * g + hh
                                    r = 64 * (h % 2)
                                    if j % 16 == 0:
                                        pe.wait_ge(s["m_rows"], 64 * (g + 1))
                                    if j >= 3:
                                        pe.wait_ge(s["p_ready"], j - 2)
                                    pe.matmul(bank(3 + j % 3), Ks[r:r + 3 * DK + 2, h // 2, kt * P:(kt + 1) * P],
                                              Qs[r:r + 3 * DK + 2, h // 2, :], start=True, stop=True).then_inc(s["st_ps"], 1)
                                u = (j - 6) // 4
                                if j >= 6 and (j - 6) % 4 == 0 and u < UNITS // 4 and u % PG == PG - 1:
                                    for n in range(u - PG + 1, u + 1):
                                        pv(n)
                            pe.wait_ge(s["oT_ready"], HG)
                            for t in range(NT):
                                for g in range(HG):
                                    ins = pe.transpose(PS[:, t, g * P:(g + 1) * P], oT[:, g, t * P:(t + 1) * P], ident[:, :])
                                ins.then_inc(s["on_ps"], 1)
                            pe.wait_ge(s["on_ready"], NT)
                            turn(on, 4, s["oS_ps"])
                            pe.wait_ge(s["oS_lo"], DC)
                            for t in range(NT):
                                product(pe, PS[:, t, 0:D], lambda a, k: oS[:, a, k, t * P:(t + 1) * P],
                                        lambda a, k: Wo_s[:, a, k, :], DC).then_inc(s["x2_ps"], 1)
                            pe.wait_ge(s["h2_ready"], 1)
                            turn(hn, 4, s["h2T_ps"])
                            pe.wait_ge(s["hT_lo"], 2 * DC)
                            for t in range(NT):
                                ins = product(pe, PS[:, 6, t * E:(t + 1) * E], lambda a, k: hT[:, a, k, t * P:(t + 1) * P],
                                              lambda a, k: Wg_s[:, a, k, :], DC)
                            ins.then_inc(s["lg_ps"], 1)
                            pe.wait_ge(s["w_ready"], 1)
                            for t in range(NT):
                                ins = pe.transpose(PS[0:E, 7, t * P:(t + 1) * P], wa[:, t, :], ident[:, :])
                            ins.then_inc(s["wT_ps"], 1)
                            pe.wait_ge(s["wT_ready"], 1)
                            for t in range(NT):
                                pe.matmul(PS[:, t, 0:D], wT[:, t * P:(t + 1) * P], b2_sb[:, :], start=True, stop=True)\
                                    .then_inc(s["bias_ps"], 1)

                        @block.scalar
                        def _(act):
                            def affine(b0, g, c, ready, n):
                                act.wait_ge(ready, n)
                                act.activation(h32[:, c, :], bank(b0 + c), ACT.Identity, bias=cols[:, g + 1, c:c + 1],
                                               scale=cols[:, g, c:c + 1]).then_inc(s["h32_ready"], 1)
                                act.wait_ge(s["h32_ready"], (g // 2) * DC + c + 1)
                                act.activation(hT[:, 0, c, :], h32[:, c, :], ACT.Copy).then_inc(s["hT_hi"], 1)

                            for c in range(DC):
                                affine(0, 0, c, s["hT_ps"], c + 1)
                            for n in range(2 * DC):
                                act.wait_ge(s["qk_ps"], n + 1)
                                act.activation(qk[:, 0, n, :], bank(2 + n), ACT.Identity, bias=bqk_col[:, n:n + 1])\
                                    .then_inc(s["qk_hi"], 1)

                            for n in range(1, H, 2):
                                act.wait_ge(s["pile_ps"], n + 1)
                                act.activation(Ks[:, n // 2, :], bank(2 + n % 4), ACT.Identity, bias=ones_at[:, 0:1])\
                                    .then_inc(s["k_piled"], 1)

                            def keep_o(g):
                                act.wait_ge(s["pv_done"], NT * (g + 1))
                                act.activation(oT[:, g, :], bank(6), ACT.Copy).then_inc(s["oT_ready"], 1)

                            def round_max(g):
                                act.wait_ge(s["m_ps"], g + 1)
                                act.activation(m2[:, g, 0, :], PS[0:4, 7, :], ACT.Copy, scale=-1.0).then_inc(s["m_hi"], 1)

                            round_max(0)
                            for j in range(UNITS):
                                if j % 16 == 10 and j // 16 + 1 < HG:
                                    round_max(j // 16 + 1)
                                u = j // 4
                                if j % 4 == 0 and u >= pe_ring:
                                    act.wait_ge(s["pv_done"], u - pe_ring + 1)
                                act.wait_ge(s["st_ps"], j + 1)
                                act.activation(pb[:, u % pe_ring, j % 4, :], bank(3 + j % 3), ACT.Exp, scale=SSCALE)\
                                    .then_inc(s["p_ready"], 1)
                                if j % 16 == 4 and j > 16:
                                    keep_o(j // 16 - 1)
                            keep_o(HG - 1)
                            for c in range(DC):
                                act.wait_ge(s["oS_ps"], c + 1)
                                act.activation(oS[:, 0, c, :], bank(4 + c), ACT.Copy).then_inc(s["oS_hi"], 1)
                            for c in range(DC):
                                affine(4, 2, c, s["h2T_ps"], c + 1)
                            act.wait_ge(s["d_ready"], 1)
                            act.activation(e2[:, :], dd[:, :], ACT.Exp).then_inc(s["e_ready"], 1)
                            act.wait_ge(s["wT_ps"], 1)
                            act.activation(wT[:, :], PS[0:E, 7, :], ACT.Copy).then_inc(s["wT_ready"], 1)

                        @block.vector
                        def _(dve):
                            own = chain(dve, s["own"])
                            layer_norm(dve, own, x1, h0, s["stats"], s["inv"], 1)
                            layer_norm(dve, own, h0, hn, s["stats"], s["inv"], 2)
                            dve.engine_nop().then_inc(s["hn_ready"], 1)
                            dve.engine_nop().then_inc(s["h0_ready"], 1)

                            def h_lo(n, c):
                                dve.wait_ge(s["hT_hi"], n)
                                dve.tensor_tensor(hT[:, 1, c, :], h32[:, c, :], hT[:, 0, c, :].bitcast(F32), ALU.subtract)\
                                    .then_inc(s["hT_lo"], 1)

                            for c in range(DC):
                                h_lo(c + 1, c)
                            for n in range(2 * DC):
                                dve.wait_ge(s["qk_hi"], n + 1)
                                dve.scalar_tensor_tensor(out=qk[:, 1, n, :], in0=bank(2 + n), scalar=bqk_col[:, n:n + 1],
                                                         in1=qk[:, 0, n, :].bitcast(F32), op0=ALU.add,
                                                         op1=ALU.subtract).then_inc(s["qk_lo"], 1)
                            for t in range(NT):
                                dve.wait_ge(s["v_ps"], t + 1)
                                dve.tensor_tensor(va[:, t, :, 0:DK],
                                                  PS[:, (6, 7, 0, 1)[t], 0:D].rearrange("p (h d) -> p h d", h=H),
                                                  bv_row[:, :].rearrange("p (h d) -> p h d", h=H), ALU.add)\
                                    .then_inc(s["v_ready"], 1)

                            for n in range(0, H, 2):
                                dve.wait_ge(s["pile_ps"], n + 1)
                                dve.tensor_copy(Qs[:, n // 2, :], bank(2 + n % 4)).then_inc(s["q_piled"], 1)

                            def max_lo(g):
                                dve.wait_ge(s["m_hi"], g + 1)
                                dve.scalar_tensor_tensor(out=m2[:, g, 1, :], in0=PS[0:4, 7, :], scalar=-1.0,
                                                         in1=m2[:, g, 0, :].bitcast(F32), op0=ALU.mult,
                                                         op1=ALU.subtract).then_inc(s["m_lo"], 1)

                            for i in range(UNITS):
                                h, qt = s_unit(i)
                                dve.wait_ge(s["s_ps"], i + 1)
                                dve.tensor_reduce(mx[:, qt, h:h + 1], bank(i % 3), AX, ALU.max).then_inc(s["s_max"], 1)
                                if i % 16 == 4 and i > 16:
                                    max_lo(i // 16 - 1)
                            max_lo(HG - 1)
                            for t in range(NT):
                                o = PS[:, t, :].rearrange("p (h d) -> p h d", d=32)
                                dve.wait_ge(s["on_ps"], t + 1)
                                own(dve.reciprocal(rec[:, t, :], o[:, :, DK]))
                                dve.tensor_tensor(on[:, t, :].rearrange("p (h d) -> p h d", h=H), o[:, :, 0:DK],
                                                  rec[:, t, :].unsqueeze(2).to_broadcast([P, H, DK]), ALU.mult)\
                                    .then_inc(s["on_ready"], 1)
                            for c in range(DC):
                                dve.wait_ge(s["oS_hi"], c + 1)
                                dve.tensor_tensor(oS[:, 1, c, :], bank(4 + c), oS[:, 0, c, :].bitcast(F32), ALU.subtract)\
                                    .then_inc(s["oS_lo"], 1)
                            dve.wait_ge(s["h0b"], NT)
                            for t in range(NT):
                                dve.wait_ge(s["x2_ps"], t + 1)
                                own(dve.tensor_tensor(x2[:, t, :], PS[:, t, 0:D], h0[:, t, :], ALU.add))
                            layer_norm(dve, own, x2, hn, s["stats"], s["inv"], 3)
                            dve.engine_nop().then_inc(s["h2_ready"], 1)
                            for t in range(NT):
                                own(dve.tensor_tensor(x2[:, t, :], x2[:, t, :], x1[:, t, :], ALU.add))
                            for c in range(DC):
                                h_lo(DC + c + 1, c)
                            dve.wait_ge(s["lg_ps"], 1)
                            for t in range(NT):
                                own(dve.tensor_tensor(lg[:, t, :], PS[:, 6, t * E:(t + 1) * E], gb_row[:, :], ALU.add))
                                own(dve.max(top[:, t, :], lg[:, t, :]))
                                own(dve.max_index(ti[:, t, :], top[:, t, :], lg[:, t, :]))
                            own(dve.tensor_copy(tf[:, :, :], ti[:, :, :]))
                            dve.tensor_tensor(dd[:, :], top[:, :, 1], top[:, :, 0], ALU.subtract).then_inc(s["d_ready"], 1)
                            dve.wait_ge(s["e_ready"], 1)
                            own(dve.tensor_scalar(sm[:, :], e2[:, :], 1.0, None, ALU.add))
                            own(dve.reciprocal(w1c[:, :], sm[:, :]))
                            own(dve.tensor_tensor(w2c[:, :], e2[:, :], w1c[:, :], ALU.mult))
                            for t in range(NT):
                                own(dve.tensor_scalar(wa[:, t, :], iota_e[:, :], tf[:, t, 0:1], w1c[:, t:t + 1],
                                                      ALU.is_equal, ALU.mult))
                                own(dve.tensor_scalar(wb[:, t, :], iota_e[:, :], tf[:, t, 1:2], w2c[:, t:t + 1],
                                                      ALU.is_equal, ALU.mult))
                            own(dve.tensor_tensor(wa[:, :, :], wa[:, :, :], wb[:, :, :], ALU.add))
                            dve.engine_nop().then_inc(s["w_ready"], 1)
                            for k, w in enumerate((w1c, w2c)):
                                dve.tensor_copy(gate[:, k, bass.ds(b * NT, NT)], w[:, :])
                                for t in range(NT):
                                    own(dve.tensor_scalar(wb[:, t, :], iota_e[:, :], tf[:, t, k:k + 1], None, ALU.is_equal))
                                own(dve.tensor_copy(pick[:, k, bass.ds(b * NT, NT), :], wb[:, :, :]))
                            for t in range(NT):
                                dve.wait_ge(s["bias_ps"], t + 1)
                                dve.tensor_tensor(x2[:, t, :], PS[:, t, 0:D], x2[:, t, :], ALU.add)\
                                    .then_inc(s["base_ready"], 1)
                    clear(every)

        with ExitStack() as est:
            slot = sb("slot", [P, 2, NB], U32, stack=est)
            block_expert = sb("block_expert", [P, NBLK + 2], I32, stack=est)
            w1r = sb("w1_raw", [P, 2, DC, DFF], stack=est)
            w2r = sb("w2_raw", [P, 2, FT, D], stack=est)
            w1s = sb("w1_s", [P, 2, 2, DC, DFF], F32R, stack=est)
            w2s = sb("w2_s", [P, 2, 2, FT, D], F32R, stack=est)
            b1c = sb("b1_now", [P, 4, FT], stack=est)
            TT = BT // P
            PIECE = DC * DFF // 4

            def expert_of(sp, j):
                return sp.value_load(block_expert[0:1, bass.ds(j, 1)], min_val=0, max_val=E - 1)

            def load_weights(sp, e, k, w_in):
                sp.dma_start(w1r[:, k % 2], W1[bass.ds(e, 1)].rearrange("a (c p) f -> p (a c) f", p=P)).then_inc(w_in, 16)
                sp.dma_start(w2r[:, k % 2], W2[bass.ds(e, 1)].rearrange("a (c p) d -> p (a c) d", p=P)).then_inc(w_in, 16)
                sp.dma_start(b1c[:, k % 4, :], b1_col[:, bass.ds(e * FT, FT)]).then_inc(w_in, 16)

            def piece(ap, i, n=4):
                size = DC * DFF // n
                return ap.rearrange("p c f -> p (c f)")[:, i * size:(i + 1) * size]

            def w1_high(act, k, i, done):
                act.activation(piece(w1s[:, k % 2, 0], i), piece(w1r[:, k % 2], i), ACT.Copy).then_inc(done, 1)

            def w1_low(dve, k, i, ready, n, done):
                dve.wait_ge(ready, n)
                dve.tensor_tensor(piece(w1s[:, k % 2, 1], i), piece(w1r[:, k % 2], i),
                                  piece(w1s[:, k % 2, 0], i).bitcast(F32), ALU.subtract).then_inc(done, 1)

            def w2_high(dve, k, i, done):
                dve.tensor_copy(piece(w2s[:, k % 2, 0], i, 2), piece(w2r[:, k % 2], i, 2)).then_inc(done, 1)

            def w2_low(pool, k, ready, n, done):
                pool.wait_ge(ready, n)
                pool.tensor_tensor(w2s[:, k % 2, 1], w2r[:, k % 2], w2s[:, k % 2, 0].bitcast(F32), ALU.subtract)\
                    .then_inc(done, 1)

            with ExitStack() as st:
                hx = sb("h_all", [P, NB, D], stack=st)
                both = sb("picked", [P, NB, E], stack=st)
                tot = sb("tile_totals", [P, NB, E], stack=st)
                pos = sb("position", [P, NB, E], stack=st)
                run = sb("tiles_before", [P, NB + 1, E], stack=st)
                nblk = sb("blocks_of", [P, E], stack=st)
                end = sb("block_end", [P, E], stack=st)
                beg = sb("first_row", [P, E], stack=st)
                num = sb("block_number", [P, NBLK + 2], stack=st)
                eb = sb("expert_of", [P, NBLK + 2], stack=st)
                sl = sb("slot_terms", [P, 2, NB, E], stack=st)
                sf = sb("slot_f", [P, 2, NB], stack=st)
                s, every = semaphores(st, "h_in own picked_ready rank_ps num_ready slot_ready scattered "
                                          "expert_ready w_in0 w_in1 w1_hi w1_lo w2_hi w2_lo")
                with nc.Block() as block:
                    @block.sync
                    def _(sp):
                        sp.dma_start(hx[:, :, :], h_rows.rearrange("(t p) d -> p t d", p=P)).then_inc(s["h_in"], 16)
                        sp.wait_ge(s["expert_ready"], 1)
                        load_weights(sp, expert_of(sp, 0), 0, s["w_in0"])
                        load_weights(sp, expert_of(sp, 1), 1, s["w_in1"])
                        sp.wait_ge(s["w_in1"], 48)

                    @block.scalar
                    def _(act):
                        act.wait_ge(s["w_in0"], 48)
                        for i in range(4):
                            w1_high(act, 0, i, s["w1_hi"])

                    @block.gpsimd
                    def _(pool):
                        for j in range(NBLK + 2):
                            ins = pool.memset(num[:, j:j + 1], float(j))
                        ins.then_inc(s["num_ready"], 1)
                        pool.wait_ge(s["h_in"], 16)
                        pool.wait_ge(s["slot_ready"], 1)
                        for t in range(NB):
                            for k in range(2):
                                pool.indirect_dma_start(
                                    out=sorted_in[:, :], out_offset=bass.IndirectOffsetOnAxis(ap=slot[:, k, t:t + 1], axis=0),
                                    in_=hx[:, t, :], in_offset=None).then_inc(s["scattered"], 16)
                        w2_low(pool, 0, s["w2_hi"], 2, s["w2_lo"])
                        pool.wait_ge(s["scattered"], 32 * NB)

                    @block.tensor
                    def _(pe):
                        pe.wait_ge(s["picked_ready"], 1)
                        flat = both[:, :, :].rearrange("p t e -> p (t e)")
                        pe.matmul(PS[:, 0, 0:NB * E], tri[:, :], flat, start=True, stop=True)
                        pe.matmul(PS[:, 1, 0:NB * E], ones[:, :], flat, start=True, stop=True).then_inc(s["rank_ps"], 1)

                    @block.vector
                    def _(dve):
                        own = chain(dve, s["own"])
                        dve.tensor_tensor(both[:, :, :], pick[:, 0], pick[:, 1], ALU.add).then_inc(s["picked_ready"], 1)
                        own(dve.memset(run[:, 0, :], 0.0))
                        dve.wait_ge(s["rank_ps"], 1)
                        own(dve.tensor_copy(tot[:, :, :].rearrange("p t e -> p (t e)"), PS[:, 1, 0:NB * E]))
                        for t in range(NB):
                            own(dve.tensor_tensor(run[:, t + 1, :], run[:, t, :], tot[:, t, :], ALU.add))
                        own(dve.tensor_scalar(nblk[:, :], run[:, NB, :], 0.0, None, ALU.is_gt))
                        for j in range(1, NB * P // BT):
                            own(dve.scalar_tensor_tensor(out=nblk[:, :], in0=run[:, NB, :], scalar=float(j * BT),
                                                         in1=nblk[:, :], op0=ALU.is_gt, op1=ALU.add))
                        own(dve.tensor_copy(end[:, 0:1], nblk[:, 0:1]))
                        for e in range(1, E):
                            own(dve.tensor_tensor(end[:, e:e + 1], end[:, e - 1:e], nblk[:, e:e + 1], ALU.add))
                        own(dve.tensor_tensor(beg[:, :], end[:, :], nblk[:, :], ALU.subtract))
                        own(dve.tensor_scalar(beg[:, :], beg[:, :], float(BT), None, ALU.mult))
                        own(dve.tensor_tensor(pos[:, :, :].rearrange("p t e -> p (t e)"), PS[:, 0, 0:NB * E],
                                              run[:, 0:NB, :].rearrange("p t e -> p (t e)"), ALU.add))
                        own(dve.tensor_tensor(pos[:, :, :], pos[:, :, :], beg[:, :].unsqueeze(1).to_broadcast([P, NB, E]),
                                              ALU.add))
                        for k in range(2):
                            own(dve.tensor_tensor(sl[:, k], pos[:, :, :], pick[:, k], ALU.mult))
                            own(dve.tensor_reduce(sf[:, k, :], sl[:, k], AX, ALU.add))
                        dve.tensor_copy(slot[:, :, :], sf[:, :, :]).then_inc(s["slot_ready"], 1)
                        dve.wait_ge(s["num_ready"], 1)
                        own(dve.tensor_scalar(eb[:, :], num[:, :], end[:, 0:1], None, ALU.is_ge))
                        for e in range(1, E - 1):
                            own(dve.scalar_tensor_tensor(out=eb[:, :], in0=num[:, :], scalar=end[:, e:e + 1],
                                                         in1=eb[:, :], op0=ALU.is_ge, op1=ALU.add))
                        dve.tensor_copy(block_expert[:, :], eb[:, :]).then_inc(s["expert_ready"], 1)
                        dve.wait_ge(s["w_in0"], 48)
                        for i in range(2):
                            w2_high(dve, 0, i, s["w2_hi"])
                        for i in range(4):
                            w1_low(dve, 0, i, s["w1_hi"], i + 1, s["w1_lo"])
                clear(every)

            with ExitStack() as st:
                xs = sb("sorted_x", [P, 2, BT // P, D], stack=st)
                x32 = sb("sorted_x_t32", [P, DC, BT], stack=st)
                xT = sb("sorted_x_t", [P, 2, 2, DC, BT], F32R, stack=st)
                RING = 3
                hid = sb("hid", [P, RING, BT], stack=st)
                hs = sb("hid_s", [P, RING, 2, BT], F32R, stack=st)
                ys = sb("sorted_y", [P, 2, BT // P, D], stack=st)
                s, every = semaphores(st, "w_in_0 w_in_1 x_in_0 x_in_1 w1_hi w1_lo w2_hi w2_lo xT_ps x32_ready xT_hi xT_lo hid_ps hid_ready "
                                          "hid_hi hid_lo used y_ready y_stored_0 y_stored_1")
                def load_x(sp, j, buf):
                    sp.dma_start(xs[:, buf], sorted_in[bass.ds(j * BT, BT), :].rearrange("(t p) d -> p t d", p=P))\
                        .then_inc(s[f"x_in_{buf}"], 16)

                with nc.Block() as block:
                    @block.sync
                    def _(sp):
                        load_x(sp, 0, 0)
                        sp.wait_ge(s["x_in_0"], 16)
                clear(every)

                with nc.Fori(0, NBLK // BODY) as it:
                    with nc.Block() as block:
                        @block.sync
                        def _(sp):
                            def store(k):
                                sp.wait_ge(s["y_ready"], TT * (k + 1))
                                sp.dma_start(sorted_out[bass.ds((it * BODY + k) * BT, BT), :]
                                             .rearrange("(t p) d -> p t d", p=P), ys[:, k % 2]).then_inc(s[f"y_stored_{k % 2}"], 16)

                            for k in range(BODY):
                                if k:
                                    sp.wait_ge(s["xT_ps"], k)
                                load_x(sp, it * BODY + k + 1, (k + 1) % 2)
                                if k:
                                    sp.wait_ge(s["w1_lo"], 4 * k)
                                    sp.wait_ge(s["w2_lo"], k)
                                load_weights(sp, expert_of(sp, it * BODY + k + 2), k + 2, s[f"w_in_{k % 2}"])
                                if k:
                                    store(k - 1)
                            store(BODY - 1)
                            for h in range(2):
                                sp.wait_ge(s[f"w_in_{h}"], 24 * BODY)
                            for h in range(2):
                                sp.wait_ge(s[f"x_in_{h}"], 8 * BODY)
                                sp.wait_ge(s[f"y_stored_{h}"], 8 * BODY)

                        @block.gpsimd
                        def _(pool):
                            for k in range(BODY):
                                w2_low(pool, k + 1, s["w2_hi"], 2 * (k + 1), s["w2_lo"])

                        @block.tensor
                        def _(pe):
                            def turn(k):
                                if k:
                                    pe.wait_ge(s[f"x_in_{k % 2}"], 16 * ((k + 1) // 2))
                                    pe.wait_ge(s["x32_ready"], DC * k)
                                for c in range(DC):
                                    for t in range(TT):
                                        ins = pe.transpose(PS[:, 7, c * BT + t * P:c * BT + (t + 1) * P],
                                                           xs[:, k % 2, t, c * P:(c + 1) * P], ident[:, :])
                                ins.then_inc(s["xT_ps"], 1)

                            def hidden(u):
                                k, f = u // FT, u % FT
                                if f == 0:
                                    pe.wait_ge(s["xT_lo"], DC * (k + 1))
                                    if k:
                                        pe.wait_ge(s["w1_lo"], 4 * k)
                                        pe.wait_ge(s["w2_lo"], k)
                                if u >= RING:
                                    pe.wait_ge(s["hid_ready"], u - RING + 1)
                                product(pe, PS[:, u % RING, 0:BT], lambda a, c: w1s[:, k % 2, a, c, f * P:(f + 1) * P],
                                        lambda a, c: xT[:, k % 2, a, c, :], DC).then_inc(s["hid_ps"], 1)

                            def outputs(u):
                                k, f = u // FT, u % FT
                                pe.wait_ge(s["hid_lo"], u + 1)
                                if f == 0 and k >= 2:
                                    pe.wait_ge(s["y_ready"], TT * (k - 1))
                                for t in range(TT):
                                    for n, (a, c) in enumerate(PASSES):
                                        ins = pe.matmul(PS[:, 3 + 2 * (k % 2) + t, 0:D], hs[:, u % RING, a, t * P:(t + 1) * P],
                                                        w2s[:, k % 2, c, f, :], start=f == 0 and n == 0,
                                                        stop=f == FT - 1 and n == 2)
                                ins.then_inc(s["used"], 1)

                            turn(0)
                            for u in range(BODY * FT + 2):
                                if u < BODY * FT:
                                    hidden(u)
                                    if u % FT == 1 and u // FT + 1 < BODY:
                                        turn(u // FT + 1)
                                if u >= 2:
                                    outputs(u - 2)

                        @block.scalar
                        def _(act):
                            def x_high(k, c):
                                act.wait_ge(s["xT_ps"], k + 1)
                                if k:
                                    act.wait_ge(s["xT_lo"], DC * (k - 1) + c + 1)
                                act.activation(x32[:, c, :], PS[:, 7, c * BT:(c + 1) * BT], ACT.Identity,
                                               bias=cols[:, 3, c:c + 1], scale=cols[:, 2, c:c + 1])\
                                    .then_inc(s["x32_ready"], 1)
                                act.wait_ge(s["x32_ready"], DC * k + c + 1)
                                if k >= 2:
                                    act.wait_ge(s["used"], (k - 1) * FT)
                                act.activation(xT[:, k % 2, 0, c, :], x32[:, c, :], ACT.Copy).then_inc(s["xT_hi"], 1)

                            for c in range(DC):
                                x_high(0, c)
                            for u in range(BODY * FT):
                                k, f = u // FT, u % FT
                                act.wait_ge(s["hid_ps"], u + 1)
                                if u >= RING:
                                    act.wait_ge(s["hid_lo"], u - RING + 1)
                                act.activation(hid[:, u % RING, :], PS[:, u % RING, 0:BT], ACT.Relu,
                                               bias=b1c[:, k % 4, f:f + 1]).then_inc(s["hid_ready"], 1)
                                if u >= RING:
                                    act.wait_ge(s["used"], u - RING + 1)
                                act.wait_ge(s["hid_ready"], u + 1)
                                act.activation(hs[:, u % RING, 0, :], hid[:, u % RING, :], ACT.Copy).then_inc(s["hid_hi"], 1)
                                if 2 <= f < 6:
                                    if f == 2 and k:
                                        act.wait_ge(s[f"w_in_{(k - 1) % 2}"], 48 * ((k + 1) // 2))
                                        act.wait_ge(s["used"], k * FT)
                                    w1_high(act, k + 1, f - 2, s["w1_hi"])
                                if 4 <= f < 6 and k + 1 < BODY:
                                    x_high(k + 1, f - 4)

                        @block.vector
                        def _(dve):
                            def x_low(k, c):
                                dve.wait_ge(s["xT_hi"], DC * k + c + 1)
                                dve.tensor_tensor(xT[:, k % 2, 1, c, :], x32[:, c, :], xT[:, k % 2, 0, c, :].bitcast(F32),
                                                  ALU.subtract).then_inc(s["xT_lo"], 1)

                            def keep_y(k):
                                dve.wait_ge(s["used"], (k + 1) * FT)
                                if k >= 2:
                                    dve.wait_ge(s[f"y_stored_{k % 2}"], 16 * (k // 2))
                                for t in range(TT):
                                    dve.tensor_copy(ys[:, k % 2, t, :], PS[:, 3 + 2 * (k % 2) + t, 0:D])\
                                        .then_inc(s["y_ready"], 1)

                            for c in range(DC):
                                x_low(0, c)
                            for u in range(BODY * FT):
                                k, f = u // FT, u % FT
                                dve.wait_ge(s["hid_hi"], u + 1)
                                dve.tensor_tensor(hs[:, u % RING, 1, :], hid[:, u % RING, :],
                                                  hs[:, u % RING, 0, :].bitcast(F32), ALU.subtract).then_inc(s["hid_lo"], 1)
                                if f == 2 and k:
                                    keep_y(k - 1)
                                if 2 <= f < 4:
                                    if f == 2 and k:
                                        dve.wait_ge(s[f"w_in_{(k - 1) % 2}"], 48 * ((k + 1) // 2))
                                        dve.wait_ge(s["used"], k * FT)
                                    w2_high(dve, k + 1, f - 2, s["w2_hi"])
                                if 2 <= f < 6:
                                    w1_low(dve, k + 1, f - 2, s["w1_hi"], 4 * k + f - 1, s["w1_lo"])
                                if 5 <= f < 7 and k + 1 < BODY:
                                    x_low(k + 1, f - 5)
                            keep_y(BODY - 1)
                    clear(every)

            with ExitStack() as st:
                base = sb("base", [P, NB, D], stack=st)
                yg = sb("expert_rows", [P, NB, 2, D], stack=st)
                s, every = semaphores(st, "base_in own stored out_ready")
                got = [st.enter_context(nc.semaphore(f"rows_in_{t}")) for t in range(NB)]
                ov = out.rearrange("b (c p r) d -> p (b c) r d", p=P, r=2)
                with nc.Block() as block:
                    @block.sync
                    def _(sp):
                        sp.dma_start(base[:, :, :], base_rows.rearrange("(t p) d -> p t d", p=P)).then_inc(s["base_in"], 16)
                        for t in range(0, NB, 2):
                            sp.wait_ge(s["out_ready"], t + 2)
                            sp.dma_start(ov[:, t // 2], base[:, t:t + 2, :]).then_inc(s["stored"], 16)
                        sp.wait_ge(s["stored"], 16 * NB // 2)

                    @block.gpsimd
                    def _(pool):
                        for t in range(NB):
                            for k in range(2):
                                pool.indirect_dma_start(
                                    out=yg[:, t, k, :], out_offset=None, in_=sorted_out[:, :],
                                    in_offset=bass.IndirectOffsetOnAxis(ap=slot[:, k, t:t + 1], axis=0))\
                                    .then_inc(got[t], 16)

                    @block.vector
                    def _(dve):
                        own = chain(dve, s["own"])
                        dve.wait_ge(s["base_in"], 16)
                        for t in range(NB):
                            dve.wait_ge(got[t], 32)
                            own(dve.scalar_tensor_tensor(out=base[:, t, :], in0=yg[:, t, 0, :], scalar=gate[:, 0, t:t + 1],
                                                         in1=base[:, t, :], op0=ALU.mult, op1=ALU.add))
                            dve.scalar_tensor_tensor(out=base[:, t, :], in0=yg[:, t, 1, :], scalar=gate[:, 1, t:t + 1],
                                                     in1=base[:, t, :], op0=ALU.mult, op1=ALU.add).then_inc(s["out_ready"], 1)


_INS = ['x', 'ctx_1024', 'mask_S2_ik0', 'L0_xattn_qkv_w', 'L0_xattn_proj_w', 'L0_xattn_proj_b', 'L0_ffn_ln1_g',
        'L0_ffn_ln1_b', 'L0_ffn_w_qkv', 'L0_ffn_b_qkv', 'L0_ffn_w_o', 'L0_ffn_b_o', 'L0_ffn_ln2_g', 'L0_ffn_ln2_b',
        'L0_ffn_gate_w', 'L0_ffn_gate_b', 'L0_ffn_W1', 'L0_ffn_b1', 'L0_ffn_W2', 'L0_ffn_b2']


def kernel(**inputs):
    import numpy as _np
    import concourse.bacc as _bacc
    from concourse import mybir as _mybir
    from concourse.bass_utils import run_bass_kernel_spmd as _run

    nc = _bacc.Bacc("TRN2", target_bir_lowering=False, num_devices=1)
    arrays, args = {}, []
    for name in _INS:
        a = _np.ascontiguousarray(inputs[name])
        arrays[f"in_{name}_dram"] = a
        args.append(nc.dram_tensor(f"in_{name}_dram", a.shape, _mybir.dt.from_np(a.dtype), kind="ExternalInput").ap())
    args.append(nc.dram_tensor("out_0_dram", (4, 512, 256), _mybir.dt.float32, kind="ExternalOutput").ap())
    xattn_moe_kernel(nc, *args)
    r = _run(nc, [arrays], core_ids=[0])
    return r.results[0]["out_0_dram"]
```

```python
from contextlib import ExitStack

import numpy as np

import concourse.bass as bass
from concourse import mybir

P = 128
F32 = mybir.dt.float32
F32R = mybir.dt.float32r
I32 = mybir.dt.int32
U32 = mybir.dt.uint32
ALU = mybir.AluOpType
ACT = mybir.ActivationFunctionType
AX = mybir.AxisListType.X

PASSES = ((1, 0), (0, 1), (0, 0))


def xattn_moe_kernel(nc, x, ctx_in, mask, qkv_w, proj_w, proj_b, ln1_g, ln1_b, w_qkv, b_qkv, w_o, b_o,
                     ln2_g, ln2_b, gate_w, gate_b, W1, b1, W2, b2, out):
    B, S, D = x.shape
    M = ctx_in.shape[1]
    E, _, DFF = W1.shape
    DC = D // P
    NT = S // P
    MT = -(-M // P)
    ML = M - (MT - 1) * P
    MG = -(-M // 512)
    H = 16
    DK = D // H
    HG = H // 4
    FT = DFF // P
    NB = B * NT
    XSCALE = float(D // 8) ** -0.5
    SSCALE = float(DK) ** -0.5
    EPS = 1e-5

    def mrows(t):
        return P if t < MT - 1 else ML

    def mcols(g):
        return min(512, M - 512 * g)

    def bcast_rows(v, n):
        return v.rearrange("(a n) -> a n", a=1).to_broadcast([P, n])

    with ExitStack() as keep:
        uses = {}

        def unique(name):
            uses[name] = uses.get(name, 0) + 1
            return name if uses[name] == 1 else f"{name}_{uses[name]}"

        def sb(name, shape, dt=F32, stack=keep):
            return stack.enter_context(nc.sbuf_tensor(unique(name), shape, dt))

        PS = keep.enter_context(nc.psum_tensor("banks", [P, 8, 512], F32))

        def bank(i):
            return PS[:, i, :]

        ident = sb("ident", [P, P])
        halves = sb("minus_half", [P, NB])
        M_s = sb("wq_wk", [P, 2, DC, D], F32R)
        WvT_s = sb("wv_t", [P, 2, DC, D], F32R)
        PT_s = sb("proj_t", [P, 2, DC, D], F32R)
        Wqkv_s = sb("w_qkv_s", [P, 2, DC, 3 * D], F32R)
        Wo_s = sb("w_o_s", [P, 2, DC, D], F32R)
        Wg_s = sb("gate_s", [P, 2, DC, E], F32R)
        b2_sb = sb("b2_sb", [E, D])
        pb_row = sb("proj_b_row", [P, D])
        bo_row = sb("b_o_row", [P, D])
        bv_row = sb("b_v_row", [P, D])
        gb_row = sb("gate_b_row", [P, E])
        iota_e = sb("iota_e", [P, E])
        cols = sb("cols", [P, 4, DC])
        bqk_col = sb("bqk_col", [P, 2 * DC])
        mask01 = sb("mask01", [P, MT])
        pile = sb("pile", [P, 2, 2, 4, P], F32R)
        ones_at = sb("ones_at", [P, 1])
        b1_col = sb("b1_col", [P, E * FT])
        tri = sb("before", [P, P])
        ones = sb("ones", [P, P])
        pick = sb("pick", [P, 2, NB, E])
        gate = sb("gate", [P, 2, NB])
        x1_rows = nc.dram_tensor("x1_rows", (NB * P, D), F32).ap()
        x2_rows = nc.dram_tensor("x2_rows", (NB * P, D), F32).ap()
        BT = 2 * P
        BODY = 12
        NBLK = -(-(2 * NB * P // BT + E - 1) // BODY) * BODY
        sorted_in = nc.dram_tensor("sorted_in", ((NBLK + 2) * BT, D), F32).ap()
        sorted_out = nc.dram_tensor("sorted_out", (NBLK * BT, D), F32).ap()
        zeroed = keep.enter_context(nc.semaphore("zeroed"))
        ZR = (NBLK + 2) * BT // P
        zeros = sb("zeros", [P, 1, D])

        def clear(sems):
            for s in sems:
                nc.sync.sem_clear(s)
            nc.all_engine_barrier()

        def semaphores(stack, names):
            made = {n: stack.enter_context(nc.semaphore(unique(n))) for n in names.split()}
            return made, list(made.values())

        def chain(eng, sem):
            count = [0]

            def step(ins):
                count[0] += 1
                ins.then_inc(sem, 1)
                eng.wait_ge(sem, count[0])
            return step

        def product(pe, out_ap, lhsT, rhs, k_chunks, first=True, last=True):
            n = 0
            for k in range(k_chunks):
                for a, b in PASSES:
                    ins = pe.matmul(out_ap, lhsT(a, k), rhs(b, k), start=first and n == 0,
                                    stop=last and n == 3 * k_chunks - 1)
                    n += 1
            return ins

        inputs = ExitStack()
        xq = sb("x_tokens", [P, NT, D], stack=inputs)
        cn = sb("ctx", [P, MT, D], stack=inputs)

        def load_batch(sp, b, done):
            xb = x[bass.ds(b, 1)].rearrange("a n d -> (a n) d")
            cb = ctx_in[bass.ds(b, 1)].rearrange("a n d -> (a n) d")
            sp.dma_start(xq[:, :, :], xb.rearrange("(t p) d -> p t d", p=P)).then_inc(done, 16)
            sp.dma_start(cn[:, 0:MT - 1, :], cb[0:(MT - 1) * P, :].rearrange("(t p) d -> p t d", p=P)).then_inc(done, 16)
            sp.dma_start(cn[0:ML, MT - 1, :], cb[(MT - 1) * P:M, :]).then_inc(done, 16)

        with ExitStack() as st:
            wq_raw = sb("wq_raw", [P, 3 * DC, D], stack=st)
            pj_raw = sb("pj_raw", [P, DC, D], stack=st)
            wqkv_raw = sb("wqkv_raw", [P, DC, 3 * D], stack=st)
            wo_raw = sb("wo_raw", [P, DC, D], stack=st)
            wg_raw = sb("wg_raw", [P, DC, E], stack=st)
            mask_i = sb("mask_i", [P, MT], I32, stack=st)
            mask_f = sb("mask_f", [P, MT], stack=st)
            b1_rows = sb("b1_rows", [E * FT, P], stack=st)
            two = sb("ones_at_terms", [P, 2], stack=st)
            s, every = semaphores(st, "w_loaded batch_in pile_zero ident_zero ident_ready w_psum w_hi raw_hi v_loaded own tri_one")
            with nc.Block() as block:
                @block.sync
                def _(sp):
                    loads = [
                        (wq_raw[:, :, :], qkv_w.rearrange("(c p) d -> p c d", p=P)),
                        (pj_raw[:, :, :], proj_w.rearrange("(c p) d -> p c d", p=P)),
                        (b1_rows[:, :], b1.rearrange("e (f p) -> (e f) p", p=P)),
                        (wqkv_raw[:, :, :], w_qkv.rearrange("(c p) n -> p c n", p=P)),
                        (wo_raw[:, :, :], w_o.rearrange("(c p) n -> p c n", p=P)),
                        (wg_raw[:, :, :], gate_w.rearrange("(c p) e -> p c e", p=P)),
                    ]
                    for dst, src in loads:
                        sp.dma_start(dst, src).then_inc(s["w_loaded"], 16)
                    load_batch(sp, 0, s["batch_in"])
                    sp.wait_ge(s["batch_in"], 48)
                    sp.wait_ge(s["w_loaded"], 16 * len(loads))

                @block.scalar
                def _(act):
                    vectors = [
                        (b2_sb[:, :], b2),
                        (pb_row[:, :], bcast_rows(proj_b, D)),
                        (bo_row[:, :], bcast_rows(b_o, D)),
                        (bv_row[:, :], bcast_rows(b_qkv[2 * D:3 * D], D)),
                        (gb_row[:, :], bcast_rows(gate_b, E)),
                        (bqk_col[:, :], b_qkv[0:2 * D].rearrange("(c p) -> p c", p=P)),
                        (mask_i[:, 0:MT - 1], mask[0:(MT - 1) * P].rearrange("(t p) -> p t", p=P)),
                        (mask_i[0:ML, MT - 1:MT], mask[(MT - 1) * P:M].rearrange("(t p) -> p t", t=1)),
                    ] + [(cols[:, n, :], v.rearrange("(c p) -> p c", p=P))
                         for n, v in enumerate((ln1_g, ln1_b, ln2_g, ln2_b))]
                    for dst, src in vectors:
                        act.dma_start(dst, src, allow_slow_non_contiguous=True).then_inc(s["v_loaded"], 16)
                    for n, dst in enumerate([M_s] * DC + [WvT_s] * DC + [PT_s] * DC):
                        act.wait_ge(s["w_psum"], n + 1)
                        act.activation(dst[:, 0, n % DC, :], PS[:, n, 0:D], ACT.Copy).then_inc(s["w_hi"], 1)
                    act.wait_ge(s["w_psum"], 3 * DC + 1)
                    act.activation(b1_col[:, :], PS[:, 6, 0:E * FT], ACT.Copy)
                    act.wait_ge(s["v_loaded"], 16 * len(vectors))

                @block.gpsimd
                def _(pool):
                    pool.memset(ident[:, :], 0.0).then_inc(s["ident_zero"], 1)
                    pool.memset(pile[:, :, :, :, :].bitcast(F32), 0.0).then_inc(s["pile_zero"], 1)
                    pool.memset(ones[:, :], 1.0).then_inc(s["tri_one"], 1)
                    pool.memset(halves[:, :], -0.5)
                    for e in range(E):
                        pool.memset(iota_e[:, e:e + 1], float(e))
                    pool.wait_ge(s["ident_zero"], 1)
                    pool.affine_select(out=ident[:, :], in_=ident[:, :], compare_op=ALU.not_equal, fill=1.0,
                                       base=0, pattern=[[-1, P]], channel_multiplier=1).then_inc(s["ident_ready"], 1)
                    pool.wait_ge(s["tri_one"], 1)
                    pool.affine_select(out=tri[:, :], in_=ones[:, :], compare_op=ALU.is_gt, fill=0.0,
                                       base=0, pattern=[[1, P]], channel_multiplier=-1)
                    pool.wait_ge(s["w_loaded"], 96)
                    for dst, src in ((Wqkv_s, wqkv_raw), (Wo_s, wo_raw), (Wg_s, wg_raw)):
                        pool.tensor_copy(dst[:, 0], src[:, :, :]).then_inc(s["raw_hi"], 1)

                @block.tensor
                def _(pe):
                    pe.wait_ge(s["ident_ready"], 1)
                    pe.wait_ge(s["w_loaded"], 96)
                    for c in range(DC):
                        for k in range(DC):
                            ins = pe.matmul(PS[:, c, 0:D], wq_raw[:, k, c * P:(c + 1) * P], wq_raw[:, DC + k, :],
                                            start=k == 0, stop=k == DC - 1)
                        ins.then_inc(s["w_psum"], 1)
                    for raw, base, b0 in ((wq_raw, 2 * DC, DC), (pj_raw, 0, 2 * DC)):
                        for c in range(DC):
                            for k in range(DC):
                                ins = pe.transpose(PS[:, b0 + c, k * P:(k + 1) * P],
                                                   raw[:, base + k, c * P:(c + 1) * P], ident[:, :])
                            ins.then_inc(s["w_psum"], 1)
                    pe.transpose(PS[:, 6, 0:E * FT], b1_rows[:, :], ident[0:E * FT, 0:E * FT]).then_inc(s["w_psum"], 1)

                @block.vector
                def _(dve):
                    own = chain(dve, s["own"])
                    dve.memset(zeros[:, :, :], 0.0)
                    for n, dst in enumerate([M_s] * DC + [WvT_s] * DC + [PT_s] * DC):
                        dve.wait_ge(s["w_hi"], n + 1)
                        dve.tensor_tensor(dst[:, 1, n % DC, :], PS[:, n, 0:D], dst[:, 0, n % DC, :].bitcast(F32),
                                          ALU.subtract)
                    for n, (dst, src) in enumerate(((Wqkv_s, wqkv_raw), (Wo_s, wo_raw), (Wg_s, wg_raw))):
                        dve.wait_ge(s["raw_hi"], n + 1)
                        dve.tensor_tensor(dst[:, 1], src[:, :, :], dst[:, 0].bitcast(F32), ALU.subtract)
                    dve.wait_ge(s["ident_ready"], 1)
                    dve.wait_ge(s["pile_zero"], 1)
                    heads = ident[:, :].rearrange("p (a b i) -> p a b i", b=2, i=DK)
                    for q_or_k, copies in enumerate(((0, 1, 0), (0, 0, 1))):
                        for n, part in enumerate(copies):
                            dst = pile[:, q_or_k, part].rearrange("p a (b n i) -> p a b n i", b=2, i=DK)
                            dve.tensor_copy(dst[:, :, :, n, :], heads)
                    own(dve.tensor_reduce(two[:, :], ident[:, :].rearrange("p (b n) -> p b n", b=2)
                                          [:, :, 3 * DK:3 * DK + 2], AX, ALU.add))
                    dve.tensor_tensor(ones_at[:, :], two[:, 0:1], two[:, 1:2], ALU.add)
                    dve.wait_ge(s["v_loaded"], 16 * 12)
                    for p, c0, c1 in ((P, 0, MT - 1), (ML, MT - 1, MT)):
                        own(dve.tensor_copy(mask_f[0:p, c0:c1], mask_i[0:p, c0:c1]))
                        dve.tensor_scalar(mask01[0:p, c0:c1], mask_f[0:p, c0:c1], 0.0, None, ALU.not_equal)
            clear(every)

        with ExitStack() as bs:
            x1 = sb("x1", [P, NT, D], stack=bs)
            st_a = sb("st_a", [P, NT, 6], stack=bs)
            mv = sb("mean_var", [P, NT, 2], stack=bs)
            veps = sb("var_eps", [P, 2, NT], stack=bs)
            rstd = sb("rstd", [P, 2, NT], stack=bs)

            def layer_norm(dve, own, src, dst, ready, stats_ready, rstd_ready, twice=None, twice_ready=None):
                for t in range(NT):
                    ins = dve.bn_stats(st_a[:, t, :], src[:, t, :])
                own(ins)
                for t in range(NT):
                    ins = dve.bn_aggr(mv[:, t, :], st_a[:, t, :])
                own(ins)
                if twice is not None:
                    dve.tensor_scalar(veps[:, 1, :], mv[:, :, 1], 1.0 + EPS, EPS * EPS, ALU.mult, ALU.add)
                dve.tensor_scalar(veps[:, 0, :], mv[:, :, 1], EPS, None, ALU.add).then_inc(stats_ready, 1)
                dve.wait_ge(rstd_ready, 1)
                if twice is not None:
                    for t in range(NT):
                        ins = dve.tensor_scalar(twice[:, t, :], src[:, t, :], mv[:, t, 0:1], rstd[:, 1, t:t + 1],
                                                ALU.subtract, ALU.mult)
                    ins.then_inc(twice_ready, 1)
                for t in range(NT):
                    ins = dve.tensor_scalar(dst[:, t, :], src[:, t, :], mv[:, t, 0:1], rstd[:, 0, t:t + 1],
                                            ALU.subtract, ALU.mult)
                ins.then_inc(ready, 1)

            def inverse_root(pool, stats_ready, rstd_ready, n):
                pool.wait_ge(stats_ready, 1)
                pool.tensor_tensor(rstd[:, 0:n].rearrange("p a t -> p (a t)"), veps[:, 0:n].rearrange("p a t -> p (a t)"),
                                   halves[:, 0:n * NT], ALU.pow).then_inc(rstd_ready, 1)

            def attention(b, more):
                with ExitStack() as st:
                    xr = sb("x_residual", [P, NT, D], stack=st)
                    xn = sb("x_norm", [P, NT, D], stack=st)
                    xnT = sb("x_norm_t", [P, 2, DC, S], F32R, stack=st)
                    qT = sb("q_t", [P, 2, DC, S], F32R, stack=st)
                    cm = sb("ctx_masked", [P, 2, MT, D], F32R, stack=st)
                    cT = sb("ctx_t", [P, 2, DC, M + 1], F32R, stack=st)
                    pr = sb("probs", [P, M], stack=st)
                    pT = sb("probs_t", [P, 2, MT, P], F32R, stack=st)
                    mx = sb("row_max", [P, NT], stack=st)
                    nb = sb("neg_max", [P, NT], stack=st)
                    rs = sb("row_sum", [P, NT], stack=st)
                    ri = sb("row_inv", [P, NT], stack=st)
                    ac = sb("attn_ctx", [P, 2, NT, D], F32R, stack=st)
                    tT = xnT
                    s, every = semaphores(st, "xr_in stats inv xn_ready own cT_ps cT_hi cT_lo cm_hi cm_lo "
                                              "xT_ps xT_hi xT_lo q_ps q_hi q_lo s_ps s_max p_ready pT_ps pT_hi pT_lo "
                                              "ac_ps ac_inv ac_hi ac_lo t_ps t_hi t_lo y_ps xr_ready pzero")
                    groups = [(g, c) for g in range(MG) for c in range(DC)]
                    xb = x[bass.ds(b, 1)].rearrange("a n d -> (a n) d")
                    with nc.Block() as block:
                        @block.sync
                        def _(sp):
                            sp.dma_start(xr[:, :, :].rearrange("p (c r) d -> p c r d", r=2),
                                         xb.rearrange("(c p r) d -> p c r d", p=P, r=2)).then_inc(s["xr_in"], 16)
                            if not more:
                                sp.dma_start(sorted_in.rearrange("(p r) d -> p r d", p=P),
                                             zeros[:, :, :].to_broadcast([P, ZR, D])).then_inc(zeroed, 16)
                            sp.wait_ge(s["xr_in"], 16)

                        @block.gpsimd
                        def _(pool):
                            inverse_root(pool, s["stats"], s["inv"], 1)
                            for t in range(MT):
                                m = mrows(t)
                                pool.tensor_scalar(cm[0:m, 0, t, :], cn[0:m, t, :], mask01[0:m, t:t + 1], None,
                                                   ALU.mult).then_inc(s["cm_hi"], 1)
                            pool.wait_ge(s["xr_in"], 16)
                            for t in range(NT):
                                pool.tensor_tensor(xr[:, t, :], xr[:, t, :], pb_row[:, :], ALU.add).then_inc(s["xr_ready"], 1)

                        @block.tensor
                        def _(pe):
                            def turn_ctx(first, end):
                                for n in range(first, end):
                                    g, c = groups[n]
                                    if n >= 4:
                                        pe.wait_ge(s["cT_lo"], n - 3)
                                    for t in range(4 * g, min(4 * g + 4, MT)):
                                        m = mrows(t)
                                        o = (t - 4 * g) * P
                                        ins = pe.transpose(PS[:, n % 4, o:o + m], cn[0:m, t, c * P:(c + 1) * P],
                                                           ident[0:m, 0:m])
                                    ins.then_inc(s["cT_ps"], 1)

                            turn_ctx(0, 4)
                            pe.wait_ge(s["xn_ready"], 1)
                            for c in range(DC):
                                for t in range(NT):
                                    ins = pe.transpose(PS[:, 4 + c, t * P:(t + 1) * P], xn[:, t, c * P:(c + 1) * P],
                                                       ident[:, :])
                                ins.then_inc(s["xT_ps"], 1)
                            turn_ctx(4, 6)
                            pe.wait_ge(s["xT_lo"], DC)
                            for c in range(DC):
                                product(pe, bank(6 + c), lambda a, k: M_s[:, a, k, c * P:(c + 1) * P],
                                        lambda a, k: xnT[:, a, k, :], DC).then_inc(s["q_ps"], 1)
                            turn_ctx(6, len(groups))
                            pe.wait_ge(s["q_lo"], DC)
                            pe.wait_ge(s["cT_lo"], len(groups))

                            def scores(t, g):
                                if t and g == 0:
                                    pe.wait_ge(s["p_ready"], t)
                                w = mcols(g) + mcols(g) % 2
                                ins = product(pe, PS[:, g, 0:w], lambda a, k: qT[:, a, k, t * P:(t + 1) * P],
                                              lambda a, k: cT[:, a, k, g * 512:g * 512 + w], DC)
                                if g == MG - 1:
                                    ins.then_inc(s["s_ps"], 1)

                            def turn_probs(t, g):
                                pe.wait_ge(s["p_ready"], t + 1)
                                n = t * MG + g
                                if n >= 2:
                                    pe.wait_ge(s["pT_lo"], n - 1)
                                for i in range(4 * g, min(4 * g + 4, MT)):
                                    m = mrows(i)
                                    o = (i - 4 * g) * P
                                    ins = pe.transpose(PS[0:m, 4 + n % 2, o:o + P], pr[:, i * P:i * P + m], ident[:, :])
                                ins.then_inc(s["pT_ps"], 1)

                            def attend(t):
                                pe.wait_ge(s["pT_lo"], MG * (t + 1))
                                if t == 0:
                                    pe.wait_ge(s["cm_lo"], MT)
                                if t >= 2:
                                    pe.wait_ge(s["ac_lo"], t - 1)
                                n = 0
                                for i in range(MT):
                                    m = mrows(i)
                                    for a, c in PASSES:
                                        ins = pe.matmul(PS[:, 6 + t % 2, 0:D], pT[0:m, a, i, :], cm[0:m, c, i, :],
                                                        start=n == 0, stop=n == 3 * MT - 1)
                                        n += 1
                                ins.then_inc(s["ac_ps"], 1)

                            for g in range(MG):
                                scores(0, g)
                            for t in range(NT):
                                turn_probs(t, 0)
                                for g in range(MG):
                                    if g + 1 < MG:
                                        turn_probs(t, g + 1)
                                    if t + 1 < NT:
                                        scores(t + 1, g)
                                attend(t)
                            for r in range(2):
                                pe.wait_ge(s["ac_lo"], 2 * r + 2)
                                for c in range(DC):
                                    ins = product(pe, PS[:, 4 + r, c * D:(c + 1) * D],
                                                  lambda a, k: ac[:, a, 2 * r + k, c * P:(c + 1) * P],
                                                  lambda a, k: PT_s[:, a, k, :], DC)
                                ins.then_inc(s["t_ps"], 1)
                            for r in range(2):
                                pe.wait_ge(s["t_lo"], r + 1)
                                for c in range(DC):
                                    product(pe, PS[:, 2 * r + c, 0:D],
                                            lambda a, k: WvT_s[:, a, k, c * P:(c + 1) * P],
                                            lambda a, k: tT[:, a, r, k * D:(k + 1) * D], DC).then_inc(s["y_ps"], 1)

                        @block.scalar
                        def _(act):
                            def round_off(src, dst, ready, n, done):
                                act.wait_ge(ready, n)
                                act.activation(dst, src, ACT.Copy).then_inc(done, 1)

                            def round_ctx(first, end):
                                for n in range(first, end):
                                    g, c = groups[n]
                                    w = mcols(g)
                                    round_off(PS[:, n % 4, 0:w], cT[:, 0, c, g * 512:g * 512 + w], s["cT_ps"], n + 1,
                                              s["cT_hi"])

                            round_ctx(0, 4)
                            for c in range(DC):
                                round_off(bank(4 + c), xnT[:, 0, c, :], s["xT_ps"], c + 1, s["xT_hi"])
                            round_ctx(4, 6)
                            for c in range(DC):
                                round_off(bank(6 + c), qT[:, 0, c, :], s["q_ps"], c + 1, s["q_hi"])
                            round_ctx(6, len(groups))

                            def exp(t):
                                act.wait_ge(s["s_max"], t + 1)
                                if t:
                                    act.wait_ge(s["pT_ps"], MG * t)
                                act.activation(pr[:, :], PS[:, 0:MG, :].rearrange("p g n -> p (g n)")[:, 0:M],
                                               ACT.Exp, bias=nb[:, t:t + 1], scale=XSCALE,
                                               accum_out=rs[:, t:t + 1]).then_inc(s["p_ready"], 1)

                            exp(0)
                            for t in range(NT):
                                if t:
                                    act.wait_ge(s["ac_ps"], t)
                                for g in range(MG):
                                    n = t * MG + g
                                    k = min(4, MT - 4 * g)
                                    m = mrows(4 * g + k - 1)
                                    round_off(PS[0:m, 4 + n % 2, 0:k * P],
                                              pT[0:m, 0, 4 * g:4 * g + k, :].rearrange("p t n -> p (t n)"),
                                              s["pT_ps"], n + 1, s["pT_hi"])
                                if t + 1 < NT:
                                    exp(t + 1)
                                act.wait_ge(s["ac_ps"], t + 1)
                                act.wait_ge(s["ac_inv"], t + 1)
                                act.activation(ac[:, 0, t, :], PS[:, 6 + t % 2, 0:D], ACT.Copy,
                                               scale=ri[:, t:t + 1]).then_inc(s["ac_hi"], 1)
                            for r in range(2):
                                round_off(bank(4 + r), tT[:, 0, r, :], s["t_ps"], r + 1, s["t_hi"])

                        @block.vector
                        def _(dve):
                            own = chain(dve, s["own"])
                            dve.memset(cT[:, :, :, M:M + 1].bitcast(F32), 0.0).then_inc(s["pzero"], 1)
                            layer_norm(dve, own, xq, xn, s["xn_ready"], s["stats"], s["inv"])

                            def remainder(src, hi, lo, ready, n, done):
                                dve.wait_ge(ready, n)
                                dve.tensor_tensor(lo, src, hi.bitcast(F32), ALU.subtract).then_inc(done, 1)

                            def ctx_remainder(first, end):
                                for n in range(first, end):
                                    g, c = groups[n]
                                    w = mcols(g)
                                    a = g * 512
                                    remainder(PS[:, n % 4, 0:w], cT[:, 0, c, a:a + w], cT[:, 1, c, a:a + w], s["cT_hi"],
                                              n + 1, s["cT_lo"])

                            ctx_remainder(0, 4)
                            for c in range(DC):
                                remainder(bank(4 + c), xnT[:, 0, c, :], xnT[:, 1, c, :], s["xT_hi"], c + 1, s["xT_lo"])
                            ctx_remainder(4, 6)
                            for c in range(DC):
                                remainder(bank(6 + c), qT[:, 0, c, :], qT[:, 1, c, :], s["q_hi"], c + 1, s["q_lo"])
                            ctx_remainder(6, len(groups))

                            def row_max(t):
                                dve.wait_ge(s["s_ps"], t + 1)
                                own(dve.tensor_reduce(mx[:, t:t + 1],
                                                      PS[:, 0:MG, :].rearrange("p g n -> p (g n)")[:, 0:M], AX, ALU.max))
                                dve.tensor_scalar(nb[:, t:t + 1], mx[:, t:t + 1], -XSCALE, None, ALU.mult)\
                                    .then_inc(s["s_max"], 1)

                            row_max(0)
                            for t in range(MT):
                                m = mrows(t)
                                dve.wait_ge(s["cm_hi"], t + 1)
                                dve.scalar_tensor_tensor(out=cm[0:m, 1, t, :], in0=cn[0:m, t, :],
                                                         scalar=mask01[0:m, t:t + 1],
                                                         in1=cm[0:m, 0, t, :].bitcast(F32), op0=ALU.mult,
                                                         op1=ALU.subtract).then_inc(s["cm_lo"], 1)
                            for t in range(NT):
                                for g in range(MG):
                                    n = t * MG + g
                                    k = min(4, MT - 4 * g)
                                    m = mrows(4 * g + k - 1)
                                    remainder(PS[0:m, 4 + n % 2, 0:k * P],
                                              pT[0:m, 0, 4 * g:4 * g + k, :].rearrange("p t n -> p (t n)"),
                                              pT[0:m, 1, 4 * g:4 * g + k, :].rearrange("p t n -> p (t n)"),
                                              s["pT_hi"], n + 1, s["pT_lo"])
                                dve.wait_ge(s["p_ready"], t + 1)
                                dve.reciprocal(ri[:, t:t + 1], rs[:, t:t + 1]).then_inc(s["ac_inv"], 1)
                                if t + 1 < NT:
                                    row_max(t + 1)
                                dve.wait_ge(s["ac_hi"], t + 1)
                                dve.scalar_tensor_tensor(out=ac[:, 1, t, :], in0=PS[:, 6 + t % 2, 0:D],
                                                         scalar=ri[:, t:t + 1], in1=ac[:, 0, t, :].bitcast(F32),
                                                         op0=ALU.mult, op1=ALU.subtract).then_inc(s["ac_lo"], 1)
                            for r in range(2):
                                remainder(bank(4 + r), tT[:, 0, r, :],
                                          tT[:, 1, r, :], s["t_hi"], r + 1, s["t_lo"])
                            dve.wait_ge(s["xr_ready"], NT)
                            for r in range(2):
                                for c in range(DC):
                                    dve.wait_ge(s["y_ps"], 2 * r + c + 1)
                                    dve.tensor_tensor(x1[:, 2 * c + r, :], PS[:, 2 * r + c, 0:D], xr[:, 2 * c + r, :],
                                                      ALU.add)
                    clear(every)

                with ExitStack() as st:
                    h0 = sb("h0", [P, NT, D], stack=st)
                    early = sb("h_norm_both", [P, 2, NT * D], stack=st)
                    hn = early[:, 0].rearrange("p (t d) -> p t d", d=D)
                    h32 = early[:, 1].rearrange("p (c n) -> p c n", n=S)
                    oT = early[:, :, :].rearrange("p a (g n) -> p (a g) n", n=S)
                    hT = sb("h_ts", [P, 2, DC, S], F32R, stack=st)
                    qk = sb("qk_t", [P, 2, 2 * DC, S], F32R, stack=st)
                    va = sb("v_ones", [P, NT, H, 32], stack=st)
                    Qs = sb("q_stack", [P, H // 2, S], F32R, stack=st)
                    Ks = sb("k_stack", [P, H // 2, S], F32R, stack=st)
                    mx = sb("s_max_rows", [P, NT, H], stack=st)
                    m2 = sb("neg_max_rows", [4, HG, 2, S], F32R, stack=st)
                    PG = 4
                    pe_ring = 6
                    pb = sb("s_probs", [P, pe_ring, 4, S], stack=st)
                    rec = sb("s_inv", [P, NT, H], stack=st)
                    on = x1
                    x2 = pb[:, 0, 2:4, :].rearrange("p a (b d) -> p (a b) d", d=D)
                    oS = hT
                    s, every = semaphores(st, "x1_stored stats inv hn_ready own hT_ps h32_ready hT_hi hT_lo qk_ps qk_hi qk_lo v_ps v_ready "
                                              "pile_ps q_piled k_piled late_piled s_ps s_max m_ps m_lo m_rows st_ps p_ready pv_done "
                                              "oT_ready on_ps on_ready oS_ps oS_hi oS_lo x2_ps x2_ready h0_ready h0b stored batch_in")
                    LAG = 30
                    UNITS = H * NT
                    OUT_AT = (UNITS + 3, UNITS + 5, UNITS + 22)
                    CHUNK_AT = UNITS + 12

                    def s_unit(i):
                        return i // NT, i % NT

                    def t_unit(j):
                        return j // (4 * NT), (j // 4) % NT, j % 4

                    with nc.Block() as block:
                        @block.sync
                        def _(sp):
                            sp.dma_start(x1_rows[bass.ds(b * S, S), :].rearrange("(t p) d -> p t d", p=P), x1[:, :, :])\
                                .then_inc(s["x1_stored"], 16)
                            if more:
                                load_batch(sp, b + 1, s["batch_in"])
                            for g in range(HG):
                                sp.wait_ge(s["m_lo"], g + 1)
                                for h in range(4):
                                    row = 64 * (h % 2) + 3 * DK
                                    sp.dma_start(Qs[row:row + 2, (4 * g + h) // 2, :].bitcast(F32),
                                                 m2[h:h + 1, g, :, :].bitcast(F32))\
                                        .then_inc(s["m_rows"], 16)
                            for t in range(NT):
                                sp.wait_ge(s["x2_ready"], t + 1)
                                sp.dma_start(x2_rows[bass.ds(b * S + t * P, P), :], x2[:, t, :]).then_inc(s["stored"], 16)
                            sp.wait_ge(s["stored"], 16 * NT)
                            if more:
                                sp.wait_ge(s["batch_in"], 48)

                        @block.gpsimd
                        def _(pool):
                            pool.memset(va[:, :, :, DK:32], 1.0)
                            inverse_root(pool, s["stats"], s["inv"], 2)
                            pool.wait_ge(s["h0_ready"], 1)
                            for t in range(NT):
                                pool.tensor_tensor(h0[:, t, :], h0[:, t, :], bo_row[:, :], ALU.add).then_inc(s["h0b"], 1)

                        @block.tensor
                        def _(pe):
                            def turn(src, b0, done):
                                for c in range(DC):
                                    for t in range(NT):
                                        ins = pe.transpose(PS[:, b0 + c, t * P:(t + 1) * P],
                                                           src[:, t, c * P:(c + 1) * P], ident[:, :])
                                    ins.then_inc(done, 1)

                            def turn_out(g):
                                pe.wait_ge(s["oT_ready"], g + 1)
                                if g == 0:
                                    pe.wait_ge(s["s_max"], UNITS)
                                if g == 3:
                                    pe.wait_ge(s["on_ready"], 1)
                                for t in range(NT):
                                    ins = pe.transpose(PS[:, g % 3, t * P:(t + 1) * P], oT[:, g, t * P:(t + 1) * P], ident[:, :])
                                ins.then_inc(s["on_ps"], 1)

                            def turn_chunk(c, b0):
                                pe.wait_ge(s["on_ready"], 2 * c + 2)
                                for t in range(NT):
                                    ins = pe.transpose(PS[:, b0, t * P:(t + 1) * P], on[:, t, c * P:(c + 1) * P], ident[:, :])
                                ins.then_inc(s["oS_ps"], 1)

                            def project(n, b0):
                                f = n % 2 * DC + n // 2
                                product(pe, bank(b0), lambda a, k: Wqkv_s[:, a, k, f * P:(f + 1) * P],
                                        lambda a, k: hT[:, a, k, :], DC).then_inc(s["qk_ps"], 1)

                            def project_v(t):
                                product(pe, PS[:, 5 + t // 2, t % 2 * D:(t % 2 + 1) * D],
                                        lambda a, k: hT[:, a, k, t * P:(t + 1) * P],
                                        lambda a, k: Wqkv_s[:, a, k, 2 * D:3 * D], DC).then_inc(s["v_ps"], 1)

                            def pile_up(n, b0):
                                at, q_or_k = n // 2, n % 2
                                pe.wait_ge(s["qk_lo"], 2 * (at // 4) + 2)
                                for part in range(2):
                                    ins = pe.matmul(bank(b0), pile[:, q_or_k, part, at % 4, :],
                                                    qk[:, part, q_or_k * DC + at // 4, :], start=part == 0, stop=part == 1)
                                ins.then_inc(s["pile_ps"], 1)

                            pe.wait_ge(s["hn_ready"], 1)
                            turn(hn, 0, s["hT_ps"])
                            pe.wait_ge(s["hT_lo"], DC)
                            for n in range(2):
                                project(n, 2 + n)
                            for n in range(H // 2):
                                if n >= 4:
                                    pe.wait_ge(s[("q_piled", "k_piled")[n % 2]], n // 2 - 1)
                                pile_up(n, 4 + n % 4)
                            pe.wait_ge(s["q_piled"], H // 4)
                            pe.wait_ge(s["k_piled"], H // 4)

                            def pv(u):
                                g, kt = u // NT, u % NT
                                pe.wait_ge(s["p_ready"], 4 * u + 4)
                                if kt == 0 and g:
                                    pe.wait_ge(s["oT_ready"], g)
                                for h in range(4):
                                    ins = pe.matmul(PS[32 * h:32 * h + 32, 6, :], va[:, kt, 4 * g + h, :],
                                                    pb[:, u % pe_ring, h, :], start=kt == 0, stop=kt == NT - 1)
                                ins.then_inc(s["pv_done"], 1)

                            for i in range(UNITS + LAG + 8):
                                if i < UNITS:
                                    h, qt = s_unit(i)
                                    r = 64 * (h % 2)
                                    if i >= 3:
                                        pe.wait_ge(s["s_max"], i - 2)
                                    if i == UNITS // 2:
                                        pe.wait_ge(s["late_piled"], H // 2)
                                    pe.matmul(bank(i % 3), Qs[r:r + 3 * DK, h // 2, qt * P:(qt + 1) * P],
                                              Ks[r:r + 3 * DK, h // 2, :], start=True, stop=True).then_inc(s["s_ps"], 1)
                                if i in (0, 2):
                                    project(2 + i // 2, 3 + i // 2)
                                if i in (4, 5, 6, 7):
                                    project_v(i - 4)
                                if 8 <= i < 8 + H // 2:
                                    n = i - 8
                                    if n >= 2:
                                        pe.wait_ge(s["late_piled"], n - 1)
                                    pile_up(H // 2 + n, 3 + n % 2)
                                if i in OUT_AT:
                                    turn_out(OUT_AT.index(i))
                                if i == CHUNK_AT:
                                    pe.wait_ge(s["m_lo"], HG)
                                    turn_chunk(0, 7)
                                if i % 16 == 2 and 1 <= i // 16 <= HG:
                                    g = i // 16 - 1
                                    pe.wait_ge(s["s_max"], 16 * (g + 1))
                                    if g:
                                        pe.wait_ge(s["m_lo"], g)
                                    for qt in range(NT):
                                        ins = pe.transpose(PS[0:4, 7, qt * P:(qt + 1) * P], mx[:, qt, 4 * g:4 * g + 4],
                                                           ident[:, :])
                                    ins.then_inc(s["m_ps"], 1)
                                j = i - LAG
                                if 0 <= j < UNITS:
                                    g, kt, hh = t_unit(j)
                                    h = 4 * g + hh
                                    r = 64 * (h % 2)
                                    if j == 0:
                                        pe.wait_ge(s["late_piled"], H // 2)
                                        pe.wait_ge(s["v_ready"], NT)
                                    if j % 16 == 0:
                                        pe.wait_ge(s["m_rows"], 64 * (g + 1))
                                    if j >= 3:
                                        pe.wait_ge(s["p_ready"], j - 2)
                                    pe.matmul(bank(3 + j % 3), Ks[r:r + 3 * DK + 2, h // 2, kt * P:(kt + 1) * P],
                                              Qs[r:r + 3 * DK + 2, h // 2, :], start=True, stop=True).then_inc(s["st_ps"], 1)
                                u = (j - 6) // 4
                                if j >= 6 and (j - 6) % 4 == 0 and u < UNITS // 4 and u % PG == PG - 1:
                                    for n in range(u - PG + 1, u + 1):
                                        pv(n)
                            turn_out(HG - 1)
                            pe.wait_ge(s["oS_lo"], 1)
                            pe.wait_ge(s["on_ready"], 3)
                            pe.wait_ge(s["p_ready"], UNITS)
                            for c in range(DC):
                                if c:
                                    turn_chunk(1, 1)
                                    pe.wait_ge(s["oS_lo"], 2)
                                for t in range(NT):
                                    ins = product(pe, PS[:, 2 + t, 0:D], lambda a, k: oS[:, a, c, t * P:(t + 1) * P],
                                                  lambda a, k: Wo_s[:, a, c, :], 1, first=c == 0, last=c == DC - 1)
                                    if c:
                                        ins.then_inc(s["x2_ps"], 1)

                        @block.scalar
                        def _(act):
                            for c in range(DC):
                                act.wait_ge(s["hT_ps"], c + 1)
                                act.activation(h32[:, c, :], bank(c), ACT.Identity, bias=cols[:, 1, c:c + 1],
                                               scale=cols[:, 0, c:c + 1]).then_inc(s["h32_ready"], 1)
                                act.wait_ge(s["h32_ready"], c + 1)
                                act.activation(hT[:, 0, c, :], h32[:, c, :], ACT.Copy).then_inc(s["hT_hi"], 1)
                            def round_qk(n, b0):
                                act.wait_ge(s["qk_ps"], n + 1)
                                f = n % 2 * DC + n // 2
                                act.activation(qk[:, 0, f, :], bank(b0), ACT.Identity, bias=bqk_col[:, f:f + 1])\
                                    .then_inc(s["qk_hi"], 1)

                            def keep_stack(n, b0, done):
                                act.wait_ge(s["pile_ps"], n + 1)
                                if n % 2:
                                    ins = act.activation(Ks[:, n // 2, :], bank(b0), ACT.Identity, bias=ones_at[:, 0:1])
                                else:
                                    ins = act.activation(Qs[:, n // 2, :], bank(b0), ACT.Copy)
                                ins.then_inc(done, 1)

                            for n in range(2):
                                round_qk(n, 2 + n)
                            for n in range(1, H // 2, 2):
                                keep_stack(n, 4 + n % 4, s["k_piled"])
                            for n in range(2, 4):
                                round_qk(n, 1 + n)
                            for n in range(H // 2):
                                keep_stack(H // 2 + n, 3 + n % 2, s["late_piled"])

                            def round_out(c, b0):
                                act.wait_ge(s["oS_ps"], c + 1)
                                act.activation(oS[:, 0, c, :], bank(b0), ACT.Copy).then_inc(s["oS_hi"], 1)

                            def keep_o(g):
                                act.wait_ge(s["pv_done"], NT * (g + 1))
                                act.activation(oT[:, g, :], bank(6), ACT.Copy).then_inc(s["oT_ready"], 1)

                            for j in range(UNITS):
                                u = j // 4
                                if j % 4 == 0 and u >= pe_ring:
                                    act.wait_ge(s["pv_done"], u - pe_ring + 1)
                                act.wait_ge(s["st_ps"], j + 1)
                                act.activation(pb[:, u % pe_ring, j % 4, :], bank(3 + j % 3), ACT.Exp, scale=SSCALE)\
                                    .then_inc(s["p_ready"], 1)
                                if j % 16 == 4 and j > 16:
                                    keep_o(j // 16 - 1)
                                if j == CHUNK_AT - LAG + 4:
                                    round_out(0, 7)
                            keep_o(HG - 1)
                            round_out(1, 1)

                        @block.vector
                        def _(dve):
                            own = chain(dve, s["own"])
                            layer_norm(dve, own, x1, h0, s["h0_ready"], s["stats"], s["inv"], hn, s["hn_ready"])

                            def h_lo(n, c):
                                dve.wait_ge(s["hT_hi"], n)
                                dve.tensor_tensor(hT[:, 1, c, :], h32[:, c, :], hT[:, 0, c, :].bitcast(F32), ALU.subtract)\
                                    .then_inc(s["hT_lo"], 1)

                            for c in range(DC):
                                h_lo(c + 1, c)
                            def qk_low(n, b0):
                                f = n % 2 * DC + n // 2
                                dve.wait_ge(s["qk_hi"], n + 1)
                                dve.scalar_tensor_tensor(out=qk[:, 1, f, :], in0=bank(b0), scalar=bqk_col[:, f:f + 1],
                                                         in1=qk[:, 0, f, :].bitcast(F32), op0=ALU.add,
                                                         op1=ALU.subtract).then_inc(s["qk_lo"], 1)

                            def keep_v(t):
                                dve.wait_ge(s["v_ps"], t // 2 * 2 + 2)
                                dve.tensor_tensor(va[:, t, :, 0:DK],
                                                  PS[:, 5 + t // 2, t % 2 * D:(t % 2 + 1) * D].rearrange("p (h d) -> p h d", h=H),
                                                  bv_row[:, :].rearrange("p (h d) -> p h d", h=H), ALU.add)\
                                    .then_inc(s["v_ready"], 1)

                            def round_max(g):
                                dve.wait_ge(s["m_ps"], g + 1)
                                own(dve.tensor_scalar(m2[:, g, 0, :], PS[0:4, 7, :], -1.0, None, ALU.mult))
                                dve.scalar_tensor_tensor(out=m2[:, g, 1, :], in0=PS[0:4, 7, :], scalar=-1.0,
                                                         in1=m2[:, g, 0, :].bitcast(F32), op0=ALU.mult,
                                                         op1=ALU.subtract).then_inc(s["m_lo"], 1)

                            for n in range(2):
                                qk_low(n, 2 + n)
                            for n in range(0, H // 2, 2):
                                dve.wait_ge(s["pile_ps"], n + 1)
                                dve.tensor_copy(Qs[:, n // 2, :], bank(4 + n % 4)).then_inc(s["q_piled"], 1)
                            for i in range(UNITS):
                                h, qt = s_unit(i)
                                dve.wait_ge(s["s_ps"], i + 1)
                                dve.tensor_reduce(mx[:, qt, h:h + 1], bank(i % 3), AX, ALU.max).then_inc(s["s_max"], 1)
                                if i in (1, 3):
                                    qk_low(2 + i // 2, 3 + i // 2)
                                if i in (6, 7, 8, 9):
                                    keep_v(i - 6)
                                if i % 16 == 3 and i > 16:
                                    round_max(i // 16 - 1)
                            round_max(HG - 1)
                            for g in range(HG):
                                o = PS[:, g % 3, :].rearrange("p (t h d) -> p t h d", h=4, d=32)
                                inv = rec[:, :, 4 * g:4 * g + 4]
                                dve.wait_ge(s["on_ps"], g + 1)
                                if g == 0:
                                    dve.wait_ge(s["x1_stored"], 16)
                                own(dve.reciprocal(inv, o[:, :, :, DK]))
                                dve.tensor_tensor(on[:, :, :].rearrange("p t (h d) -> p t h d", h=H)[:, :, 4 * g:4 * g + 4, :],
                                                  o[:, :, :, 0:DK], inv.unsqueeze(3).to_broadcast([P, NT, 4, DK]), ALU.mult)\
                                    .then_inc(s["on_ready"], 1)
                                if g % 2:
                                    c = g // 2
                                    dve.wait_ge(s["oS_hi"], c + 1)
                                    dve.tensor_tensor(oS[:, 1, c, :], bank((7, 1)[c]), oS[:, 0, c, :].bitcast(F32),
                                                      ALU.subtract).then_inc(s["oS_lo"], 1)
                            dve.wait_ge(s["h0b"], NT)
                            for t in range(NT):
                                dve.wait_ge(s["x2_ps"], t + 1)
                                dve.tensor_tensor(x2[:, t, :], PS[:, 2 + t, 0:D], h0[:, t, :], ALU.add).then_inc(s["x2_ready"], 1)
                    clear(every)

            with nc.Fori(0, B - 1) as b:
                attention(b, True)
            attention(B - 1, False)
        inputs.close()

        with ExitStack() as est:
            slot = sb("slot", [P, 2, NB], U32, stack=est)
            block_expert = sb("block_expert", [P, NBLK + 2], I32, stack=est)
            base = sb("base", [P, NB, D], stack=est)
            hx = sb("h_all", [P, NB, D], stack=est)
            w1r = sb("w1_raw", [P, 2, DC, DFF], stack=est)
            w2r = sb("w2_raw", [P, 2, FT, D], stack=est)
            w1s = sb("w1_s", [P, 2, 2, DC, DFF], F32R, stack=est)
            w2s = sb("w2_s", [P, 2, 2, FT, D], F32R, stack=est)
            b1c = sb("b1_now", [P, 4, FT], stack=est)
            TT = BT // P

            def expert_of(sp, j):
                return sp.value_load(block_expert[0:1, bass.ds(j, 1)], min_val=0, max_val=E - 1)

            def load_weights(sp, e, k, w_in):
                sp.dma_start(w1r[:, k % 2], W1[bass.ds(e, 1)].rearrange("a (c p) f -> p (a c) f", p=P)).then_inc(w_in, 16)
                sp.dma_start(w2r[:, k % 2], W2[bass.ds(e, 1)].rearrange("a (c p) d -> p (a c) d", p=P)).then_inc(w_in, 16)
                sp.dma_start(b1c[:, k % 4, :], b1_col[:, bass.ds(e * FT, FT)]).then_inc(w_in, 16)

            def piece(ap, i, n):
                size = DC * DFF // n
                return ap.rearrange("p c f -> p (c f)")[:, i * size:(i + 1) * size]

            def w1_piece(ap, i):
                return ap[:, i % DC, i // DC * (DFF // 2):(i // DC + 1) * (DFF // 2)]

            def w1_high(act, k, i, done):
                act.activation(w1_piece(w1s[:, k % 2, 0], i), w1_piece(w1r[:, k % 2], i), ACT.Copy).then_inc(done, 1)

            def w1_low(dve, k, i, ready, n, done):
                dve.wait_ge(ready, n)
                dve.tensor_tensor(w1_piece(w1s[:, k % 2, 1], i), w1_piece(w1r[:, k % 2], i),
                                  w1_piece(w1s[:, k % 2, 0], i).bitcast(F32), ALU.subtract).then_inc(done, 1)

            def w2_high(dve, k, i, done):
                dve.tensor_copy(piece(w2s[:, k % 2, 0], i, 2), piece(w2r[:, k % 2], i, 2)).then_inc(done, 1)

            def w2_low(pool, k, i, ready, n, done):
                pool.wait_ge(ready, n)
                pool.tensor_tensor(piece(w2s[:, k % 2, 1], i, 2), piece(w2r[:, k % 2], i, 2),
                                   piece(w2s[:, k % 2, 0], i, 2).bitcast(F32), ALU.subtract).then_inc(done, 1)

            with ExitStack() as st:
                x1a = [w[:, 1].rearrange("p c f -> p (c f)").rearrange("p (t d) -> p t d", d=D) for w in (w1r, w2r)]
                h32 = sb("g_t32", [P, 2, DC, S], stack=st)
                hT = sb("g_ts", [P, 2, 2, DC, S], F32R, stack=st)
                st_a = sb("g_stats", [P, NB, 6], stack=st)
                mv = sb("g_mean_var", [P, NB, 2], stack=st)
                veps = sb("g_var_eps", [P, NB], stack=st)
                rstd = sb("g_rstd", [P, NB], stack=st)
                lg = sb("logits", [P, NB, E], stack=st)
                top = sb("top", [P, NB, 8], stack=st)
                ti = sb("top_index", [P, NB, 8], U32, stack=st)
                tf = sb("top_index_f", [P, NB, 8], stack=st)
                dd = sb("top_diff", [P, NB], stack=st)
                e2 = sb("top_exp", [P, NB], stack=st)
                sm = sb("top_sum", [P, NB], stack=st)
                wa = sb("w_first", [P, NB, E], stack=st)
                wb = sb("w_second", [P, NB, E], stack=st)
                wT = h32[0:E, :, :, :].rearrange("e a c n -> e (a c n)")
                both = sb("picked", [P, NB, E], stack=st)
                tot = sb("tile_totals", [P, NB, E], stack=st)
                pos = sb("position", [P, NB, E], stack=st)
                run = sb("tiles_before", [P, NB + 1, E], stack=st)
                nblk = sb("blocks_of", [P, E], stack=st)
                end = sb("block_end", [P, E], stack=st)
                beg = sb("first_row", [P, E], stack=st)
                num = sb("block_number", [P, NBLK + 2], stack=st)
                eb = sb("expert_of", [P, NBLK + 2], stack=st)
                sl = sb("slot_terms", [P, 2, NB, E], stack=st)
                sf = sb("slot_f", [P, 2, NB], stack=st)
                s, every = semaphores(st, "own stats inv h_ready hT_ps h32_ready hT_hi hT_lo lg_ps d_ready e_ready w_ready wT_ps "
                                          "wT_ready bias_ps x1_in x1_added expert_ready w_in0 w_in1 w1_hi w1_lo w2_hi picked_ready rank_ps num_ready slot_ready scattered")
                loaded = [st.enter_context(nc.semaphore(f"rows_in_{b}")) for b in range(B)]

                def by_token(w):
                    return w.unsqueeze(2).to_broadcast([P, NB, E])

                def by_expert(w):
                    return w.unsqueeze(1).to_broadcast([P, NB, E])

                with nc.Block() as block:
                    @block.sync
                    def _(sp):
                        for b in range(B):
                            sp.dma_start(base[:, b * NT:(b + 1) * NT, :],
                                         x2_rows[b * S:(b + 1) * S, :].rearrange("(t p) d -> p t d", p=P))\
                                .then_inc(loaded[b], 16)
                        for n in range(2):
                            sp.dma_start(x1a[n], x1_rows[n * NB * P // 2:(n + 1) * NB * P // 2, :]
                                         .rearrange("(t p) d -> p t d", p=P)).then_inc(s["x1_in"], 16)
                        sp.wait_ge(s["expert_ready"], 1)
                        load_weights(sp, expert_of(sp, 0), 0, s["w_in0"])
                        sp.wait_ge(s["x1_added"], 2)
                        load_weights(sp, expert_of(sp, 1), 1, s["w_in1"])
                        sp.wait_ge(s["w_in1"], 48)

                    @block.scalar
                    def _(act):
                        for b in range(B):
                            for c in range(DC):
                                n = b * DC + c
                                act.wait_ge(s["hT_ps"], n + 1)
                                if n >= 2 * DC:
                                    act.wait_ge(s["hT_lo"], n - 2 * DC + 1)
                                act.activation(h32[:, b % 2, c, :], PS[:, n % 4, :], ACT.Identity,
                                               bias=cols[:, 3, c:c + 1], scale=cols[:, 2, c:c + 1])\
                                    .then_inc(s["h32_ready"], 1)
                                act.wait_ge(s["h32_ready"], n + 1)
                                if n >= 2 * DC:
                                    act.wait_ge(s["lg_ps"], b - 1)
                                act.activation(hT[:, b % 2, 0, c, :], h32[:, b % 2, c, :], ACT.Copy)\
                                    .then_inc(s["hT_hi"], 1)
                        act.wait_ge(s["d_ready"], 1)
                        act.activation(e2[:, :], dd[:, :], ACT.Exp).then_inc(s["e_ready"], 1)
                        for n in range(NB // 4):
                            act.wait_ge(s["wT_ps"], n + 1)
                            act.activation(wT[:, n * 4 * P:(n + 1) * 4 * P], PS[0:E, 2 + n, :], ACT.Copy)\
                                .then_inc(s["wT_ready"], 1)
                        act.wait_ge(s["w_in0"], 48)
                        for i in range(4):
                            w1_high(act, 0, i, s["w1_hi"])

                    @block.gpsimd
                    def _(pool):
                        for j in range(NBLK + 2):
                            ins = pool.memset(num[:, j:j + 1], float(j))
                        ins.then_inc(s["num_ready"], 1)
                        pool.wait_ge(s["stats"], 1)
                        pool.tensor_tensor(rstd[:, :], veps[:, :], halves[:, :], ALU.pow).then_inc(s["inv"], 1)
                        pool.wait_ge(s["slot_ready"], 1)
                        pool.wait_ge(zeroed, 16)
                        for t in range(NB):
                            for k in range(2):
                                pool.indirect_dma_start(
                                    out=sorted_in[:, :], out_offset=bass.IndirectOffsetOnAxis(ap=slot[:, k, t:t + 1], axis=0),
                                    in_=hx[:, t, :], in_offset=None).then_inc(s["scattered"], 16)
                        pool.wait_ge(s["scattered"], 32 * NB)

                    @block.tensor
                    def _(pe):
                        def turn(b):
                            pe.wait_ge(s["h_ready"], NT * (b + 1))
                            for c in range(DC):
                                n = b * DC + c
                                if n >= 4:
                                    pe.wait_ge(s["h32_ready"], n - 3)
                                for t in range(NT):
                                    ins = pe.transpose(PS[:, n % 4, t * P:(t + 1) * P],
                                                       hx[:, b * NT + t, c * P:(c + 1) * P], ident[:, :])
                                ins.then_inc(s["hT_ps"], 1)

                        turn(0)
                        for b in range(B):
                            if b + 1 < B:
                                turn(b + 1)
                            pe.wait_ge(s["hT_lo"], DC * (b + 1))
                            for t in range(NT):
                                ins = product(pe, PS[:, 6, (b * NT + t) * E:(b * NT + t + 1) * E],
                                              lambda a, k: hT[:, b % 2, a, k, t * P:(t + 1) * P],
                                              lambda a, k: Wg_s[:, a, k, :], DC)
                            ins.then_inc(s["lg_ps"], 1)
                        pe.wait_ge(s["picked_ready"], 1)
                        flat = both[:, :, :].rearrange("p t e -> p (t e)")
                        pe.matmul(PS[:, 0, 0:NB * E], tri[:, :], flat, start=True, stop=True)
                        pe.matmul(PS[:, 1, 0:NB * E], ones[:, :], flat, start=True, stop=True).then_inc(s["rank_ps"], 1)
                        pe.wait_ge(s["w_ready"], 1)
                        for t in range(NB):
                            ins = pe.transpose(PS[0:E, 2 + t // 4, t % 4 * P:(t % 4 + 1) * P], wa[:, t, :], ident[:, :])
                            if t % 4 == 3:
                                ins.then_inc(s["wT_ps"], 1)
                        pe.wait_ge(s["wT_ready"], NB // 4)
                        for t in range(NB):
                            ins = pe.matmul(PS[:, t // 2, t % 2 * D:(t % 2 + 1) * D], wT[:, t * P:(t + 1) * P], b2_sb[:, :],
                                            start=True, stop=True)
                            if t % 2:
                                ins.then_inc(s["bias_ps"], 1)

                    @block.vector
                    def _(dve):
                        own = chain(dve, s["own"])
                        for t in range(NB):
                            if t % NT == 0:
                                dve.wait_ge(loaded[t // NT], 16)
                            ins = dve.bn_stats(st_a[:, t, :], base[:, t, :])
                        own(ins)
                        for t in range(NB):
                            ins = dve.bn_aggr(mv[:, t, :], st_a[:, t, :])
                        own(ins)
                        dve.tensor_scalar(veps[:, :], mv[:, :, 1], EPS, None, ALU.add).then_inc(s["stats"], 1)
                        dve.wait_ge(s["inv"], 1)
                        for t in range(NB):
                            dve.tensor_scalar(hx[:, t, :], base[:, t, :], mv[:, t, 0:1], rstd[:, t:t + 1],
                                              ALU.subtract, ALU.mult).then_inc(s["h_ready"], 1)
                        for n in range(B * DC):
                            b, c = n // DC, n % DC
                            dve.wait_ge(s["hT_hi"], n + 1)
                            dve.tensor_tensor(hT[:, b % 2, 1, c, :], h32[:, b % 2, c, :],
                                              hT[:, b % 2, 0, c, :].bitcast(F32), ALU.subtract).then_inc(s["hT_lo"], 1)
                        dve.wait_ge(s["lg_ps"], B)
                        own(dve.tensor_tensor(lg[:, :, :], PS[:, 6, 0:NB * E].rearrange("p (t e) -> p t e", e=E),
                                              by_expert(gb_row[:, :]), ALU.add))
                        for t in range(NB):
                            ins = dve.max(top[:, t, :], lg[:, t, :])
                        own(ins)
                        dve.tensor_tensor(dd[:, :], top[:, :, 1], top[:, :, 0], ALU.subtract).then_inc(s["d_ready"], 1)
                        for t in range(NB):
                            ins = dve.max_index(ti[:, t, :], top[:, t, :], lg[:, t, :])
                        own(ins)
                        own(dve.tensor_copy(tf[:, :, :], ti[:, :, :]))
                        for k in range(2):
                            ins = dve.tensor_tensor(pick[:, k], by_expert(iota_e[:, :]), by_token(tf[:, :, k]), ALU.is_equal)
                        own(ins)
                        dve.tensor_tensor(both[:, :, :], pick[:, 0], pick[:, 1], ALU.add).then_inc(s["picked_ready"], 1)
                        own(dve.memset(run[:, 0, :], 0.0))
                        dve.wait_ge(s["rank_ps"], 1)
                        own(dve.tensor_copy(tot[:, :, :].rearrange("p t e -> p (t e)"), PS[:, 1, 0:NB * E]))
                        for t in range(NB):
                            own(dve.tensor_tensor(run[:, t + 1, :], run[:, t, :], tot[:, t, :], ALU.add))
                        own(dve.tensor_scalar(nblk[:, :], run[:, NB, :], 0.0, None, ALU.is_gt))
                        for j in range(1, NB * P // BT):
                            own(dve.scalar_tensor_tensor(out=nblk[:, :], in0=run[:, NB, :], scalar=float(j * BT),
                                                         in1=nblk[:, :], op0=ALU.is_gt, op1=ALU.add))
                        own(dve.tensor_copy(end[:, 0:1], nblk[:, 0:1]))
                        for e in range(1, E):
                            own(dve.tensor_tensor(end[:, e:e + 1], end[:, e - 1:e], nblk[:, e:e + 1], ALU.add))
                        own(dve.tensor_tensor(beg[:, :], end[:, :], nblk[:, :], ALU.subtract))
                        own(dve.tensor_scalar(beg[:, :], beg[:, :], float(BT), None, ALU.mult))
                        own(dve.tensor_tensor(pos[:, :, :].rearrange("p t e -> p (t e)"), PS[:, 0, 0:NB * E],
                                              run[:, 0:NB, :].rearrange("p t e -> p (t e)"), ALU.add))
                        own(dve.tensor_tensor(pos[:, :, :], pos[:, :, :], beg[:, :].unsqueeze(1).to_broadcast([P, NB, E]),
                                              ALU.add))
                        for k in range(2):
                            own(dve.tensor_tensor(sl[:, k], pos[:, :, :], pick[:, k], ALU.mult))
                            own(dve.tensor_reduce(sf[:, k, :], sl[:, k], AX, ALU.add))
                        dve.tensor_copy(slot[:, :, :], sf[:, :, :]).then_inc(s["slot_ready"], 1)
                        dve.wait_ge(s["num_ready"], 1)
                        own(dve.tensor_scalar(eb[:, :], num[:, :], end[:, 0:1], None, ALU.is_ge))
                        for e in range(1, E - 1):
                            own(dve.scalar_tensor_tensor(out=eb[:, :], in0=num[:, :], scalar=end[:, e:e + 1],
                                                         in1=eb[:, :], op0=ALU.is_ge, op1=ALU.add))
                        dve.tensor_copy(block_expert[:, :], eb[:, :]).then_inc(s["expert_ready"], 1)
                        dve.wait_ge(s["e_ready"], 1)
                        own(dve.tensor_scalar(sm[:, :], e2[:, :], 1.0, None, ALU.add))
                        own(dve.reciprocal(gate[:, 0], sm[:, :]))
                        own(dve.tensor_tensor(gate[:, 1], e2[:, :], gate[:, 0], ALU.mult))
                        own(dve.tensor_tensor(wa[:, :, :], pick[:, 0], by_token(gate[:, 0]), ALU.mult))
                        own(dve.tensor_tensor(wb[:, :, :], pick[:, 1], by_token(gate[:, 1]), ALU.mult))
                        dve.tensor_tensor(wa[:, :, :], wa[:, :, :], wb[:, :, :], ALU.add).then_inc(s["w_ready"], 1)
                        dve.wait_ge(s["x1_in"], 32)
                        for n in range(2):
                            own(dve.tensor_tensor(base[:, 8 * n:8 * n + 8, :], base[:, 8 * n:8 * n + 8, :], x1a[n], ALU.add))
                            dve.engine_nop().then_inc(s["x1_added"], 1)
                        for n in range(NB // 2):
                            dve.wait_ge(s["bias_ps"], n + 1)
                            dve.tensor_tensor(base[:, 2 * n:2 * n + 2, :].rearrange("p t d -> p (t d)"), PS[:, n, :],
                                              base[:, 2 * n:2 * n + 2, :].rearrange("p t d -> p (t d)"), ALU.add)
                        dve.wait_ge(s["w_in0"], 48)
                        for i in range(2):
                            w2_high(dve, 0, i, s["w2_hi"])
                        for i in range(2):
                            dve.wait_ge(s["w2_hi"], 2)
                            dve.tensor_tensor(piece(w2s[:, 0, 1], i, 2), piece(w2r[:, 0], i, 2),
                                              piece(w2s[:, 0, 0], i, 2).bitcast(F32), ALU.subtract)
                        for i in range(4):
                            w1_low(dve, 0, i, s["w1_hi"], i + 1, s["w1_lo"])
                clear(every)

            with ExitStack() as st:
                xs = sb("sorted_x", [P, 2, BT // P, D], stack=st)
                x32 = sb("sorted_x_t32", [P, DC, BT], stack=st)
                xT = sb("sorted_x_t", [P, 2, 2, DC, BT], F32R, stack=st)
                RING = 3
                HIGH_AT, X_AT, W2_AT, LOW_AT = (2, 3, 4, 5), (0, 1), (2, 4), (3, 5, 6, 7)
                hid = sb("hid", [P, RING, BT], stack=st)
                hs = sb("hid_s", [P, RING, 2, BT], F32R, stack=st)
                ys = sb("sorted_y", [P, 2, BT // P, D], stack=st)
                s, every = semaphores(st, "w_in_0 w_in_1 x_in_0 x_in_1 w1_hi w1_lo w2_hi w2_lo xT_ps x32_ready xT_hi xT_lo hid_ps hid_ready "
                                          "hid_hi hid_lo used y_ready y_stored_0 y_stored_1")
                def turn(pe, k):
                    for c in range(DC):
                        for t in range(TT):
                            ins = pe.transpose(PS[:, 7, c * BT + t * P:c * BT + (t + 1) * P],
                                               xs[:, k % 2, t, c * P:(c + 1) * P], ident[:, :])
                    ins.then_inc(s["xT_ps"], 1)

                def x_high(act, k, c, n):
                    act.activation(x32[:, c, :], PS[:, 7, c * BT:(c + 1) * BT], ACT.Identity,
                                   bias=cols[:, 3, c:c + 1], scale=cols[:, 2, c:c + 1]).then_inc(s["x32_ready"], 1)
                    act.wait_ge(s["x32_ready"], n)
                    act.activation(xT[:, k % 2, 0, c, :], x32[:, c, :], ACT.Copy).then_inc(s["xT_hi"], 1)

                def x_low(dve, k, c, n):
                    dve.wait_ge(s["xT_hi"], n)
                    dve.tensor_tensor(xT[:, k % 2, 1, c, :], x32[:, c, :], xT[:, k % 2, 0, c, :].bitcast(F32),
                                      ALU.subtract).then_inc(s["xT_lo"], 1)

                def load_x(sp, j, buf):
                    sp.dma_start(xs[:, buf], sorted_in[bass.ds(j * BT, BT), :].rearrange("(t p) d -> p t d", p=P))\
                        .then_inc(s[f"x_in_{buf}"], 16)

                with nc.Block() as block:
                    @block.sync
                    def _(sp):
                        load_x(sp, 0, 0)
                        load_x(sp, 1, 1)
                        sp.wait_ge(s["x_in_1"], 16)

                    @block.scalar
                    def _(act):
                        for c in range(DC):
                            act.wait_ge(s["xT_ps"], 1)
                            x_high(act, 0, c, c + 1)

                    @block.tensor
                    def _(pe):
                        pe.wait_ge(s["x_in_0"], 16)
                        turn(pe, 0)

                    @block.vector
                    def _(dve):
                        for c in range(DC):
                            x_low(dve, 0, c, c + 1)
                clear(every)

                with nc.Fori(0, NBLK // BODY) as it:
                    with nc.Block() as block:
                        @block.sync
                        def _(sp):
                            def store(k):
                                sp.wait_ge(s["y_ready"], TT * (k + 1))
                                sp.dma_start(sorted_out[bass.ds((it * BODY + k) * BT, BT), :]
                                             .rearrange("(t p) d -> p t d", p=P), ys[:, k % 2]).then_inc(s[f"y_stored_{k % 2}"], 16)

                            for k in range(BODY):
                                if k:
                                    sp.wait_ge(s["xT_ps"], k)
                                load_x(sp, it * BODY + k + 2, k % 2)
                                if k:
                                    sp.wait_ge(s["w1_lo"], 4 * k)
                                    sp.wait_ge(s["w2_lo"], 2 * k)
                                load_weights(sp, expert_of(sp, it * BODY + k + 2), k + 2, s[f"w_in_{k % 2}"])
                                if k:
                                    store(k - 1)
                            store(BODY - 1)
                            for h in range(2):
                                sp.wait_ge(s[f"w_in_{h}"], 24 * BODY)
                            for h in range(2):
                                sp.wait_ge(s[f"x_in_{h}"], 8 * BODY)
                                sp.wait_ge(s[f"y_stored_{h}"], 8 * BODY)

                        @block.gpsimd
                        def _(pool):
                            for k in range(BODY):
                                for i in range(2):
                                    w2_low(pool, k + 1, i, s["w2_hi"], 2 * k + i + 1, s["w2_lo"])

                        @block.tensor
                        def _(pe):
                            def hidden(u):
                                k, f = u // FT, u % FT
                                if f == 0 and k:
                                    pe.wait_ge(s["xT_lo"], DC * k)
                                    pe.wait_ge(s["w1_lo"], 4 * k - 2)
                                if f == FT // 2 and k:
                                    pe.wait_ge(s["w1_lo"], 4 * k)
                                if u >= RING:
                                    pe.wait_ge(s["hid_ready"], u - RING + 1)
                                product(pe, PS[:, u % RING, 0:BT], lambda a, c: w1s[:, k % 2, a, c, f * P:(f + 1) * P],
                                        lambda a, c: xT[:, k % 2, a, c, :], DC).then_inc(s["hid_ps"], 1)

                            def outputs(u):
                                k, f = u // FT, u % FT
                                pe.wait_ge(s["hid_lo"], u + 1)
                                if k and f % (FT // 2) == 0:
                                    pe.wait_ge(s["w2_lo"], 2 * (k - 1) + f // (FT // 2) + 1)
                                if f == 0 and k >= 2:
                                    pe.wait_ge(s["y_ready"], TT * (k - 1))
                                for t in range(TT):
                                    for n, (a, c) in enumerate(PASSES):
                                        ins = pe.matmul(PS[:, 3 + 2 * (k % 2) + t, 0:D], hs[:, u % RING, a, t * P:(t + 1) * P],
                                                        w2s[:, k % 2, c, f, :], start=f == 0 and n == 0,
                                                        stop=f == FT - 1 and n == 2)
                                ins.then_inc(s["used"], 1)

                            for u in range(BODY * FT + 2):
                                if u < BODY * FT:
                                    hidden(u)
                                    if u % FT == 0:
                                        k = u // FT + 1
                                        if k >= 2:
                                            pe.wait_ge(s[f"x_in_{k % 2}"], 16 * (k // 2))
                                            pe.wait_ge(s["x32_ready"], DC * (k - 1))
                                        turn(pe, k)
                                if u >= 2:
                                    outputs(u - 2)

                        @block.scalar
                        def _(act):
                            def next_x(k, c):
                                act.wait_ge(s["xT_ps"], k)
                                if k >= 2:
                                    act.wait_ge(s["xT_lo"], DC * (k - 2) + c + 1)
                                    act.wait_ge(s["hid_ps"], (k - 1) * FT)
                                x_high(act, k, c, DC * (k - 1) + c + 1)

                            for u in range(BODY * FT):
                                k, f = u // FT, u % FT
                                act.wait_ge(s["hid_ps"], u + 1)
                                if u >= RING:
                                    act.wait_ge(s["hid_lo"], u - RING + 1)
                                act.activation(hid[:, u % RING, :], PS[:, u % RING, 0:BT], ACT.Relu,
                                               bias=b1c[:, k % 4, f:f + 1]).then_inc(s["hid_ready"], 1)
                                if u >= RING:
                                    act.wait_ge(s["used"], u - RING + 1)
                                act.wait_ge(s["hid_ready"], u + 1)
                                act.activation(hs[:, u % RING, 0, :], hid[:, u % RING, :], ACT.Copy).then_inc(s["hid_hi"], 1)
                                if f in HIGH_AT:
                                    if f == HIGH_AT[0] and k:
                                        act.wait_ge(s[f"w_in_{(k - 1) % 2}"], 48 * ((k + 1) // 2))
                                        act.wait_ge(s["hid_ps"], k * FT)
                                    w1_high(act, k + 1, HIGH_AT.index(f), s["w1_hi"])
                                if f in X_AT:
                                    next_x(k + 1, X_AT.index(f))

                        @block.vector
                        def _(dve):
                            def keep_y(k):
                                dve.wait_ge(s["used"], (k + 1) * FT)
                                if k >= 2:
                                    dve.wait_ge(s[f"y_stored_{k % 2}"], 16 * (k // 2))
                                for t in range(TT):
                                    dve.tensor_copy(ys[:, k % 2, t, :], PS[:, 3 + 2 * (k % 2) + t, 0:D])\
                                        .then_inc(s["y_ready"], 1)

                            for u in range(BODY * FT):
                                k, f = u // FT, u % FT
                                dve.wait_ge(s["hid_hi"], u + 1)
                                dve.tensor_tensor(hs[:, u % RING, 1, :], hid[:, u % RING, :],
                                                  hs[:, u % RING, 0, :].bitcast(F32), ALU.subtract).then_inc(s["hid_lo"], 1)
                                if f in W2_AT:
                                    if k and f == W2_AT[0]:
                                        dve.wait_ge(s[f"w_in_{(k - 1) % 2}"], 48 * ((k + 1) // 2))
                                        dve.wait_ge(s["used"], k * FT)
                                    w2_high(dve, k + 1, W2_AT.index(f), s["w2_hi"])
                                if f == 2 and k:
                                    keep_y(k - 1)
                                if f - 1 in X_AT:
                                    n = X_AT.index(f - 1)
                                    x_low(dve, k + 1, n, DC * k + n + 1)
                                for n in range(4):
                                    if LOW_AT[n] == f:
                                        w1_low(dve, k + 1, n, s["w1_hi"], 4 * k + n + 1, s["w1_lo"])
                            keep_y(BODY - 1)
                    clear(every)

            with ExitStack() as st:
                yg = sb("expert_rows", [P, NB, 2, D], stack=st)
                s, every = semaphores(st, "own stored out_ready")
                got = [st.enter_context(nc.semaphore(f"picked_in_{t}")) for t in range(NB)]
                ov = out.rearrange("b (c p r) d -> p (b c) r d", p=P, r=2)
                with nc.Block() as block:
                    @block.sync
                    def _(sp):
                        for t in range(0, NB, 2):
                            sp.wait_ge(s["out_ready"], t + 2)
                            sp.dma_start(ov[:, t // 2], base[:, t:t + 2, :]).then_inc(s["stored"], 16)
                        sp.wait_ge(s["stored"], 16 * NB // 2)

                    @block.gpsimd
                    def _(pool):
                        for t in range(NB):
                            for k in range(2):
                                pool.indirect_dma_start(
                                    out=yg[:, t, k, :], out_offset=None, in_=sorted_out[:, :],
                                    in_offset=bass.IndirectOffsetOnAxis(ap=slot[:, k, t:t + 1], axis=0))\
                                    .then_inc(got[t], 16)

                    @block.vector
                    def _(dve):
                        own = chain(dve, s["own"])
                        for t in range(NB):
                            dve.wait_ge(got[t], 32)
                            own(dve.scalar_tensor_tensor(out=base[:, t, :], in0=yg[:, t, 0, :], scalar=gate[:, 0, t:t + 1],
                                                         in1=base[:, t, :], op0=ALU.mult, op1=ALU.add))
                            dve.scalar_tensor_tensor(out=base[:, t, :], in0=yg[:, t, 1, :], scalar=gate[:, 1, t:t + 1],
                                                     in1=base[:, t, :], op0=ALU.mult, op1=ALU.add).then_inc(s["out_ready"], 1)


_INS = ['x', 'ctx_1024', 'mask_S2_ik0', 'L0_xattn_qkv_w', 'L0_xattn_proj_w', 'L0_xattn_proj_b', 'L0_ffn_ln1_g',
        'L0_ffn_ln1_b', 'L0_ffn_w_qkv', 'L0_ffn_b_qkv', 'L0_ffn_w_o', 'L0_ffn_b_o', 'L0_ffn_ln2_g', 'L0_ffn_ln2_b',
        'L0_ffn_gate_w', 'L0_ffn_gate_b', 'L0_ffn_W1', 'L0_ffn_b1', 'L0_ffn_W2', 'L0_ffn_b2']


def kernel(**inputs):
    import numpy as _np
    import concourse.bacc as _bacc
    from concourse import mybir as _mybir
    from concourse.bass_utils import run_bass_kernel_spmd as _run

    nc = _bacc.Bacc("TRN2", target_bir_lowering=False, num_devices=1)
    arrays, args = {}, []
    for name in _INS:
        a = _np.ascontiguousarray(inputs[name])
        arrays[f"in_{name}_dram"] = a
        args.append(nc.dram_tensor(f"in_{name}_dram", a.shape, _mybir.dt.from_np(a.dtype), kind="ExternalInput").ap())
    args.append(nc.dram_tensor("out_0_dram", (4, 512, 256), _mybir.dt.float32, kind="ExternalOutput").ap())
    xattn_moe_kernel(nc, *args)
    r = _run(nc, [arrays], core_ids=[0])
    return r.results[0]["out_0_dram"]
```
